# Optimizing a Trainium2 kernel written in Bass

```python
import numpy as np
import jax
import jax.numpy as jnp

def _softmax(x, axis=-1):
    return jax.nn.softmax(x, axis=axis)

def _gelu(x):
    return jax.nn.gelu(x, approximate=True)

def _silu(x):
    return jax.nn.silu(x)

def _sigmoid(x):
    return jax.nn.sigmoid(x)

def _layernorm(x, axis=-1, eps=1e-05):
    m = jnp.mean(x, axis=axis, keepdims=True)
    v = jnp.var(x, axis=axis, keepdims=True)
    return (x - m) / jnp.sqrt(v + eps)

def _scatter_add(tgt, idx, src, axis=0):
    return tgt.at[idx].add(src)

def _segment_sum(src, seg, n):
    return jax.ops.segment_sum(src, seg, n)
kernel_name = 'mk_hybrid_d2_jaxref_r8_6a40ac'

def setup_inputs(seed: int=0):
    np.random.seed(seed)
    _w = jnp.asarray

    def _L0_attn_a_setup():
        import jax, jax.numpy as jnp
        import numpy as np
        B, T, D, H = (4, 128, 128, 16)
        DH = D // H
        EPS = 1e-05

        def _rwkv6(x, W_r, W_k, W_v, W_w, W_o, u, tm_r, tm_k, tm_v, tm_w, ln_w, ln_b):
            b, t, d = x.shape
            x_prev = jnp.concatenate([jnp.zeros_like(x[:, :1]), x[:, :-1]], axis=1)
            xr = tm_r * x + (1.0 - tm_r) * x_prev
            xk = tm_k * x + (1.0 - tm_k) * x_prev
            xv = tm_v * x + (1.0 - tm_v) * x_prev
            xw = tm_w * x + (1.0 - tm_w) * x_prev
            r = jax.nn.sigmoid(xr @ W_r.T)
            k = xk @ W_k.T
            v = xv @ W_v.T
            w = -jax.nn.softplus(-(xw @ W_w.T)) - 0.0001
            r = r.reshape(b, t, H, DH)
            k = k.reshape(b, t, H, DH)
            v = v.reshape(b, t, H, DH)
            w = w.reshape(b, t, H, DH)

            def step(s, rkvw):
                r_t, k_t, v_t, w_t = rkvw
                bonus = jnp.exp(u + k_t)[..., :, None] * v_t[..., None, :]
                o_t = jnp.einsum('bhi,bhij->bhj', r_t, s + bonus)
                s = jnp.exp(w_t)[..., None] * s + k_t[..., :, None] * v_t[..., None, :]
                return (s, o_t)
            s0 = jnp.zeros((b, H, DH, DH), x.dtype)
            rkvw = tuple((a.transpose(1, 0, 2, 3) for a in (r, k, v, w)))
            _, o = jax.lax.scan(step, s0, rkvw)
            o = o.transpose(1, 0, 2, 3)
            mu = jnp.mean(o, axis=-1, keepdims=True)
            var = jnp.var(o, axis=-1, keepdims=True)
            o = (o - mu) * jax.lax.rsqrt(var + EPS) * ln_w + ln_b
            o = o * r
            return o.reshape(b, t, d) @ W_o.T
        key = jax.random.key(seed)
        ks = jax.random.split(key, 14)
        sc = 1.0 / np.sqrt(D)
        x = jax.random.normal(ks[0], (B, T, D), jnp.float32)
        W_r = jax.random.normal(ks[1], (D, D), jnp.float32) * sc
        W_k = jax.random.normal(ks[2], (D, D), jnp.float32) * sc
        W_v = jax.random.normal(ks[3], (D, D), jnp.float32) * sc
        W_w = jax.random.normal(ks[4], (D, D), jnp.float32) * sc
        W_o = jax.random.normal(ks[5], (D, D), jnp.float32) * sc
        u = jax.random.normal(ks[6], (H, DH), jnp.float32) * 0.1
        tm_r = jax.random.uniform(ks[7], (D,), jnp.float32)
        tm_k = jax.random.uniform(ks[8], (D,), jnp.float32)
        tm_v = jax.random.uniform(ks[9], (D,), jnp.float32)
        tm_w = jax.random.uniform(ks[10], (D,), jnp.float32)
        ln_w = jnp.ones((DH,), jnp.float32) + 0.1 * jax.random.normal(ks[11], (DH,), jnp.float32)
        ln_b = 0.1 * jax.random.normal(ks[12], (DH,), jnp.float32)
        return {'x': x, 'W_r': W_r, 'W_k': W_k, 'W_v': W_v, 'W_w': W_w, 'W_o': W_o, 'u': u, 'tm_r': tm_r, 'tm_k': tm_k, 'tm_v': tm_v, 'tm_w': tm_w, 'ln_w': ln_w, 'ln_b': ln_b}
    _L0_attn_a_in = _L0_attn_a_setup()

    def _L0_attn_b_setup():
        import jax, jax.numpy as jnp
        import numpy as np
        D_MODEL = 128
        NUM_HEADS = 16
        HEAD_DIM = D_MODEL // NUM_HEADS
        THETA = 10000.0
        B, T = (4, 256)

        def _cos_sin(seq_len, head_dim, theta):
            freqs = 1.0 / theta ** (jnp.arange(0, head_dim, 2, dtype=jnp.float32) / head_dim)
            t = jnp.arange(seq_len, dtype=jnp.float32)
            angles = jnp.outer(t, freqs)
            return jnp.concatenate([jnp.cos(angles), jnp.sin(angles)], axis=-1)

        def _apply_rope(x, cos_sin):
            x1 = x[..., 0::2]
            x2 = x[..., 1::2]
            half = x.shape[-1] // 2
            cos = cos_sin[:, :half]
            sin = cos_sin[:, half:]
            out = jnp.stack([x1 * cos - x2 * sin, x1 * sin + x2 * cos], axis=-1)
            return out.reshape(x.shape)
        key = jax.random.key(seed)
        k1, k2, k3 = jax.random.split(key, 3)
        x = jax.random.normal(k1, (B, T, D_MODEL), dtype=jnp.float32)
        W_qkv = jax.random.normal(k2, (3 * D_MODEL, D_MODEL), dtype=jnp.float32) * D_MODEL ** (-0.5)
        W_out = jax.random.normal(k3, (D_MODEL, D_MODEL), dtype=jnp.float32) * D_MODEL ** (-0.5)
        return {'x': x, 'W_qkv': W_qkv, 'W_out': W_out}
    _L0_attn_b_in = _L0_attn_b_setup()

    def _L0_ffn_setup():
        import jax, jax.numpy as jnp
        import numpy as np
        B, S, D, H, E, K = (4, 256, 128, 256, 8, 2)
        TEMP = 5.0
        EPS = 1e-09
        key = jax.random.key(seed)
        k_x, k_wg, k_w1, k_w2 = jax.random.split(key, 4)
        scale = 0.02
        return {'x': jax.random.normal(k_x, (B, S, D), dtype=jnp.float32), 'Wg': jax.random.normal(k_wg, (D, E), dtype=jnp.float32) * scale, 'bg': jnp.zeros((E,), dtype=jnp.float32), 'W1': jax.random.normal(k_w1, (E, D, H), dtype=jnp.float32) * scale, 'b1': jnp.zeros((E, H), dtype=jnp.float32), 'W2': jax.random.normal(k_w2, (E, H, D), dtype=jnp.float32) * scale, 'b2': jnp.zeros((E, D), dtype=jnp.float32)}
    _L0_ffn_in = _L0_ffn_setup()

    def _L1_attn_a_setup():
        import math
        import jax, jax.numpy as jnp
        import numpy as np
        D, DK, DV = (128, 128, 128)
        B, S = (4, 256)
        key = jax.random.key(seed)
        ks = jax.random.split(key, 4)
        std_qk = math.sqrt(2.0 / (D + DK))
        std_v = math.sqrt(2.0 / (D + DV))
        return {'X': jax.random.normal(ks[0], (B, S, D), dtype=jnp.float32), 'W_q': jax.random.normal(ks[1], (D, DK), dtype=jnp.float32) * std_qk, 'W_k': jax.random.normal(ks[2], (D, DK), dtype=jnp.float32) * std_qk, 'W_v': jax.random.normal(ks[3], (D, DV), dtype=jnp.float32) * std_v, 'b_q': jnp.zeros((DK,), dtype=jnp.float32), 'b_k': jnp.zeros((DK,), dtype=jnp.float32), 'b_v': jnp.zeros((DV,), dtype=jnp.float32)}
    _L1_attn_a_in = _L1_attn_a_setup()

    def _L1_attn_b_setup():
        import jax, jax.numpy as jnp
        import numpy as np
        D_MODEL, N_HEADS, N_KV, HEAD_DIM, D_LAT = (128, 8, 2, 128, 32)
        N_REP = N_HEADS // N_KV
        B, T = (2, 256)
        key = jax.random.key(seed)
        ks = jax.random.split(key, 8)
        s = lambda fan_in: 1.0 / np.sqrt(fan_in)
        return {'x': jax.random.normal(ks[0], (B, T, D_MODEL), jnp.float32), 'wq': jax.random.normal(ks[1], (D_MODEL, N_HEADS * HEAD_DIM), jnp.float32) * s(D_MODEL), 'wk_down': jax.random.normal(ks[2], (D_MODEL, N_KV * D_LAT), jnp.float32) * s(D_MODEL), 'wv_down': jax.random.normal(ks[3], (D_MODEL, N_KV * D_LAT), jnp.float32) * s(D_MODEL), 'wk_up': jax.random.normal(ks[4], (D_LAT, HEAD_DIM), jnp.float32) * s(D_LAT), 'wv_up': jax.random.normal(ks[5], (D_LAT, HEAD_DIM), jnp.float32) * s(D_LAT), 'wo': jax.random.normal(ks[6], (N_HEADS * HEAD_DIM, D_MODEL), jnp.float32) * s(N_HEADS * HEAD_DIM)}
    _L1_attn_b_in = _L1_attn_b_setup()

    def _L1_ffn_setup():
        import jax, jax.numpy as jnp
        import numpy as np
        NUM_EXPERTS = 8
        HIDDEN = 128
        D_FF = 512
        SCALE = 0.8
        SPARSITY = 0.1

        def _perturb_attractive(w, scale=SCALE, sparsity=SPARSITY):
            a = jnp.abs(w)
            flat = a.ravel()
            n = flat.shape[0]
            k = max(1, int(n * sparsity / 2))
            s = jnp.sort(flat)
            thr_bot = s[k - 1]
            thr_top = s[n - k]
            tier = jnp.where(a >= thr_top, -1.0, jnp.where(a <= thr_bot, 1.0, 0.0))
            return w + scale * w * tier

        def _stack_expert_params(w):
            pw = _perturb_attractive(w)
            return jnp.concatenate([w[None], jnp.broadcast_to(pw, (NUM_EXPERTS - 1,) + w.shape)], axis=0)
        key = jax.random.key(seed)
        ks = jax.random.split(key, 6)
        B, S, H, F, E = (2, 256, HIDDEN, D_FF, NUM_EXPERTS)
        return {'x': jax.random.normal(ks[0], (B, S, H), dtype=jnp.float32), 'W1': jax.random.normal(ks[1], (H, F), dtype=jnp.float32) * (1.0 / np.sqrt(H)), 'b1': jax.random.normal(ks[2], (F,), dtype=jnp.float32) * 0.02, 'W2': jax.random.normal(ks[3], (F, H), dtype=jnp.float32) * (1.0 / np.sqrt(F)), 'b2': jax.random.normal(ks[4], (H,), dtype=jnp.float32) * 0.02, 'ln_gamma': jnp.ones((H,), dtype=jnp.float32), 'ln_beta': jnp.zeros((H,), dtype=jnp.float32), 'Wr': jax.random.normal(ks[5], (H, E), dtype=jnp.float32) * (1.0 / np.sqrt(H)), 'br': jnp.zeros((E,), dtype=jnp.float32)}
    _L1_ffn_in = _L1_ffn_setup()
    _d = {'L0_attn_a_x': _L0_attn_a_in['x'], 'L0_attn_a_W_r': _L0_attn_a_in['W_r'], 'L0_attn_a_W_k': _L0_attn_a_in['W_k'], 'L0_attn_a_W_v': _L0_attn_a_in['W_v'], 'L0_attn_a_W_w': _L0_attn_a_in['W_w'], 'L0_attn_a_W_o': _L0_attn_a_in['W_o'], 'L0_attn_a_u': _L0_attn_a_in['u'], 'L0_attn_a_tm_r': _L0_attn_a_in['tm_r'], 'L0_attn_a_tm_k': _L0_attn_a_in['tm_k'], 'L0_attn_a_tm_v': _L0_attn_a_in['tm_v'], 'L0_attn_a_tm_w': _L0_attn_a_in['tm_w'], 'L0_attn_a_ln_w': _L0_attn_a_in['ln_w'], 'L0_attn_a_ln_b': _L0_attn_a_in['ln_b'], 'L0_attn_b_W_qkv': _L0_attn_b_in['W_qkv'], 'L0_attn_b_W_out': _L0_attn_b_in['W_out'], 'L0_ffn_Wg': _L0_ffn_in['Wg'], 'L0_ffn_bg': _L0_ffn_in['bg'], 'L0_ffn_W1': _L0_ffn_in['W1'], 'L0_ffn_b1': _L0_ffn_in['b1'], 'L0_ffn_W2': _L0_ffn_in['W2'], 'L0_ffn_b2': _L0_ffn_in['b2'], 'L1_attn_a_W_q': _L1_attn_a_in['W_q'], 'L1_attn_a_W_k': _L1_attn_a_in['W_k'], 'L1_attn_a_W_v': _L1_attn_a_in['W_v'], 'L1_attn_a_b_q': _L1_attn_a_in['b_q'], 'L1_attn_a_b_k': _L1_attn_a_in['b_k'], 'L1_attn_a_b_v': _L1_attn_a_in['b_v'], 'L1_attn_b_wq': _L1_attn_b_in['wq'], 'L1_attn_b_wk_down': _L1_attn_b_in['wk_down'], 'L1_attn_b_wv_down': _L1_attn_b_in['wv_down'], 'L1_attn_b_wk_up': _L1_attn_b_in['wk_up'], 'L1_attn_b_wv_up': _L1_attn_b_in['wv_up'], 'L1_attn_b_wo': _L1_attn_b_in['wo'], 'L1_ffn_W1': _L1_ffn_in['W1'], 'L1_ffn_b1': _L1_ffn_in['b1'], 'L1_ffn_W2': _L1_ffn_in['W2'], 'L1_ffn_b2': _L1_ffn_in['b2'], 'L1_ffn_ln_gamma': _L1_ffn_in['ln_gamma'], 'L1_ffn_ln_beta': _L1_ffn_in['ln_beta'], 'L1_ffn_Wr': _L1_ffn_in['Wr'], 'L1_ffn_br': _L1_ffn_in['br']}
    _x0 = _d['L0_attn_a_x']
    _d['L0_attn_a_x'] = jax.random.normal(jax.random.fold_in(jax.random.key(seed), 1), (1, 2048, 128), dtype=_x0.dtype)
    del _x0
    return _d

def reference(L0_attn_a_x, L0_attn_a_W_r, L0_attn_a_W_k, L0_attn_a_W_v, L0_attn_a_W_w, L0_attn_a_W_o, L0_attn_a_u, L0_attn_a_tm_r, L0_attn_a_tm_k, L0_attn_a_tm_v, L0_attn_a_tm_w, L0_attn_a_ln_w, L0_attn_a_ln_b, L0_attn_b_W_qkv, L0_attn_b_W_out, L0_ffn_Wg, L0_ffn_bg, L0_ffn_W1, L0_ffn_b1, L0_ffn_W2, L0_ffn_b2, L1_attn_a_W_q, L1_attn_a_W_k, L1_attn_a_W_v, L1_attn_a_b_q, L1_attn_a_b_k, L1_attn_a_b_v, L1_attn_b_wq, L1_attn_b_wk_down, L1_attn_b_wv_down, L1_attn_b_wk_up, L1_attn_b_wv_up, L1_attn_b_wo, L1_ffn_W1, L1_ffn_b1, L1_ffn_W2, L1_ffn_b2, L1_ffn_ln_gamma, L1_ffn_ln_beta, L1_ffn_Wr, L1_ffn_br):

    def _L0_attn_a_ref(x, W_r, W_k, W_v, W_w, W_o, u, tm_r, tm_k, tm_v, tm_w, ln_w, ln_b):
        import jax, jax.numpy as jnp
        import numpy as np
        B, T, D, H = (4, 128, 128, 16)
        DH = D // H
        EPS = 1e-05

        def _rwkv6(x, W_r, W_k, W_v, W_w, W_o, u, tm_r, tm_k, tm_v, tm_w, ln_w, ln_b):
            b, t, d = x.shape
            x_prev = jnp.concatenate([jnp.zeros_like(x[:, :1]), x[:, :-1]], axis=1)
            xr = tm_r * x + (1.0 - tm_r) * x_prev
            xk = tm_k * x + (1.0 - tm_k) * x_prev
            xv = tm_v * x + (1.0 - tm_v) * x_prev
            xw = tm_w * x + (1.0 - tm_w) * x_prev
            r = jax.nn.sigmoid(xr @ W_r.T)
            k = xk @ W_k.T
            v = xv @ W_v.T
            w = -jax.nn.softplus(-(xw @ W_w.T)) - 0.0001
            r = r.reshape(b, t, H, DH)
            k = k.reshape(b, t, H, DH)
            v = v.reshape(b, t, H, DH)
            w = w.reshape(b, t, H, DH)

            def step(s, rkvw):
                r_t, k_t, v_t, w_t = rkvw
                bonus = jnp.exp(u + k_t)[..., :, None] * v_t[..., None, :]
                o_t = jnp.einsum('bhi,bhij->bhj', r_t, s + bonus)
                s = jnp.exp(w_t)[..., None] * s + k_t[..., :, None] * v_t[..., None, :]
                return (s, o_t)
            s0 = jnp.zeros((b, H, DH, DH), x.dtype)
            rkvw = tuple((a.transpose(1, 0, 2, 3) for a in (r, k, v, w)))
            _, o = jax.lax.scan(step, s0, rkvw)
            o = o.transpose(1, 0, 2, 3)
            mu = jnp.mean(o, axis=-1, keepdims=True)
            var = jnp.var(o, axis=-1, keepdims=True)
            o = (o - mu) * jax.lax.rsqrt(var + EPS) * ln_w + ln_b
            o = o * r
            return o.reshape(b, t, d) @ W_o.T
        return _rwkv6(x, W_r, W_k, W_v, W_w, W_o, u, tm_r, tm_k, tm_v, tm_w, ln_w, ln_b)

    def _L0_attn_b_ref(x, W_qkv, W_out):
        import jax, jax.numpy as jnp
        import numpy as np
        D_MODEL = 128
        NUM_HEADS = 16
        HEAD_DIM = D_MODEL // NUM_HEADS
        THETA = 10000.0
        B, T = (4, 256)

        def _cos_sin(seq_len, head_dim, theta):
            freqs = 1.0 / theta ** (jnp.arange(0, head_dim, 2, dtype=jnp.float32) / head_dim)
            t = jnp.arange(seq_len, dtype=jnp.float32)
            angles = jnp.outer(t, freqs)
            return jnp.concatenate([jnp.cos(angles), jnp.sin(angles)], axis=-1)

        def _apply_rope(x, cos_sin):
            x1 = x[..., 0::2]
            x2 = x[..., 1::2]
            half = x.shape[-1] // 2
            cos = cos_sin[:, :half]
            sin = cos_sin[:, half:]
            out = jnp.stack([x1 * cos - x2 * sin, x1 * sin + x2 * cos], axis=-1)
            return out.reshape(x.shape)
        Bsz, Tlen, _ = x.shape
        qkv = jnp.einsum('bti,oi->bto', x, W_qkv)
        qkv = qkv.reshape(Bsz, Tlen, 3 * NUM_HEADS, HEAD_DIM).transpose(0, 2, 1, 3)
        q, k, v = jnp.split(qkv, 3, axis=1)
        cos_sin = _cos_sin(Tlen, HEAD_DIM, THETA)
        q = _apply_rope(q, cos_sin)
        k = _apply_rope(k, cos_sin)
        scores = jnp.einsum('bhqd,bhkd->bhqk', q, k) / np.sqrt(HEAD_DIM).astype(np.float32)
        causal = jnp.tril(jnp.ones((Tlen, Tlen), dtype=bool))
        scores = jnp.where(causal[None, None], scores, -jnp.inf)
        attn = jax.nn.softmax(scores, axis=-1)
        o = jnp.einsum('bhqk,bhkd->bhqd', attn, v)
        o = o.transpose(0, 2, 1, 3).reshape(Bsz, Tlen, D_MODEL)
        return jnp.einsum('bti,oi->bto', o, W_out)

    def _L0_ffn_ref(x, Wg, bg, W1, b1, W2, b2):
        import jax, jax.numpy as jnp
        import numpy as np
        B, S, D, H, E, K = (4, 256, 128, 256, 8, 2)
        TEMP = 5.0
        EPS = 1e-09
        logits = jnp.einsum('bsd,de->bse', x, Wg) + bg
        probs = jax.nn.softmax(logits / TEMP, axis=-1)
        vals, idx = jax.lax.top_k(probs, K)
        onehot = jax.nn.one_hot(idx, E, dtype=x.dtype)
        mask = jnp.einsum('bske,bsk->bse', onehot, vals)
        gates = mask / (jnp.sum(mask, axis=-1, keepdims=True) + EPS)
        h = jax.nn.gelu(jnp.einsum('bsd,edh->besh', x, W1) + b1[None, :, None, :], approximate=False)
        out = jnp.einsum('besh,ehd->besd', h, W2) + b2[None, :, None, :]
        y = jnp.einsum('bse,besd->bsd', gates, out)
        return y

    def _L1_attn_a_ref(X, W_q, W_k, W_v, b_q, b_k, b_v):
        import math
        import jax, jax.numpy as jnp
        import numpy as np
        D, DK, DV = (128, 128, 128)
        B, S = (4, 256)
        scale = 1.0 / math.sqrt(DK)
        Q = X @ W_q + b_q
        K = X @ W_k + b_k
        V = X @ W_v + b_v
        A = jnp.einsum('bsd,btd->bst', Q, K) * scale
        A = jax.nn.softmax(A, axis=2)
        return jnp.einsum('bst,btv->bsv', A, V)

    def _L1_attn_b_ref(x, wq, wk_down, wv_down, wk_up, wv_up, wo):
        import jax, jax.numpy as jnp
        import numpy as np
        D_MODEL, N_HEADS, N_KV, HEAD_DIM, D_LAT = (128, 8, 2, 128, 32)
        N_REP = N_HEADS // N_KV
        B, T = (2, 256)
        Bq, Tq, _ = x.shape
        scale = HEAD_DIM ** (-0.5)
        q = (x @ wq).reshape(Bq, Tq, N_KV, N_REP, HEAD_DIM)
        k_lat = (x @ wk_down).reshape(Bq, Tq, N_KV, D_LAT)
        v_lat = (x @ wv_down).reshape(Bq, Tq, N_KV, D_LAT)
        k = jnp.einsum('bkhl,ld->bkhd', k_lat, wk_up)
        v = jnp.einsum('bkhl,ld->bkhd', v_lat, wv_up)
        scores = jnp.einsum('bqhrd,bkhd->bhrqk', q, k) * scale
        causal = jnp.tril(jnp.ones((Tq, Tq), dtype=bool))
        scores = jnp.where(causal, scores, jnp.finfo(scores.dtype).min)
        probs = jax.nn.softmax(scores, axis=-1)
        y = jnp.einsum('bhrqk,bkhd->bqhrd', probs, v)
        y = y.reshape(Bq, Tq, N_HEADS * HEAD_DIM)
        return y @ wo

    def _L1_ffn_ref(x, W1, b1, W2, b2, ln_gamma, ln_beta, Wr, br):
        import jax, jax.numpy as jnp
        import numpy as np
        NUM_EXPERTS = 8
        HIDDEN = 128
        D_FF = 512
        SCALE = 0.8
        SPARSITY = 0.1

        def _perturb_attractive(w, scale=SCALE, sparsity=SPARSITY):
            a = jnp.abs(w)
            flat = a.ravel()
            n = flat.shape[0]
            k = max(1, int(n * sparsity / 2))
            s = jnp.sort(flat)
            thr_bot = s[k - 1]
            thr_top = s[n - k]
            tier = jnp.where(a >= thr_top, -1.0, jnp.where(a <= thr_bot, 1.0, 0.0))
            return w + scale * w * tier

        def _stack_expert_params(w):
            pw = _perturb_attractive(w)
            return jnp.concatenate([w[None], jnp.broadcast_to(pw, (NUM_EXPERTS - 1,) + w.shape)], axis=0)
        mu = jnp.mean(x, axis=-1, keepdims=True)
        var = jnp.mean(jnp.square(x - mu), axis=-1, keepdims=True)
        h = (x - mu) * jax.lax.rsqrt(var + 1e-05) * ln_gamma + ln_beta
        logits = jnp.einsum('bsh,he->bse', h, Wr) + br
        probs = jax.nn.softmax(logits, axis=-1)
        W1s = _stack_expert_params(W1)
        b1s = _stack_expert_params(b1)
        W2s = _stack_expert_params(W2)
        b2s = _stack_expert_params(b2)
        pre = jnp.einsum('bsh,ehf->besf', x, W1s) + b1s[None, :, None, :]
        act = jax.nn.gelu(pre)
        y = jnp.einsum('besf,efh->besh', act, W2s) + b2s[None, :, None, :]
        out = jnp.einsum('bse,besh->bsh', probs, y)
        return out
    x = L0_attn_a_x
    x = x + _L0_attn_a_ref(_layernorm(x, axis=-1), L0_attn_a_W_r, L0_attn_a_W_k, L0_attn_a_W_v, L0_attn_a_W_w, L0_attn_a_W_o, L0_attn_a_u, L0_attn_a_tm_r, L0_attn_a_tm_k, L0_attn_a_tm_v, L0_attn_a_tm_w, L0_attn_a_ln_w, L0_attn_a_ln_b)
    x = x + _L0_ffn_ref(_layernorm(x, axis=-1), L0_ffn_Wg, L0_ffn_bg, L0_ffn_W1, L0_ffn_b1, L0_ffn_W2, L0_ffn_b2)
    x = x + _L0_attn_b_ref(_layernorm(x, axis=-1), L0_attn_b_W_qkv, L0_attn_b_W_out)
    x = x + _L0_ffn_ref(_layernorm(x, axis=-1), L0_ffn_Wg, L0_ffn_bg, L0_ffn_W1, L0_ffn_b1, L0_ffn_W2, L0_ffn_b2)
    x = x + _L1_attn_a_ref(_layernorm(x, axis=-1), L1_attn_a_W_q, L1_attn_a_W_k, L1_attn_a_W_v, L1_attn_a_b_q, L1_attn_a_b_k, L1_attn_a_b_v)
    x = x + _L1_ffn_ref(_layernorm(x, axis=-1), L1_ffn_W1, L1_ffn_b1, L1_ffn_W2, L1_ffn_b2, L1_ffn_ln_gamma, L1_ffn_ln_beta, L1_ffn_Wr, L1_ffn_br)
    x = x + _L1_attn_b_ref(_layernorm(x, axis=-1), L1_attn_b_wq, L1_attn_b_wk_down, L1_attn_b_wv_down, L1_attn_b_wk_up, L1_attn_b_wv_up, L1_attn_b_wo)
    x = x + _L1_ffn_ref(_layernorm(x, axis=-1), L1_ffn_W1, L1_ffn_b1, L1_ffn_W2, L1_ffn_b2, L1_ffn_ln_gamma, L1_ffn_ln_beta, L1_ffn_Wr, L1_ffn_br)
    return x

_drawn_inputs = setup_inputs


def setup_inputs(seed=0):
    import zlib

    import numpy as np

    out = dict(_drawn_inputs(seed))
    spreads = {'L0_ffn_bg': (0.0, 0.1),
     'L0_ffn_b1': (0.0, 0.338),
     'L0_ffn_b2': (0.0, 0.1),
     'L1_attn_a_b_q': (0.0, 0.607),
     'L1_attn_a_b_k': (0.0, 2.0),
     'L1_attn_a_b_v': (0.0, 0.1),
     'L1_ffn_ln_gamma': (1.0, 0.6),
     'L1_ffn_ln_beta': (0.0, 2.0),
     'L1_ffn_br': (0.0, 0.8)}
    factors = {'L0_attn_a_u': 5.554, 'L0_attn_a_tm_w': 2.767, 'L1_ffn_b1': 4.189}
    for name, (base, spread) in spreads.items():
        noise = np.random.default_rng([zlib.crc32(name.encode()), seed]).standard_normal(out[name].shape)
        drawn = base * np.exp(spread * noise) if base else spread * noise
        out[name] = jnp.asarray(drawn.astype(out[name].dtype))
    for name, factor in factors.items():
        out[name] = (out[name] * factor).astype(out[name].dtype)
    return out
```

```python
from contextlib import ExitStack

import numpy as np
import concourse.bass as bass
from concourse import mybir

F32 = mybir.dt.float32
BF16 = mybir.dt.bfloat16
I32 = mybir.dt.int32
ALU = mybir.AluOpType
ACT = mybir.ActivationFunctionType
AX = mybir.AxisListType
RADD = bass.bass_isa.ReduceOp.add

P = 128
T = 2048
NT = T // P
CH = 512
NC = T // CH
TPC = CH // P
MASKED = -1.0e30
LOWEST = -3.0e38


class Stage:

    def sync(self, sp):
        pass

    def gpsimd(self, g):
        pass

    def tensor(self, pe):
        pass

    def scalar(self, s):
        pass

    def vector(self, v):
        pass


def each(eng, turns, body):
    body(0)
    with eng.Fori(1, turns) as turn:
        body(turn)


class Chain:

    def __init__(self, eng, sem, base=0):
        self.eng, self.sem, self.base, self.n = eng, sem, base, 0

    def mark(self, ins):
        self.n += 1
        return ins.then_inc(self.sem, 1)

    def wait(self):
        self.eng.wait_ge(self.sem, self.base + self.n)

    def __call__(self, ins):
        self.mark(ins)
        self.wait()


class Kernel:

    def __init__(self, nc, ctx, dram):
        self.nc, self.ctx, self.d = nc, ctx, dram
        self.n_sem = 0
        sb = self.sb
        self.X = sb("X", [P, NT, P])
        self.H = sb("H", [P, NT, P])
        self.HT = sb("HT", [P, 1 + T])
        self.cst = sb("cst", [P, CST_COLS])
        self.gates = sb("gates", [P, NT, 8])
        self.experts_mem = ExpertsMemory(self)
        self.router_mem = RouterMemory(self)
        self.ident = self.cst[:, 0:P]
        self.group_sum = self.cst[:, P:2 * P]
        self.group_mean = self.cst[:, 2 * P:3 * P]
        self.den_rope = self.cst[:, 3 * P:4 * P]
        self.den_latent = self.cst[:, 4 * P:5 * P]
        self.mask_qk = sb("mask_qk", [P, P], BF16)
        self.mask_kq = sb("mask_kq", [P, P], BF16)
        self.identb = sb("identb", [P, P], BF16)
        self.onesb = sb("onesb", [P, P], BF16)
        self.eps = sb("eps", [P, 1])
        self.PS = ctx.enter_context(nc.psum_tensor("PS", [P, 8, CH], F32))

    def sb(self, name, shape, dt=F32, ctx=None):
        return (ctx or self.ctx).enter_context(self.nc.sbuf_tensor("sb_" + name, shape, dt))

    def sem(self, name):
        self.n_sem += 1
        return self.ctx.enter_context(self.nc.semaphore(name))

    def bank(self, b, cols=CH):
        return self.PS[:, b, 0:cols]


N_CST = 5 + 8 + 2


class NormMemory:

    def __init__(self, k):
        self.stats = k.sb("stats", [P, NT, 6])
        self.mv = k.sb("mv", [P, NT, 2])
        self.sd = k.sb("sd", [P, NT])
        self.rstd = k.sb("rstd", [P, NT])
        self.uses = 0
        self.moments = k.sem("ln_moments")
        self.deviation = k.sem("ln_deviation")
        self.normed = k.sem("ln_normed")
        self.turned = k.sem("ln_turned")
        self.ready = k.sem("ln_ready")
        self.steps = k.sem("ln_steps")


class ExpertsMemory:

    def __init__(self, k):
        self.hid = [k.sem(f"hid{b}") for b in range(4)]
        self.hid_used = [k.sem(f"hid_used{b}") for b in range(4)]
        self.out = [k.sem(f"expert{b}") for b in range(2)]
        self.out_used = [k.sem(f"expert_used{b}") for b in range(2)]
        self.ready = k.sem("experts_ready")
        self.hid_count = self.out_count = self.ready_count = 0


class RouterMemory:

    def __init__(self, k):
        self.logits = k.sem("logits")
        self.read = k.sem("logits_read")
        self.shifted = k.sem("logits_shifted")
        self.exps = k.sem("router_exps")
        self.steps = k.sem("router_steps")
        self.uses = self.step_count = 0
        self.p = k.sb("rt_p", [P, NT, 8])
        self.a = k.sb("rt_a", [P, NT, 1])
        self.left = k.sb("rt_left", [P, NT, 8])
        self.sel = k.sb("rt_sel", [P, 2, NT, 8])


class LayerNorm(Stage):

    def __init__(self, k, src, dst, dst_t, src_ready, gamma=None, beta=None, banks=(0, 1, 2, 3)):
        self.k, self.src, self.dst, self.dst_t = k, src, dst, dst_t
        self.src_ready, self.gamma, self.beta, self.banks = src_ready, gamma, beta, banks
        self.mem = k.ln_mem
        self.use = self.mem.uses
        self.mem.uses += 1
        self.ready = self.mem.ready

    def chunk_ready(self, c):
        return self.use * NC + c + 1

    @property
    def all_ready(self):
        return self.use * NC + NC

    def vector(self, v):
        m, first = self.mem, self.use * (NT + 1)
        for c in range(NC):
            for sem, val in self.src_ready(c):
                v.wait_ge(sem, val)
            for n in range(c * TPC, (c + 1) * TPC):
                v.bn_stats(m.stats[:, n, :], self.src[:, n, :]).then_inc(m.steps, 1)
        for n in range(NT):
            v.wait_ge(m.steps, first + n + 1)
            ins = v.bn_aggr(m.mv[:, n, :], m.stats[:, n, :])
        ins.then_inc(m.moments, 1)
        v.wait_ge(m.deviation, self.use + 1)
        v.reciprocal(m.rstd[:, :], m.sd[:, :]).then_inc(m.steps, 1)
        v.wait_ge(m.steps, first + NT + 1)
        for n in range(NT):
            ins = v.tensor_scalar(self.dst[:, n, :], self.src[:, n, :], m.mv[:, n, 0:1], m.rstd[:, n:n + 1],
                                  ALU.subtract, ALU.mult)
            if n % TPC == TPC - 1:
                ins.then_inc(m.normed, 1)

    def tensor(self, pe):
        for c in range(NC):
            pe.wait_ge(self.mem.normed, self.chunk_ready(c))
            for i in range(TPC):
                ins = pe.transpose(self.k.PS[:, self.banks[c], i * P:(i + 1) * P], self.dst[:, c * TPC + i, :],
                                   self.k.ident)
            ins.then_inc(self.mem.turned, 1)

    def scalar(self, s):
        m = self.mem
        s.wait_ge(m.moments, self.use + 1)
        s.activation(m.sd[:, :], m.mv[:, :, 1], ACT.Sqrt, bias=self.k.eps[:, :]).then_inc(m.deviation, 1)
        for c in range(NC):
            s.wait_ge(m.turned, self.chunk_ready(c))
            out = self.dst_t[:, 1 + c * CH:1 + (c + 1) * CH]
            if self.gamma is None:
                s.activation(out, self.k.bank(self.banks[c]), ACT.Copy).then_inc(m.ready, 1)
            else:
                s.activation(out, self.k.bank(self.banks[c]), ACT.Identity, bias=self.beta,
                             scale=self.gamma).then_inc(m.ready, 1)


class Setup:

    def __init__(self, k):
        self.k = k
        sb = k.sb
        nc = k.nc
        self.loaded = k.sem("loaded")
        self.loaded_x = k.sem("loaded_x")
        self.turned = [k.sem(f"weights_turned{i}") for i in range(2)]
        self.copied = [k.sem(f"weights_copied{i}") for i in range(2)]
        self.steps = k.sem("setup_steps")
        self.ready = k.sem("setup_ready")
        self.zeroed = k.sem("setup_zeroed")
        self.pool = k.sem("setup_pool")
        k.ln_mem = NormMemory(k)
        k.w0 = sb("w0", [P, 8, 256])
        k.w0b = sb("w0b", [P, 8, 2, P])
        k.wg = sb("wg", [P, 8])
        k.bg = sb("bg", [P, 8])
        k.w1 = sb("w1", [P, 2, CH])
        k.w1b = sb("w1b", [P, 2, 4, P])
        k.b1 = sb("b1", [P, 2, 4])
        k.b1col = sb("b1col", [P, 2])
        k.wr = sb("wr", [P, 8])
        k.br = sb("br", [P, 8])
        k.vec = sb("vec", [P, 32])
        k.b0 = k.vec[:, 16:32].rearrange("p (e m) -> p e m", m=2)
        k.seed0 = sb("seed0", [3, 8, P], BF16)
        k.seed1 = sb("seed1", [3, 2, P], BF16)
        k.wqkvT = sb("wqkvT", [P, 5, P])
        k.woutT = sb("woutT", [P, 4, P])
        k.bv = sb("bv", [P, P])
        k.w3 = sb("w3", [P, 3, P])
        k.wkv = sb("wkv", [P, 2, 64])
        k.wc = sb("wc", [P, 8, 32])
        k.wy = sb("wy", [P, 4, P])

        self.n_zeroed = 5

    def alloc(self, ctx):
        sb = lambda n, sh, dt=F32: self.k.sb(n, sh, dt, ctx)
        self.k.wT = sb("wT", [P, 5, P])
        self.k.wvrep = sb("wvrep", [P, 8, P])
        self.rows = sb("rows", [32, P])
        self.wraw = sb("wraw", [P, 9, P])
        self.wpad = sb("wpad", [P, 4, 4, 32])
        self.wq = sb("wq", [P, 8, P])
        self.wqT = sb("wqT", [P, 8, P])
        self.wup = sb("wup", [32, 2, P])
        self.wkupT = sb("wkupT", [P, 32])
        self.wvupT = sb("wvupT", [P, 2, P])
        self.wo = sb("wo", [P, 8, P])
        self.row0 = sb("row0", [3, 8, P])
        self.rowr = sb("rowr", [3, 8, P])
        self.rowb = sb("rowb", [3, 8, P], BF16)
        self.n_loaded = 16 * len(self.loads())

    def loads(self):
        k, d = self.k, self.k.d
        out = []

        def load(dst, src):
            out.append((dst, src))

        load(k.cst[:, :], d["const"])
        for i, w in enumerate((d["L0_attn_a_W_r"], d["L0_attn_a_W_k"], d["L0_attn_a_W_v"], d["L0_attn_a_W_w"], d["L0_attn_a_W_o"])):
            load(self.wraw[:, i, :], w)
        load(self.wraw[:, 5:8, :], d["L0_attn_b_W_qkv"].rearrange("(n p) d -> p n d", p=P))
        load(self.wraw[:, 8, :], d["L0_attn_b_W_out"])
        load(self.wq[:, :, :], d["L1_attn_b_wq"].rearrange("p (h d) -> p h d", h=8))
        load(self.wup[:, 0, :], d["L1_attn_b_wk_up"])
        load(self.wup[:, 1, :], d["L1_attn_b_wv_up"])
        load(self.wo[:, :, :], d["L1_attn_b_wo"].rearrange("(h p) n -> p h n", p=P))
        load(k.wkv[:, 0, :], d["L1_attn_b_wk_down"])
        load(k.wkv[:, 1, :], d["L1_attn_b_wv_down"])
        for i, w in enumerate((d["L0_attn_a_tm_r"], d["L0_attn_a_tm_k"], d["L0_attn_a_tm_v"], d["L0_attn_a_tm_w"],
                               d["L0_attn_a_u"].rearrange("h d -> (h d)"))):
            load(self.rows[i:i + 1, :], w.rearrange("(a p) -> a p", a=1))
        for i, w in ((5, d["L0_attn_a_ln_w"]), (6, d["L0_attn_a_ln_b"])):
            load(self.rows[i:i + 1, :].rearrange("a (h d) -> a h d", h=16),
                 w.rearrange("(a b d) -> a b d", a=1, b=1).broadcast_to([1, 16, 8]))
        for i, w in ((7, d["L1_attn_a_b_q"]), (8, d["L1_attn_a_b_k"]), (9, d["L1_ffn_ln_gamma"]), (10, d["L1_ffn_ln_beta"]),
                     (11, d["L1_ffn_b2"])):
            load(self.rows[i:i + 1, :], w.rearrange("(a p) -> a p", a=1))
        load(self.rows[12:16, :], d["L1_ffn_b1"].rearrange("(m p) -> m p", p=P))
        load(self.rows[16:32, :], d["L0_ffn_b1"].rearrange("e (m p) -> (e m) p", p=P))
        for i, w in enumerate((d["L1_attn_a_W_q"], d["L1_attn_a_W_k"], d["L1_attn_a_W_v"])):
            load(k.w3[:, i, :], w)
        load(k.bv[:, :], d["L1_attn_a_b_v"].rearrange("(a p) -> a p", a=1).broadcast_to([P, P]))
        load(k.w0[:, :, :], d["L0_ffn_W1"].rearrange("e d h -> d e h"))
        for e in range(8):
            load(k.w0b[:, e, :, :], d["L0_ffn_W2"][e].rearrange("(m p) d -> p m d", p=P))
        load(k.wg[:, :], d["L0_ffn_Wg"])
        load(k.bg[:, :], d["L0_ffn_bg"].rearrange("(a e) -> a e", a=1).broadcast_to([P, 8]))
        load(self.row0[:, :, :], d["L0_ffn_b2"].rearrange("(a e) d -> a e d", a=1).broadcast_to([3, 8, P]))
        load(k.w1[:, 0, :], d["L1_ffn_W1"])
        load(k.w1b[:, 0, :, :], d["L1_ffn_W2"].rearrange("(m p) d -> p m d", p=P))
        load(k.wr[:, :], d["L1_ffn_Wr"])
        load(k.br[:, :], d["L1_ffn_br"].rearrange("(a e) -> a e", a=1).broadcast_to([P, 8]))
        return out

    def sync(self, sp):
        sp.dma_start(self.k.X[:, :, :], self.k.d["L0_attn_a_x"][0].rearrange("(n p) d -> p n d", p=P)) \
            .then_inc(self.loaded_x, 16)
        for dst, src in self.loads():
            sp.dma_start(dst, src).then_inc(self.loaded, 16)

    def gpsimd(self, g):
        k = self.k
        g.memset(k.eps[:, :], 1e-5).then_inc(self.zeroed, 1)
        g.memset(k.onesb[:, :], 1.0).then_inc(self.zeroed, 1)
        g.memset(self.wpad[:, :, :, :], 0.0).then_inc(self.zeroed, 1)
        g.memset(self.wvupT[:, :, :], 0.0).then_inc(self.zeroed, 1)
        g.memset(k.HT[:, 0:1], 0.0).then_inc(self.zeroed, 1)

    def groups(self):
        k = self.k
        raw = [self.wraw[:, i, :] for i in range(8)]
        pads = [self.wpad[:, g, :, :].rearrange("p j c -> p (j c)") for g in range(4)]
        return [(raw[0:4], k.wT[:, 0:4, :]), (raw[4:5], k.wT[:, 4:5, :]), (raw[5:8], k.wqkvT[:, 0:3, :]),
                (pads, k.woutT[:, :, :]), ([self.wq[:, i, :] for i in range(4)], self.wqT[:, 0:4, :]),
                ([self.wq[:, i, :] for i in range(4, 8)], self.wqT[:, 4:8, :])]

    def tensor(self, pe):
        k = self.k
        pe.wait_ge(self.loaded, self.n_loaded)
        pe.wait_ge(self.steps, 1)
        n = 0
        for ins_, _ in self.groups():
            pe.wait_ge(self.copied[n % 2], n // 2)
            for i, a in enumerate(ins_):
                ins = pe.transpose(k.PS[:, n % 2, i * P:(i + 1) * P], a, k.ident)
            ins.then_inc(self.turned[n % 2], 1)
            n += 1
        pe.wait_ge(self.copied[n % 2], n // 2)
        for i in range(2):
            pe.transpose(k.PS[:, n % 2, i * 32:(i + 1) * 32], self.wup[:, i, :], k.cst[0:32, 0:32])
        ins = pe.transpose(k.PS[:, n % 2, 64:96], self.rows[:, :], k.cst[0:32, 0:32])
        ins.then_inc(self.turned[n % 2], 1)
        n += 1
        pe.wait_ge(self.copied[(n - 1) % 2], (n - 1) // 2 + 1)
        pe.wait_ge(self.copied[n % 2], n // 2)
        for h in range(8):
            ins = pe.matmul(k.PS[:, n % 2, h * 32:(h + 1) * 32], self.wqT[:, h, :], self.wkupT[:, :],
                            start=True, stop=True)
        ins.then_inc(self.turned[n % 2], 1)
        n += 1
        pe.wait_ge(self.copied[n % 2], n // 2)
        for y in range(4):
            for s in range(2):
                ins = pe.matmul(k.PS[:, n % 2, y * P:(y + 1) * P], self.wvupT[:, s, :], self.wo[:, 2 * y + s, :],
                                start=(s == 0), stop=(s == 1))
        ins.then_inc(self.turned[n % 2], 1)

    def vector(self, v):
        k, ch = self.k, Chain(v, self.steps)
        v.wait_ge(self.loaded, self.n_loaded)
        v.wait_ge(self.zeroed, self.n_zeroed)
        ch(v.tensor_copy(self.wpad[:, :, :, 0:8], self.wraw[:, 8, :].rearrange("p (g j d) -> p g j d", g=4, j=4)))
        ch(v.tensor_copy(k.identb[:, :], k.ident))
        ch(v.tensor_copy(k.mask_qk[:, :], k.cst[:, (5 + 8) * P:(6 + 8) * P]))
        ch(v.tensor_copy(k.mask_kq[:, :], k.cst[:, (6 + 8) * P:(7 + 8) * P]))
        n = 0
        for _, out in self.groups():
            v.wait_ge(self.turned[n % 2], n // 2 + 1)
            w = out.shape[1]
            v.tensor_copy(out, k.PS[:, n % 2, 0:w * P].rearrange("p (n d) -> p n d", n=w)) \
                .then_inc(self.copied[n % 2], 1)
            n += 1
        v.wait_ge(self.turned[n % 2], n // 2 + 1)
        ch(v.tensor_copy(self.wkupT[:, :], k.PS[:, n % 2, 0:32]))
        ch(v.tensor_copy(self.wvupT[:, 0, 0:32], k.PS[:, n % 2, 32:64]))
        ch(v.tensor_copy(k.vec[:, :], k.PS[:, n % 2, 64:96]))
        ch(v.tensor_copy(k.b1[:, 0, :], k.vec[:, 12:16]))
        ch(v.tensor_copy(k.b1col[:, 0:1], k.vec[:, 11:12]))
        v.tensor_copy(self.wvupT[:, 1, 64:96], k.PS[:, n % 2, 32:64]).then_inc(self.copied[n % 2], 1)
        n += 1
        v.wait_ge(self.turned[n % 2], n // 2 + 1)
        v.tensor_copy(k.wc[:, :, :], k.PS[:, n % 2, 0:256].rearrange("p (h l) -> p h l", h=8)) \
            .then_inc(self.copied[n % 2], 1)
        n += 1
        v.wait_ge(self.turned[n % 2], n // 2 + 1)
        v.tensor_copy(k.wy[:, :, :], k.PS[:, n % 2, :].rearrange("p (h l) -> p h l", h=4)) \
            .then_inc(self.copied[n % 2], 1)
        n += 1
        v.wait_ge(self.copied[0], 5)
        v.wait_ge(self.copied[1], 4)
        for j in range(8):
            ch(v.tensor_copy(k.wvrep[:, j, :].rearrange("p (h i) -> p h i", h=16),
                             k.wT[:, 2, :].rearrange("p (h i) -> p h i", h=16)[:, :, j:j + 1]
                             .broadcast_to([P, 16, 8])))
        for i in range(2):
            for a in range(2):
                ch(v.tensor_copy(k.wqkvT[:, 3 + i, :].rearrange("p (m a) -> p m a", a=2)[:, :, a:a + 1],
                                 k.wqkvT[:, i, :].rearrange("p (m a) -> p m a", a=2)[:, :, 1 - a:2 - a]))
        split_rows(ch, v, self.row0[:, :, :], self.rowr[:, :, :], self.rowb[:, :, :], k.seed0[:, :, :], k)
        v.tensor_copy(self.rowb[:, 0, :], self.rowb[:, 0, :]).then_inc(self.ready, 1)


def split_rows(ch, v, full, rest, part, out, k):
    for r in range(3):
        src = full if r == 0 else rest
        ch(v.tensor_copy(part, src))
        if r == 0:
            ch(v.tensor_scalar(out, part, k.cst[0:3, 0:1], None, ALU.mult))
        else:
            ch(v.scalar_tensor_tensor(out, part, k.cst[0:3, r:r + 1], out, ALU.mult, ALU.add))
        if r < 2:
            ch(v.tensor_tensor(rest, src, part, ALU.subtract))


class Perturb:

    def __init__(self, k):
        self.k = k
        sb = k.sb
        self.steps = k.sem("perturb_steps")
        self.ready = k.sem("perturb_ready")
        self.b2_out = k.sem("perturb_b2_out")
        self.rows_split = k.sem("perturb_rows_split")
        self.a = sb("pa", [P, 2, CH])
        self.ab = sb("pab", [P, 4])
        self.ac = sb("pac", [P, 1])
        self.below = sb("pbelow", [P, 2, 2, CH])
        self.belowb = sb("pbelowb", [P, 2, 4])
        self.cnt = sb("pcnt", [P, 8])
        self.tot = sb("ptot", [P, 8])
        self.rank = sb("prank", [P, 8])
        self.found = sb("pfound", [P, 8], I32)
        self.trial = sb("ptrial", [P, 8], I32)
        self.keep = sb("pkeep", [P, 8], I32)
        self.bit = sb("pbit", [P, 8], I32)
        self.bitf = sb("pbitf", [P, 8])
        self.row1 = sb("prow1", [3, 2, P])
        self.rowr = sb("prowr", [3, 2, P])
        self.rowb = sb("prowb", [3, 2, P], BF16)

    def gpsimd(self, g):
        k = self.k
        ch = Chain(g, self.steps)
        g.wait_ge(k.setup.ready, 1)
        w2 = k.w1b[:, 0, :, :].rearrange("p m d -> p (m d)")
        for i, n in enumerate((P * CH, P * CH, CH, P)):
            kth = max(1, int(n * 0.1 / 2))
            ch(g.memset(self.rank[:, 2 * i:2 * i + 1], float(kth - 1)))
            ch(g.memset(self.rank[:, 2 * i + 1:2 * i + 2], float(n - kth)))
        ch(g.memset(self.found[:, :], 0))
        ch(g.memset(self.bitf[:, :], float(1 << 30)))
        for out, src in ((self.a[:, 0, :], k.w1[:, 0, :]), (self.a[:, 1, :], w2), (self.ab[:, :], k.b1[:, 0, :]),
                         (self.ac[:, :], k.b1col[:, 0:1])):
            low = self.below[:, 0, 0, 0:src.shape[-1]]
            ch(g.tensor_scalar(low, src, -1.0, 0.0, ALU.mult, ALU.max))
            ch(g.tensor_scalar(out, src, 0.0, None, ALU.max))
            ch(g.tensor_tensor(out, out, low, ALU.add))
        g.sem_clear(self.steps)
        with g.Fori(0, 31):
            ch = Chain(g, self.steps)
            tr = self.trial[:, :].bitcast(F32)
            ch(g.tensor_scalar(self.bit[:, :], self.bitf[:, :], 1.0, None, ALU.mult))
            ch(g.tensor_tensor(self.trial[:, :], self.found[:, :], self.bit[:, :], ALU.add))
            for s in range(2):
                for w in range(2):
                    ch.mark(g.tensor_scalar(self.below[:, w, s, :], self.a[:, w, :], tr[:, 2 * w + s:2 * w + s + 1],
                                            None, ALU.is_lt))
                ch.mark(g.tensor_scalar(self.belowb[:, s, :], self.ab[:, :], tr[:, 4 + s:5 + s], None, ALU.is_lt))
                ch(g.tensor_scalar(self.cnt[:, 6 + s:7 + s], self.ac[:, :], tr[:, 6 + s:7 + s], None, ALU.is_lt))
            bl = self.below[:, :, :, :].rearrange("p w s n -> p (w s) n")
            n = CH // 2
            while n > 1:
                ch(g.tensor_tensor(bl[:, :, 0:n], bl[:, :, 0:n], bl[:, :, n:2 * n], ALU.add))
                n //= 2
            ch.mark(g.tensor_tensor(self.cnt[:, 0:4], bl[:, :, 0], bl[:, :, 1], ALU.add))
            ch(g.tensor_tensor(self.belowb[:, :, 0:2], self.belowb[:, :, 0:2], self.belowb[:, :, 2:4], ALU.add))
            ch(g.tensor_tensor(self.cnt[:, 4:6], self.belowb[:, :, 0], self.belowb[:, :, 1], ALU.add))
            ch(g.partition_all_reduce(self.tot[:, :], self.cnt[:, :], P, RADD))
            ch(g.tensor_tensor(self.tot[:, :], self.tot[:, :], self.rank[:, :], ALU.subtract))
            ch(g.tensor_scalar(self.keep[:, :], self.tot[:, :], 0.0, self.bitf[:, 0:1], ALU.is_le, ALU.mult))
            ch(g.tensor_tensor(self.found[:, :], self.found[:, :], self.keep[:, :], ALU.add))
            ch(g.tensor_scalar(self.bitf[:, :], self.bitf[:, :], 0.5, None, ALU.mult))
            g.sem_clear(self.steps)
        ch = Chain(g, self.steps)
        th = self.found[:, :].bitcast(F32)
        for i, (a, src, out) in enumerate(((self.a[:, 0, :], k.w1[:, 0, :], k.w1[:, 1, :]),
                                           (self.a[:, 1, :], w2, k.w1b[:, 1, :, :].rearrange("p m d -> p (m d)")),
                                           (self.ab[:, :], k.b1[:, 0, :], k.b1[:, 1, :]),
                                           (self.ac[:, :], k.b1col[:, 0:1], k.b1col[:, 1:2]))):
            w = a.shape[-1]
            low = self.below[:, 0, 0, 0:w]
            top = self.below[:, 0, 1, 0:w]
            one = self.below[:, 1, 0, 0:w]
            ch(g.tensor_scalar(low, a, th[:, 2 * i:2 * i + 1], None, ALU.is_le))
            ch(g.tensor_scalar(top, a, th[:, 2 * i + 1:2 * i + 2], None, ALU.is_ge))
            ch(g.tensor_scalar(one, low, 1.0, None, ALU.add))
            ch(g.tensor_tensor(top, top, one, ALU.mult))
            ch(g.tensor_tensor(low, low, top, ALU.subtract))
            ch(g.tensor_scalar(one, src, 0.8, None, ALU.mult))
            ch(g.tensor_tensor(one, one, low, ALU.mult))
            ch(g.tensor_tensor(out, src, one, ALU.add))
        g.dma_start(k.d["b2_scratch"].rearrange("(v p) -> p v", v=2), k.b1col[:, :],
                    allow_slow_non_contiguous=True).then_inc(self.b2_out, 16)
        g.wait_ge(self.b2_out, 16)
        g.dma_start(self.row1[:, :, :], k.d["b2_scratch"].rearrange("(a v p) -> a v p", a=1, v=2)
                    .broadcast_to([3, 2, P])).then_inc(self.ready, 16)

    def split_b2(self, v):
        ch = Chain(v, self.rows_split)
        v.wait_ge(self.ready, 16)
        split_rows(ch, v, self.row1[:, :, :], self.rowr[:, :, :], self.rowb[:, :, :], self.k.seed1[:, :, :], self.k)



class PerturbedRows(Stage):

    def __init__(self, perturb):
        self.perturb = perturb

    def vector(self, v):
        self.perturb.split_b2(v)


class Rwkv(Stage):

    STEPS = 15
    def __init__(self, k, ht, ln):
        self.k, self.ht, self.ln = k, ht, ln
        s = lambda n: k.sem("rwkv_" + n)
        self.mixed = s("mixed")
        self.projected = s("projected")
        self.taken = s("taken")
        self.rk_ready = s("rk_ready")
        self.bonus = s("bonus")
        self.vrep = [s(f"vrep{b}") for b in range(2)]
        self.vrep_used = [s(f"vrep_used{b}") for b in range(2)]
        self.kv = [s(f"kv{b}") for b in range(2)]
        self.kv_used = [s(f"kv_used{b}") for b in range(2)]
        self.rs = [s(f"rs{b}") for b in range(2)]
        self.rs_used = [s(f"rs_used{b}") for b in range(2)]
        self.o_sb = s("o_sb")
        self.mean = s("mean")
        self.centred = s("centred")
        self.squared = s("squared")
        self.var = s("var")
        self.dev = s("dev")
        self.gated = s("gated")
        self.y = s("y")
        self.ready = s("ready")
        self.steps = s("steps")
        self.zeroed = s("zeroed")

    def alloc(self, ctx):
        sb = lambda n, sh: self.k.sb("rw_" + n, sh, ctx=ctx)
        self.diff = sb("diff", [P, CH])
        self.mix = sb("mix", [P, 4, CH])
        self.r, self.kk, self.v, self.w, self.ek = (sb(n, [P, CH]) for n in ("r", "k", "v", "w", "ek"))
        self.rk = sb("rk", [P, CH])
        self.vj = sb("vj", [P, 2, CH])
        self.kvj = sb("kvj", [P, 2, CH])
        self.state = sb("state", [P, 8, 1 + CH])
        self.rsj = sb("rsj", [P, 2, CH])
        self.o = sb("o", [P, CH])
        self.oc = sb("oc", [P, CH])
        self.sq = sb("sq", [P, CH])
        self.sd = sb("sd", [P, CH])
        self.z = sb("z", [P, CH])

    def vector(self, v):
        k = self.k
        v.wait_ge(k.setup.ready, 1)
        v.memset(self.state[:, :, CH:CH + 1], 0.0).then_inc(self.zeroed, 1)
        v.wait_ge(self.zeroed, 1)
        def turn(c):
            ch = Chain(v, self.steps, c * self.STEPS)
            v.wait_ge(self.ln.ready, self.ln.chunk_ready(c))
            v.wait_ge(self.projected, c * 4)
            ch(v.tensor_copy(self.state[:, :, 0:1], self.state[:, :, CH:CH + 1]))
            now = self.ht[:, bass.ds(1 + c * CH, CH)]
            before = self.ht[:, bass.ds(c * CH, CH)]
            ch(v.tensor_tensor(self.diff[:, :], now, before, ALU.subtract))
            for i in range(4):
                v.scalar_tensor_tensor(self.mix[:, i, :], self.diff[:, :], k.vec[:, i:i + 1], before,
                                       ALU.mult, ALU.add).then_inc(self.mixed, 1)
            v.wait_ge(self.taken, c * 5 + 5)
            v.tensor_tensor(self.rk[:, :], self.r[:, :], self.ek[:, :], ALU.mult).then_inc(self.rk_ready, 1)
            ch(v.tensor_scalar(self.w[:, :], self.w[:, :], float(np.exp(-1e-4)), None, ALU.mult))
            for j in range(8):
                b = j % 2
                v.wait_ge(self.kv[b], c * 4 + j // 2 + 1)
                ch(v.tensor_tensor_scan(self.state[:, j, 1:1 + CH], self.w[:, :], self.kvj[:, b, :],
                                        self.state[:, j, 0:1], ALU.mult, ALU.add))
                v.wait_ge(self.rs_used[b], c * 4 + j // 2)
                v.tensor_tensor(self.rsj[:, b, :], self.r[:, :], self.state[:, j, 0:CH], ALU.mult) \
                    .then_inc(self.rs[b], 1)
            v.wait_ge(self.bonus, c + 1)
            ch(v.tensor_tensor(self.o[:, :], k.bank(0), self.v[:, :], ALU.mult))
            v.wait_ge(self.rs_used[1], c * 4 + 4)
            v.tensor_tensor(self.o[:, :], self.o[:, :], k.bank(6), ALU.add).then_inc(self.o_sb, 1)
            v.wait_ge(self.mean, c + 1)
            v.tensor_tensor(self.oc[:, :], self.o[:, :], k.bank(1), ALU.subtract).then_inc(self.centred, 1)
            v.wait_ge(self.dev, c + 1)
            ch(v.reciprocal(self.sd[:, :], self.sd[:, :]))
            ch(v.tensor_tensor(self.oc[:, :], self.oc[:, :], self.sd[:, :], ALU.mult))
            ch(v.tensor_scalar(self.oc[:, :], self.oc[:, :], k.vec[:, 5:6], k.vec[:, 6:7], ALU.mult, ALU.add))
            v.tensor_tensor(self.z[:, :], self.oc[:, :], self.r[:, :], ALU.mult).then_inc(self.gated, 1)
            v.wait_ge(self.y, c + 1)
            xc = k.X[:, bass.ds(c * TPC, TPC), :]
            v.tensor_tensor(xc, xc, k.bank(3).rearrange("p (n d) -> p n d", n=TPC), ALU.add) \
                .then_inc(self.ready, 1)
            assert ch.n == self.STEPS, ch.n

        each(v, NC, turn)

    def scalar(self, s):
        k = self.k
        s.wait_ge(k.setup.ready, 1)
        def turn(c):
            s.wait_ge(self.gated, c)
            for i, (out, f, kw) in enumerate(((self.r, ACT.Sigmoid, {}), (self.kk, ACT.Copy, {}),
                                              (self.v, ACT.Copy, {}), (self.w, ACT.Sigmoid, {}))):
                s.wait_ge(self.projected, c * 4 + i + 1)
                s.activation(out[:, :], k.bank(i), f, **kw).then_inc(self.taken, 1)
            s.activation(self.ek[:, :], k.bank(1), ACT.Exp, bias=k.vec[:, 4:5]).then_inc(self.taken, 1)
            for j in range(8):
                b = j % 2
                s.wait_ge(self.vrep[b], c * 4 + j // 2 + 1)
                s.wait_ge(self.kv[b], c * 4 + j // 2)
                s.activation(self.vj[:, b, :], k.bank(4 + b), ACT.Copy).then_inc(self.vrep_used[b], 1)
            s.wait_ge(self.centred, c + 1)
            s.activation(self.sq[:, :], self.oc[:, :], ACT.Square).then_inc(self.squared, 1)
            s.wait_ge(self.var, c + 1)
            s.activation(self.sd[:, :], k.bank(2), ACT.Sqrt, bias=k.eps[:, :]).then_inc(self.dev, 1)

        each(s, NC, turn)

    def gpsimd(self, g):
        def turn(c):
            for j in range(8):
                b = j % 2
                g.wait_ge(self.taken, c * 5 + 2)
                g.wait_ge(self.vrep_used[b], c * 4 + j // 2 + 1)
                g.wait_ge(self.steps, c * self.STEPS + (3 + j - 1 if j >= 2 else 0))
                g.tensor_tensor(self.kvj[:, b, :], self.kk[:, :], self.vj[:, b, :], ALU.mult).then_inc(self.kv[b], 1)

        each(g, NC, turn)

    def tensor(self, pe):
        k = self.k
        pe.wait_ge(self.ln.ready, self.ln.all_ready)
        def turn(c):
            pe.wait_ge(self.ready, c)
            for i in range(4):
                pe.wait_ge(self.mixed, c * 4 + i + 1)
                pe.matmul(k.bank(i), k.wT[:, i, :], self.mix[:, i, :], start=True, stop=True) \
                    .then_inc(self.projected, 1)

            def values(j):
                b = j % 2
                pe.wait_ge(self.vrep_used[b], c * 4 + j // 2)
                pe.matmul(k.bank(4 + b), k.wvrep[:, j, :], self.mix[:, 2, :], start=True, stop=True) \
                    .then_inc(self.vrep[b], 1)

            values(0)
            values(1)
            pe.wait_ge(self.rk_ready, c + 1)
            pe.wait_ge(self.taken, c * 5 + 5)
            pe.matmul(k.bank(0), k.group_sum, self.rk[:, :], start=True, stop=True).then_inc(self.bonus, 1)
            for j in range(8):
                b = j % 2
                if j + 2 < 8:
                    values(j + 2)
                pe.wait_ge(self.rs[b], c * 4 + j // 2 + 1)
                pe.matmul(k.bank(6), k.cst[:, (5 + j) * P:(6 + j) * P], self.rsj[:, b, :],
                          start=(j == 0), stop=(j == 7)).then_inc(self.rs_used[b], 1)
            pe.wait_ge(self.o_sb, c + 1)
            pe.matmul(k.bank(1), k.group_mean, self.o[:, :], start=True, stop=True).then_inc(self.mean, 1)
            pe.wait_ge(self.squared, c + 1)
            pe.matmul(k.bank(2), k.group_mean, self.sq[:, :], start=True, stop=True).then_inc(self.var, 1)
            pe.wait_ge(self.gated, c + 1)
            for n in range(TPC):
                ins = pe.matmul(k.PS[:, 3, n * P:(n + 1) * P], self.z[:, n * P:(n + 1) * P], k.wT[:, 4, :],
                                start=True, stop=True)
            ins.then_inc(self.y, 1)

        each(pe, NC, turn)


class Experts(Stage):

    def __init__(self, k, name, ht, ln, router, w1, w2, b1, seed, func, experts, tiles,
                 needs=()):
        self.k, self.name, self.ht, self.ln, self.router = k, name, ht, ln, router
        self.w1, self.w2, self.b1, self.seed, self.func = w1, w2, b1, seed, func
        self.E, self.M, self.needs = experts, tiles, needs
        m = k.experts_mem
        self.hid, self.hid_used, self.out, self.out_used, self.ready = m.hid, m.hid_used, m.out, m.out_used, m.ready
        self.hid0, self.out0, self.ready0 = m.hid_count, m.out_count, m.ready_count
        m.hid_count += NC * experts * tiles // 4
        m.out_count += NC * experts // 2
        m.ready_count += NC

    def alloc(self, ctx):
        self.g = self.k.sb(self.name + "_hidden", [P, 2, self.M, CH], ctx=ctx)

    def tensor(self, pe):
        k, E, M = self.k, self.E, self.M
        uses = E * M // 4
        for sem, val in [*self.router.banks_free(), *self.needs]:
            pe.wait_ge(sem, val)
        def turn(c):
            x = self.ht[:, bass.ds(1 + c * CH, CH)]

            def hidden(e):
                for m in range(M):
                    b, n = (e * M + m) % 4, (e * M + m) // 4
                    pe.wait_ge(self.hid_used[b], self.hid0 + c * uses + n)
                    pe.matmul(k.bank(b), self.w1(e, m), x, start=True, stop=True).then_inc(self.hid[b], 1)

            def output(e):
                b = e % 2
                pe.wait_ge(self.out_used[b], self.out0 + c * (E // 2) + e // 2)
                pe.matmul(k.bank(4 + b), k.onesb[0:3, :],
                          self.seed[:, e:e + 1, :].broadcast_to([3, TPC, P]), start=True, stop=False,
                          skip_group_check=True)
                for m in range(M):
                    q, n = (e * M + m) % 4, (e * M + m) // 4
                    pe.wait_ge(self.hid_used[q], self.hid0 + c * uses + n + 1)
                    for i in range(TPC):
                        ins = pe.matmul(k.PS[:, 4 + b, i * P:(i + 1) * P], self.g[:, b, m, i * P:(i + 1) * P],
                                        self.w2(e, m), start=False, stop=(m == M - 1),
                                        skip_group_check=True)
                ins.then_inc(self.out[b], 1)

            for e in range(E):
                hidden(e)
                if e:
                    output(e - 1)
            output(E - 1)

        each(pe, NC, turn)

    def scalar(self, s):
        k, E, M = self.k, self.E, self.M
        uses = E * M // 4
        for sem, val in self.needs:
            s.wait_ge(sem, val)
        def turn(c):
            for e in range(E):
                s.wait_ge(self.out[e % 2], self.out0 + c * (E // 2) + e // 2)
                for m in range(M):
                    b, n = (e * M + m) % 4, (e * M + m) // 4
                    s.wait_ge(self.hid[b], self.hid0 + c * uses + n + 1)
                    s.activation(self.g[:, e % 2, m, :], k.bank(b), self.func, bias=self.b1(e, m)) \
                        .then_inc(self.hid_used[b], 1)

        each(s, NC, turn)

    def vector(self, v):
        k, E = self.k, self.E
        def turn(c):
            for e in range(E):
                b = e % 2
                v.wait_ge(self.out[b], self.out0 + c * (E // 2) + e // 2 + 1)
                if e:
                    v.wait_ge(self.out_used[1 - b], self.out0 + c * (E // 2) + (e - 1) // 2 + 1)
                for i in range(TPC):
                    xi = k.X[:, bass.ds(c * TPC + i, 1), :]
                    gate = k.gates[:, bass.ds(c * TPC + i, 1), e:e + 1].rearrange("p a b -> p (a b)")
                    ins = v.scalar_tensor_tensor(xi, k.PS[:, 4 + b:5 + b, i * P:(i + 1) * P], gate, xi,
                                                 ALU.mult, ALU.add)
                ins.then_inc(self.out_used[b], 1)
            v.wait_ge(self.out_used[1], self.out0 + c * (E // 2) + E // 2)
            v.sem_inc(self.ready, 1)

        each(v, NC, turn)

    def x_ready(self, c):
        return [(self.ready, self.ready0 + c + 1)]


class Router(Stage):

    def __init__(self, k, name, ht, ln, w, bias, top2):
        self.k, self.ht, self.ln, self.w, self.bias, self.top2 = k, ht, ln, w, bias, top2
        m = k.router_mem
        self.logits, self.shifted, self.exps, self.steps, self.read = m.logits, m.shifted, m.exps, m.steps, m.read
        self.nth, self.step0 = m.uses + 1, m.step_count
        m.uses += 1
        m.step_count += 22 if top2 else 6

    def tensor(self, pe):
        k = self.k
        pe.wait_ge(self.ln.ready, self.ln.all_ready)
        for n in range(NT):
            ins = pe.matmul(k.PS[:, 7, n * 8:(n + 1) * 8], self.ht[:, 1 + n * P:1 + (n + 1) * P], self.w,
                            start=True, stop=True)
        ins.then_inc(self.logits, 1)

    def scalar(self, s):
        m = self.k.router_mem
        s.wait_ge(self.shifted, self.nth)
        s.activation(m.p[:, :, :], m.p[:, :, :], ACT.Exp, scale=0.2 if self.top2 else 1.0).then_inc(self.exps, 1)

    def banks_free(self):
        return [(self.read, self.nth)]

    def vector(self, v):
        k, m, ch = self.k, self.k.router_mem, Chain(v, self.steps, self.step0)
        full = [P, NT, 8]
        col = lambda a: a.broadcast_to(full)
        v.wait_ge(self.logits, self.nth)
        v.tensor_tensor(m.p[:, :, :], k.PS[:, 7, 0:NT * 8].rearrange("p (n e) -> p n e", n=NT),
                        self.bias[:, :].rearrange("p (a e) -> p a e", a=1).broadcast_to(full), ALU.add) \
            .then_inc(self.read, 1)
        v.wait_ge(self.read, self.nth)
        ch(v.tensor_reduce(m.a[:, :, :], m.p[:, :, :], AX.X, ALU.max))
        v.tensor_tensor(m.p[:, :, :], m.p[:, :, :], col(m.a[:, :, :]), ALU.subtract).then_inc(self.shifted, 1)
        v.wait_ge(self.exps, self.nth)
        ch(v.tensor_reduce(m.a[:, :, :], m.p[:, :, :], AX.X, ALU.add))
        ch(v.reciprocal(m.a[:, :, :], m.a[:, :, :]))
        ch(v.tensor_tensor(m.p[:, :, :], m.p[:, :, :], col(m.a[:, :, :]), ALU.mult))
        if not self.top2:
            ch(v.tensor_copy(k.gates[:, :, 0:1], m.p[:, :, 0:1]))
            ch(v.tensor_reduce(k.gates[:, :, 1:2], m.p[:, :, 1:8], AX.X, ALU.add))
            assert ch.n == 6
            return
        order = k.cst[:, CST_ORDER:CST_ORDER + 8].rearrange("p (a e) -> p a e", a=1).broadcast_to(full)
        ch(v.tensor_copy(m.left[:, :, :], m.p[:, :, :]))
        for r in range(2):
            sel = m.sel[:, r, :, :]
            ch(v.tensor_reduce(m.a[:, :, :], m.left[:, :, :], AX.X, ALU.max))
            ch(v.tensor_tensor(sel, m.left[:, :, :], col(m.a[:, :, :]), ALU.is_equal))
            ch(v.tensor_tensor(sel, sel, order, ALU.mult))
            ch(v.tensor_reduce(m.a[:, :, :], sel, AX.X, ALU.max))
            ch(v.tensor_tensor(sel, sel, col(m.a[:, :, :]), ALU.is_equal))
            if r == 0:
                ch(v.scalar_tensor_tensor(m.left[:, :, :], sel, -2.0, m.left[:, :, :], ALU.mult, ALU.add))
        ch(v.tensor_tensor(m.sel[:, 0, :, :], m.sel[:, 0, :, :], m.sel[:, 1, :, :], ALU.add))
        ch(v.tensor_tensor(m.p[:, :, :], m.p[:, :, :], m.sel[:, 0, :, :], ALU.mult))
        ch(v.tensor_reduce(m.a[:, :, :], m.p[:, :, :], AX.X, ALU.add))
        ch(v.tensor_scalar(m.a[:, :, :], m.a[:, :, :], 1e-9, None, ALU.add))
        ch(v.reciprocal(m.a[:, :, :], m.a[:, :, :]))
        ch(v.tensor_tensor(k.gates[:, :, :], m.p[:, :, :], col(m.a[:, :, :]), ALU.mult))
        assert ch.n == 22, ch.n


class CausalHeads(Stage):

    LAG = 5

    def __init__(self, k, name, ln, quads, sources, blocks, rows, kheads, value_w, vheads, vdim, scale, den, wout,
                 blocks_out, scratch, rotate):
        self.k, self.name, self.ln, self.NQ = k, name, ln, quads
        self.sources, self.blocks, self.rows, self.kheads = sources, blocks, rows, kheads
        self.value_w, self.vheads, self.vdim, self.scale = value_w, vheads, vdim, scale
        self.den, self.wout, self.nb, self.scratch, self.rotate = den, wout, blocks_out, scratch, rotate
        self.NP = 1 + max(b[0] for b in blocks[0])
        s = lambda n: k.sem(name + "_" + n)
        self.filled = s("filled")
        self.table = s("table")
        self.projected = s("projected")
        self.split = s("split")
        self.stored = [s(f"stored{i}") for i in range(len(sources))]
        self.steps = s("steps")
        self.vproj = s("vproj")
        self.values = s("values")
        self.stacked = [s(f"stacked{b}") for b in range(2)]
        self.ring_full = [s(f"ring_full{b}") for b in range(2)]
        self.ring_free = [s(f"ring_free{b}") for b in range(2)]
        self.maxima = s("maxima")
        self.max_rows = [s(f"max_rows{b}") for b in range(2)]
        self.scores = [s(f"scores{p}") for p in range(2)]
        self.exps = [s(f"exps{p}") for p in range(2)]
        self.weighted = s("weighted")
        self.moved = s("moved")
        self.normed = s("normed")
        self.ready = s("ready")
        self.units = [(c, kj) for c in range(NC) for kj in range((c + 1) * TPC)]
        self.plan = self.make_plan()

    def alloc(self, ctx):
        sb = lambda n, sh, dt=F32: self.k.sb(self.name + "_" + n, sh, dt, ctx)
        self.Q = sb("Q", [P, 2, 4, self.NP, T], BF16)
        self.K = sb("K", [P, 2, self.kheads, self.NP, T], BF16)
        self.V = sb("V", [P, NT, self.vheads, self.vdim + 1])
        self.mp = sb("mp", [P, 4, NT, NC])
        self.neg = sb("neg", [P, 2, NT])
        self.negp = sb("negp", [P, 2, 3, NT], BF16)
        self.negT = sb("negT", [3 * NT, 2, P], BF16)
        self.O = sb("O", [P, 2, self.nb, CH])
        self.On = sb("On", [P, 2, self.nb, CH])
        self.rec = sb("rec", [P, CH])
        with ExitStack() as c:
            self.PT = self.k.sb(self.name + "_PT", [P, 2, 4, CH], F32, c)
        with ExitStack() as c:
            self.parts = self.k.sb(self.name + "_parts", [P, 2, 3, CH], BF16, c)
            self.x = self.k.sb(self.name + "_x", [P, CH], F32, c)
            self.y = self.k.sb(self.name + "_y", [P, CH], F32, c)
            self.tab = self.k.sb(self.name + "_tab", [P, 2, CH], F32, c)

    def make_plan(self):
        def maxima(g):
            items = []
            for j in range(4):
                mine = [("max", g, j, i, kc) for i in range(NT) for kc in range(i // TPC + 1)]
                if j:
                    mine.insert(6, ("turn", g, j - 1))
                items += mine
            return items + [("turn", g, 3)]

        n = len(self.units)
        steps = [[] for _ in range(self.NQ * n + 4)]
        for g in range(self.NQ):
            if g + 1 < self.NQ:
                items = maxima(g + 1)
                slots = n - self.LAG - 1
                for i, it in enumerate(items):
                    steps[g * n + self.LAG + i * slots // len(items)].append(it)
            for c in range(NC):
                end = g * n + self.units.index((c, (c + 1) * TPC - 1))
                steps[end + 2] += [("sum", g, c, b) for b in range(self.nb)]
                steps[end + 3] += [("out", g, c)]
        plan = [(None, it) for it in maxima(0)]
        for u, items in enumerate(steps):
            plan.append((u, None))
            plan += [(None, it) for it in items]
        return plan

    def unit(self, u):
        g, i = divmod(u, len(self.units))
        c, kj = self.units[i]
        q0 = max(0, kj - c * TPC) * P
        return g, c, kj, q0

    def chunk(self, g, c):
        return g * NC + c

    def tensor(self, pe):
        k, ns = self.k, len(self.sources)
        pe.wait_ge(self.ln.ready, self.ln.all_ready)
        def turn(c):
            for i, (w, partner, m) in enumerate(self.sources):
                if i >= 2:
                    pe.wait_ge(self.split, c * ns + i - 1)
                else:
                    pe.wait_ge(self.split, c * ns)
                h = self.k.HT[:, bass.ds(1 + c * CH, CH)]
                b = 2 * (i % 2)
                ins = pe.matmul(k.PS[0:m, b, :], w, h, start=True, stop=True)
                if partner is not None:
                    ins = pe.matmul(k.PS[0:m, b + 1, :], partner, h, start=True, stop=True)
                ins.then_inc(self.projected, 1)

        each(pe, NC, turn)
        pe.wait_ge(self.filled, 1)
        for c in range(NC):
            pe.wait_ge(self.values, max(0, c - 1))
            for i in range(TPC):
                n = c * TPC + i
                ins = pe.matmul(k.PS[:, 4 + c % 2, i * P:i * P + self.value_w.shape[-1]],
                                k.HT[:, 1 + n * P:1 + (n + 1) * P], self.value_w, start=True, stop=True)
            ins.then_inc(self.vproj, 1)
        ring = 0
        done = 0
        for u, item in self.plan:
            if u is not None:
                if u < self.NQ * len(self.units):
                    self.pe_scores(pe, u)
                if 1 <= u <= self.NQ * len(self.units):
                    self.pe_weighted(pe, u - 1)
                continue
            b = ring % 2
            pe.wait_ge(self.ring_free[b], ring // 2)
            self.pe_item(pe, item, 6 + b).then_inc(self.ring_full[b], 1)
            ring += 1

    def pe_item(self, pe, item, bank):
        k, kind = self.k, item[0]
        if kind == "max":
            _, g, j, i, kc = item
            pe.wait_ge(self.stacked[g % 2], 16 * self.stack_dmas * (g // 2 + 1))
            w = min(CH, (i + 1) * P - kc * CH)
            diag = kc == i // TPC
            ins = pe.matmul(k.PS[:, bank, 0:w], self.Q[0:self.rows, g % 2, j, 0, i * P:(i + 1) * P],
                            self.K[0:self.rows, g % 2, j % self.kheads, 0, kc * CH:kc * CH + w],
                            start=True, stop=not diag)
            if diag:
                ins = pe.matmul(k.PS[:, bank, w - P:w], k.identb[:, :], k.mask_qk[:, :], start=False, stop=True)
            return ins
        if kind == "turn":
            _, g, j = item
            n = 4 * g + j
            pe.wait_ge(self.maxima, n + 1)
            return pe.transpose(k.PS[:, bank, :].bitcast(BF16)[0:3 * NT, 0:P],
                                self.negp[:, n % 2, :, :].rearrange("p r n -> p (r n)"), k.identb[:, :])
        if kind == "sum":
            _, g, c, blk = item
            n = self.chunk(g, c)
            pe.wait_ge(self.moved, n + 1)
            return pe.matmul(k.bank(bank), self.den, self.O[:, n % 2, blk, :], start=True, stop=True)
        _, g, c = item
        n = self.chunk(g, c)
        pe.wait_ge(self.normed, self.nb * (n + 1))
        for i in range(TPC):
            for blk in range(self.nb):
                ins = pe.matmul(k.PS[:, bank, i * P:(i + 1) * P], self.On[:, n % 2, blk, i * P:(i + 1) * P],
                                self.wout[:, g * self.nb + blk, :], start=(blk == 0), stop=(blk == self.nb - 1))
        return ins

    def pe_scores(self, pe, u):
        k = self.k
        g, c, kj, q0 = self.unit(u)
        for b in range(2):
            pe.wait_ge(self.max_rows[b], 16 * 2 * (g + 1))
        if u == 0:
            pe.wait_ge(self.split, NC * len(self.sources))
        for p in range(2):
            pe.wait_ge(self.exps[p], u)
            for j in (2 * p, 2 * p + 1):
                diag = kj >= c * TPC
                for m in range(self.NP):
                    r = self.rows + (3 if m == 0 else 0)
                    ins = pe.matmul(k.PS[:, j, q0:CH], self.K[0:r, g % 2, j % self.kheads, m, kj * P:(kj + 1) * P],
                                    self.Q[0:r, g % 2, j, m, c * CH + q0:(c + 1) * CH],
                                    start=(m == 0), stop=(m == self.NP - 1 and not diag))
                if diag:
                    ins = pe.matmul(k.PS[:, j, q0:q0 + P], k.identb[:, :], k.mask_kq[:, :], start=False, stop=True)
            ins.then_inc(self.scores[p], 1)

    def o_bank(self, n, j):
        if self.nb == 1:
            return 4 + n % 2, 32 * j
        return 4 + j // 2, 64 * (j % 2)

    def pe_weighted(self, pe, u):
        k = self.k
        g, c, kj, q0 = self.unit(u)
        n = self.chunk(g, c)
        last = (c + 1) * TPC - 1
        if kj == 0:
            before = n - 1 if self.nb == 1 else n
            if before > 0:
                pe.wait_ge(self.moved, before)
        if u == 0:
            pe.wait_ge(self.values, NC)
        for p in range(2):
            pe.wait_ge(self.exps[p], u + 1)
        for j in range(4):
            b, p0 = self.o_bank(n, j)
            v = self.V[:, kj, (4 * g + j) if self.vheads > 4 else g, :]
            ins = pe.matmul(k.PS[p0:p0 + self.vdim + 1, b, q0:CH], v, self.PT[:, u % 2, j, q0:CH],
                            start=(kj == 0), stop=(kj == last))
        ins.then_inc(self.weighted, 1)

    def scalar(self, s):
        k, v = self.k, self.vdim
        s.wait_ge(self.filled, 1)
        for c in range(NC):
            s.wait_ge(self.vproj, c + 1)
            s.activation(self.V[:, c * TPC:(c + 1) * TPC, :, 0:v],
                         k.PS[:, 4 + c % 2, :].rearrange("p (n d) -> p n d", n=TPC)[:, :, 0:self.vheads * v]
                         .rearrange("p n (h d) -> p n h d", h=self.vheads), ACT.Copy).then_inc(self.values, 1)
        total = self.NQ * len(self.units)
        for sem in self.stored:
            s.wait_ge(sem, 16 * NC)
        for u in range(total + 1):
            if u < total:
                _, _, _, q0 = self.unit(u)
                if u >= 2:
                    s.wait_ge(self.weighted, u - 1)
                for p in range(2):
                    s.wait_ge(self.scores[p], u + 1)
                    s.activation(self.PT[:, u % 2, 2 * p:2 * p + 2, q0:CH], k.PS[:, 2 * p:2 * p + 2, q0:CH],
                                 ACT.Exp, scale=self.scale).then_inc(self.exps[p], 1)
            if u:
                g, c, kj, _ = self.unit(u - 1)
                if kj == (c + 1) * TPC - 1:
                    n = self.chunk(g, c)
                    s.wait_ge(self.weighted, u)
                    if n >= 2:
                        s.wait_ge(self.normed, self.nb * (n - 1))
                    b = 4 + n % 2 if self.nb == 1 else 4
                    s.activation(self.O[:, n % 2, :, :], k.PS[:, b:b + self.nb, :], ACT.Copy).then_inc(self.moved, 1)

    def vector(self, v):
        k, ch, ns = self.k, Chain(v, self.steps), len(self.sources)
        v.wait_ge(self.ln.ready, self.ln.all_ready)
        ch(v.memset(self.K[:, :, :, 0, :], 1.0))
        ch(v.memset(self.V[:, :, :, self.vdim:self.vdim + 1], 1.0))
        ch(v.memset(self.mp[:, :, :, :], LOWEST))
        v.memset(k.PS[:, 4:6, :], 0.0).then_inc(self.filled, 1)
        per = sum((3 if partner is not None else 1) + 3 for _, partner, _ in self.sources)
        def turn(c):
            ch = Chain(v, self.steps, 3 + c * per)
            if self.rotate:
                v.wait_ge(self.table, 16 * c + 16)
            for i, (w, partner, m) in enumerate(self.sources):
                b = 2 * (i % 2)
                x, y, part = self.x[0:m, :], self.y[0:m, :], self.parts[0:m, i % 2, :, :]
                v.wait_ge(self.projected, c * ns + i + 1)
                if partner is not None:
                    ch.mark(v.tensor_tensor(x, k.PS[0:m, b, :], self.tab[0:m, 0, :], ALU.mult))
                    ch(v.tensor_tensor(y, k.PS[0:m, b + 1, :], self.tab[0:m, 1, :], ALU.mult))
                    ch(v.tensor_tensor(x, x, y, ALU.add))
                else:
                    ch(v.tensor_copy(x, k.PS[0:m, b, :]))
                if i >= 2:
                    v.wait_ge(self.stored[i - 2], 16 * c + 16)
                else:
                    v.wait_ge(self.stored[ns - 1 - (ns - 1 - i) % 2], 16 * c)
                ch(v.tensor_copy(part[:, 0, :], x))
                ch(v.tensor_tensor(x, x, part[:, 0, :], ALU.subtract))
                ch(v.tensor_copy(part[:, 1, :], x))
                v.tensor_tensor(part[:, 2, :], x, part[:, 1, :], ALU.subtract).then_inc(self.split, 1)
                v.wait_ge(self.split, c * ns + i + 1)
            assert ch.n == per, ch.n

        each(v, NC, turn)
        ch = Chain(v, self.steps, 3 + NC * per)
        ring = 0
        for u, item in self.plan:
            if u is not None:
                continue
            b = ring % 2
            v.wait_ge(self.ring_full[b], ring // 2 + 1)
            self.dve_item(v, ch, item, 6 + b, ring)
            ring += 1

    def turned_at(self, g, j):
        items = [it for _, it in self.plan if it is not None]
        return items.index(("turn", g, j))

    def dve_item(self, v, ch, item, bank, ring):
        k, kind, free = self.k, item[0], self.ring_free[ring % 2]
        if kind == "max":
            _, g, j, i, kc = item
            w = min(CH, (i + 1) * P - kc * CH)
            v.tensor_reduce(self.mp[:, j, i, kc:kc + 1], k.PS[:, bank, 0:w], AX.X, ALU.max).then_inc(free, 1)
            if (i, kc) == (NT - 1, NC - 1):
                n = 4 * g + j
                neg, part = self.neg[:, n % 2, :], self.negp[:, n % 2, :, :]
                v.wait_ge(free, ring // 2 + 1)
                v.wait_ge(self.ring_free[1 - ring % 2], (ring + 1) // 2)
                ch(v.tensor_reduce(neg, self.mp[:, j, :, :], AX.X, ALU.max, negate=True))
                if n >= 2:
                    v.wait_ge(self.max_rows[n % 2], 16 * (n // 2))
                ch(v.tensor_copy(part[:, 0, :], neg))
                ch(v.tensor_tensor(neg, neg, part[:, 0, :], ALU.subtract))
                ch(v.tensor_copy(part[:, 1, :], neg))
                v.tensor_tensor(part[:, 2, :], neg, part[:, 1, :], ALU.subtract).then_inc(self.maxima, 1)
        elif kind == "turn":
            _, g, j = item
            n = 4 * g + j
            if n >= 2:
                v.wait_ge(self.max_rows[n % 2], 16 * (n // 2))
            v.tensor_copy(self.negT[:, n % 2, :], k.PS[:, bank, :].bitcast(BF16)[0:3 * NT, 0:P]).then_inc(free, 1)
        elif kind == "sum":
            _, g, c, blk = item
            n = self.chunk(g, c)
            if self.nb * n + blk:
                v.wait_ge(self.normed, self.nb * n + blk)
            v.reciprocal(self.rec[:, :], k.bank(bank)).then_inc(free, 1)
            v.wait_ge(free, ring // 2 + 1)
            v.tensor_tensor(self.On[:, n % 2, blk, :], self.O[:, n % 2, blk, :], self.rec[:, :], ALU.mult) \
                .then_inc(self.normed, 1)
        else:
            _, g, c = item
            xc = k.X[:, c * TPC:(c + 1) * TPC, :]
            v.tensor_tensor(xc, xc, k.bank(bank).rearrange("p (n d) -> p n d", n=TPC), ALU.add).then_inc(free, 1)
            if g == self.NQ - 1:
                v.wait_ge(free, ring // 2 + 1)
                v.sem_inc(self.ready, 1)

    def x_ready(self, c):
        return [(self.ready, c + 1)]

    def stacks(self, g):
        out = []
        qb, kb = self.blocks
        for j in range(4):
            for pas, row, parts, rep, rows in qb:
                out.append(self.stack(self.Q[:, g % 2, j, pas, :], row, parts, rep, rows, *self.q_source(g, j)))
        for j in range(self.kheads):
            for pas, row, parts, rep, rows in kb:
                out.append(self.stack(self.K[:, g % 2, j, pas, :], row, parts, rep, rows, *self.k_source(g, j)))
        return out

    def stack(self, dst, row, parts, rep, rows, src, r0):
        if rep == 1 and len(parts) == 1:
            return dst[row:row + rows, :], self.scratch[src, parts[0], r0:r0 + rows, :]
        if rep > 1:
            return (dst[row:row + rep * rows, :],
                    self.scratch[src, parts[0]:parts[0] + 1, r0:r0 + rows, :].broadcast_to([rep, rows, T]))
        n = len(parts)
        return dst[row:row + n * rows, :], self.scratch[src, 0:n, r0:r0 + rows, :]

    def q_source(self, g, j):
        return (0, 8 * (4 * g + j)) if self.rotate else (g, 32 * j)

    def k_source(self, g, j):
        return (1, 8 * (4 * g + j)) if self.rotate else (2, 32 * g)

    @property
    def stack_dmas(self):
        return 4 * len(self.blocks[0]) + self.kheads * len(self.blocks[1])

    def sync(self, sp):
        ns = len(self.sources)
        if self.rotate:
            sp.wait_ge(self.ln.ready, self.ln.all_ready)
        for c in range(NC):
            if self.rotate:
                sp.wait_ge(self.split, c * ns)
                sp.dma_start(self.tab[:, :, :], self.k.d["rotation"][:, :, c * CH:(c + 1) * CH]).then_inc(self.table, 16)
            for i, (w, partner, m) in enumerate(self.sources):
                sp.wait_ge(self.split, c * ns + i + 1)
                sp.dma_start(self.scratch[i, :, 0:m, c * CH:(c + 1) * CH].rearrange("a p t -> p a t"),
                             self.parts[0:m, i % 2, :, :]).then_inc(self.stored[i], 16)
        for sem in self.stored:
            sp.wait_ge(sem, 16 * NC)
        for g in range(self.NQ):
            if g >= 2:
                sp.wait_ge(self.weighted, (g - 1) * len(self.units))
            for dst, src in self.stacks(g):
                sp.dma_start(dst, src).then_inc(self.stacked[g % 2], 16)
            for j in range(4):
                ring = self.turned_at(g, j)
                sp.wait_ge(self.ring_free[ring % 2], ring // 2 + 1)
                n = 4 * g + j
                sp.dma_start(self.Q[self.rows:self.rows + 3, g % 2, j, 0, :],
                             self.negT[:, n % 2, :]).then_inc(self.max_rows[n % 2], 16)


class FullHead(Stage):

    def __init__(self, k, name, ln):
        self.k, self.name, self.ln = k, name, ln
        s = lambda n: k.sem(name + "_" + n)
        self.projected = s("projected")
        self.q_ready = s("q_ready")
        self.k_ready = s("k_ready")
        self.vproj = s("vproj")
        self.values = s("values")
        self.tile = s("tile")
        self.scores = s("scores")
        self.maxima = s("maxima")
        self.exps = s("exps")
        self.turned = s("turned")
        self.moved = s("moved")
        self.weighted = s("weighted")
        self.added = s("added")
        self.steps = s("steps")
        self.scale = float(P ** -0.5)

    def alloc(self, ctx):
        sb = lambda n, sh, dt=F32: self.k.sb(self.name + "_" + n, sh, dt, ctx)
        self.qT = sb("qT", [P, T])
        self.kT = sb("kT", [P, T])
        self.v = sb("v", [P, NT, P])
        self.qi = sb("qi", [P, 2, P])
        self.pr = sb("pr", [P, 2, T])
        self.pT = sb("pT", [P, NT, P])
        self.neg = sb("neg", [P, 2])
        self.sum = sb("sum", [P, 2])
        self.rec = sb("rec", [P, 2])

    def tensor(self, pe):
        k = self.k
        pe.wait_ge(self.ln.ready, self.ln.all_ready)
        def turn(c):
            pe.wait_ge(self.q_ready, c)
            pe.wait_ge(self.k_ready, c)
            for i in range(2):
                ins = pe.matmul(k.bank(i), k.w3[:, i, :], k.HT[:, bass.ds(1 + c * CH, CH)], start=True, stop=True)
            ins.then_inc(self.projected, 1)

        each(pe, NC, turn)
        for c in range(NC):
            if c >= 2:
                pe.wait_ge(self.values, c - 1)
            for i in range(TPC):
                n = c * TPC + i
                ins = pe.matmul(k.PS[:, 4 + c % 2, i * P:(i + 1) * P], k.HT[:, 1 + n * P:1 + (n + 1) * P],
                                k.w3[:, 2, :], start=True, stop=True)
            ins.then_inc(self.vproj, 1)
        pe.wait_ge(self.q_ready, NC)
        pe.wait_ge(self.k_ready, NC)
        pe.wait_ge(self.values, NC)

        def scores(i, b):
            pe.wait_ge(self.tile, i + 1)
            pe.wait_ge(self.exps, i)
            for c in range(NC):
                ins = pe.matmul(k.bank(c), self.qi[:, b, :], self.kT[:, c * CH:(c + 1) * CH], start=True, stop=True)
            ins.then_inc(self.scores, 1)

        def weigh(i, b):
            pe.wait_ge(self.exps, i + 1)
            for q in range(NC):
                if q < 2:
                    pe.wait_ge(self.moved, i * NC)
                else:
                    pe.wait_ge(self.moved, i * NC + q - 1)
                for m in range(TPC):
                    n = q * TPC + m
                    ins = pe.transpose(k.PS[:, 4 + q % 2, m * P:(m + 1) * P], self.pr[:, b, n * P:(n + 1) * P],
                                       k.ident)
                ins.then_inc(self.turned, 1)
            for n in range(NT):
                if n % TPC == 0:
                    pe.wait_ge(self.moved, i * NC + n // TPC + 1)
                ins = pe.matmul(k.PS[:, 6 + b, 0:P], self.pT[:, n, :], self.v[:, n, :],
                                start=(n == 0), stop=(n == NT - 1))
            ins.then_inc(self.weighted, 1)

        scores(0, 0)
        def turn(t):
            scores(2 * t + 1, 1)
            weigh(2 * t, 0)
            scores(2 * t + 2, 0)
            weigh(2 * t + 1, 1)

        each(pe, NT // 2 - 1, turn)
        scores(NT - 1, 1)
        weigh(NT - 2, 0)
        weigh(NT - 1, 1)

    def scalar(self, s):
        k = self.k
        def turn(c):
            s.wait_ge(self.projected, c + 1)
            s.activation(self.qT[:, bass.ds(c * CH, CH)], k.bank(0), ACT.Identity, bias=k.vec[:, 7:8]) \
                .then_inc(self.q_ready, 1)

        each(s, NC, turn)
        s.wait_ge(self.q_ready, NC)

        def tile(i, b):
            s.activation(self.qi[:, b, :], self.qT[:, bass.ds(i * P, P)], ACT.Copy).then_inc(self.tile, 1)

        def exps(i, b):
            s.wait_ge(self.maxima, i + 1)
            s.activation(self.pr[:, b, :], k.PS[:, 0:NC, :].rearrange("p c n -> p (c n)"), ACT.Exp,
                         bias=self.neg[:, b:b + 1], scale=self.scale, accum_out=self.sum[:, b:b + 1]) \
                .then_inc(self.exps, 1)

        def move(i, b):
            for q in range(NC):
                s.wait_ge(self.turned, i * NC + q + 1)
                if q == 0:
                    s.wait_ge(self.weighted, i)
                s.activation(self.pT[:, q * TPC:(q + 1) * TPC, :],
                             k.bank(4 + q % 2).rearrange("p (n d) -> p n d", n=TPC), ACT.Copy) \
                    .then_inc(self.moved, 1)

        tile(0, 0)
        tile(1, 1)
        exps(0, 0)
        def turn(t):
            move(2 * t, 0)
            tile(2 * t + 2, 0)
            exps(2 * t + 1, 1)
            move(2 * t + 1, 1)
            tile(2 * t + 3, 1)
            exps(2 * t + 2, 0)

        each(s, NT // 2 - 1, turn)
        move(NT - 2, 0)
        exps(NT - 1, 1)
        move(NT - 1, 1)

    def vector(self, v):
        k = self.k
        def turn(c):
            v.wait_ge(self.projected, c + 1)
            v.tensor_scalar(self.kT[:, bass.ds(c * CH, CH)], k.bank(1), k.vec[:, 8:9], None, ALU.add) \
                .then_inc(self.k_ready, 1)

        each(v, NC, turn)
        for c in range(NC):
            v.wait_ge(self.vproj, c + 1)
            v.tensor_tensor(self.v[:, c * TPC:(c + 1) * TPC, :],
                            k.bank(4 + c % 2).rearrange("p (n d) -> p n d", n=TPC),
                            k.bv[:, :].rearrange("p (a d) -> p a d", a=1).broadcast_to([P, TPC, P]), ALU.add) \
                .then_inc(self.values, 1)

        def maxima(i, b, first=0):
            v.wait_ge(self.scores, i + 1)
            v.tensor_reduce(self.neg[:, b:b + 1], k.PS[:, 0:NC, :].rearrange("p c n -> p (c n)"), AX.X, ALU.max,
                            negate=True).then_inc(self.steps, 1)
            v.wait_ge(self.steps, first + 2 * i)
            v.tensor_scalar(self.neg[:, b:b + 1], self.neg[:, b:b + 1], self.scale, None, ALU.mult) \
                .then_inc(self.maxima, 1)

        def add(i, b):
            v.wait_ge(self.weighted, i + 1)
            v.reciprocal(self.rec[:, b:b + 1], self.sum[:, b:b + 1]).then_inc(self.steps, 1)
            v.wait_ge(self.steps, 2 * i + 3)
            xi = k.X[:, bass.ds(i, 1), :].rearrange("p a d -> p (a d)")
            v.scalar_tensor_tensor(xi, k.PS[:, 6 + b, 0:P], self.rec[:, b:b + 1], xi, ALU.mult, ALU.add) \
                .then_inc(self.added, 1)

        maxima(0, 0, first=1)
        def turn(t):
            maxima(2 * t + 1, 1)
            add(2 * t, 0)
            maxima(2 * t + 2, 0)
            add(2 * t + 1, 1)

        each(v, NT // 2 - 1, turn)
        maxima(NT - 1, 1)
        add(NT - 2, 0)
        i = NT - 1
        v.wait_ge(self.weighted, i + 1)
        v.reciprocal(self.rec[:, 1:2], self.sum[:, 1:2]).then_inc(self.steps, 1)
        v.wait_ge(self.steps, 2 * NT)
        v.scalar_tensor_tensor(k.X[:, i, :], k.PS[:, 7, 0:P], self.rec[:, 1:2], k.X[:, i, :], ALU.mult, ALU.add) \
            .then_inc(self.added, 1)

    def x_ready(self, c):
        return [(self.added, (c + 1) * TPC)]


CST_ORDER = N_CST * P
CST_COLS = N_CST * P + 8


def constants():
    c = np.zeros((P, CST_COLS), np.float32)
    r = np.arange(P)
    c[:, 0:P] = np.eye(P)
    same = (r[:, None] // 8 == r[None, :] // 8).astype(np.float32)
    c[:, P:2 * P] = same
    c[:, 2 * P:3 * P] = same / 8
    c[:, 3 * P:4 * P] = (r[:, None] // 32 == r[None, :] // 32) & (r[:, None] % 32 == 8)
    c[:, 4 * P:5 * P] = (r[:, None] // 64 == r[None, :] // 64) & (r[:, None] % 64 == 32)
    for j in range(8):
        c[:, (5 + j) * P:(6 + j) * P] = same * (r[None, :] % 8 == j)
    c[:, 13 * P:14 * P] = np.where(r[None, :] > r[:, None], MASKED, 0.0)
    c[:, 14 * P:15 * P] = np.where(r[:, None] > r[None, :], MASKED, 0.0)
    c[:, CST_ORDER:] = 8 - np.arange(8)
    return c


def rotation():
    freqs = (np.float32(1.0) / np.float32(10000.0) ** (np.arange(0, 8, 2, dtype=np.float32) / np.float32(8))) \
        .astype(np.float32)
    ang = np.outer(freqs, np.arange(T, dtype=np.float32)).astype(np.float32)
    p = np.arange(P)
    a = ang[(p % 8) // 2]
    sign = np.where(p % 2 == 0, -1.0, 1.0).astype(np.float32)[:, None]
    return np.ascontiguousarray(np.stack([np.cos(a), sign * np.sin(a)], axis=1).astype(np.float32))


INPUTS = ["L0_attn_a_x", "L0_attn_a_W_r", "L0_attn_a_W_k", "L0_attn_a_W_v", "L0_attn_a_W_w", "L0_attn_a_W_o",
          "L0_attn_a_u", "L0_attn_a_tm_r", "L0_attn_a_tm_k", "L0_attn_a_tm_v", "L0_attn_a_tm_w", "L0_attn_a_ln_w",
          "L0_attn_a_ln_b", "L0_attn_b_W_qkv", "L0_attn_b_W_out", "L0_ffn_Wg", "L0_ffn_bg", "L0_ffn_W1", "L0_ffn_b1",
          "L0_ffn_W2", "L0_ffn_b2", "L1_attn_a_W_q", "L1_attn_a_W_k", "L1_attn_a_W_v", "L1_attn_a_b_q",
          "L1_attn_a_b_k", "L1_attn_a_b_v", "L1_attn_b_wq", "L1_attn_b_wk_down", "L1_attn_b_wv_down",
          "L1_attn_b_wk_up", "L1_attn_b_wv_up", "L1_attn_b_wo", "L1_ffn_W1", "L1_ffn_b1", "L1_ffn_W2", "L1_ffn_b2",
          "L1_ffn_ln_gamma", "L1_ffn_ln_beta", "L1_ffn_Wr", "L1_ffn_br"]


def build(nc, d, upto=8, start=0):
    with ExitStack() as ctx:
        k = Kernel(nc, ctx, d)
        k.setup = Setup(k)
        perturb = Perturb(k)
        stages = []
        x_ready = lambda c: [(k.setup.loaded_x, 16), (k.setup.ready, 1)]

        def norm():
            ln = LayerNorm(k, k.X, k.H, k.HT, x_ready)
            stages.append(ln)
            return ln

        def experts0(name):
            ln = norm()
            r = Router(k, name + "_router", ln.dst_t, ln, k.wg[:, :], k.bg, True)
            e = Experts(k, name, ln.dst_t, ln, r, lambda e, m: k.w0[:, e, m * P:(m + 1) * P],
                        lambda e, m: k.w0b[:, e, m, :], lambda e, m: k.b0[:, e, m:m + 1], k.seed0, ACT.Gelu, 8, 2)
            with ExitStack() as arena:
                e.alloc(arena)
            stages.extend([r, e])
            return e.x_ready

        def rope_attention():
            ln = norm()
            blocks = ([(0, 24 * a, [a], 3, 8) for a in range(3)], [(0, 24 * a, [0, 1, 2], 1, 8) for a in range(3)])
            a = CausalHeads(k, "rope", ln, 4, [(k.wqkvT[:, i, :], k.wqkvT[:, 3 + i, :], P) for i in range(2)],
                            blocks, 72, 4, k.wqkvT[:, 2, :], 16, 8, float(8 ** -0.5), k.den_rope, k.woutT, 1,
                            d["rope_parts"], True)
            with ExitStack() as arena:
                a.alloc(arena)
            stages.append(a)
            return a.x_ready

        def rwkv():
            ln = norm()
            rw = Rwkv(k, ln.dst_t, ln)
            with ExitStack() as arena:
                k.setup.alloc(arena)
                rw.alloc(arena)
            stages.append(rw)
            return lambda c: [(rw.ready, c + 1)]

        if start:
            with ExitStack() as arena:
                k.setup.alloc(arena)
        def full_attention():
            ln = norm()
            a = FullHead(k, "full", ln)
            with ExitStack() as arena:
                a.alloc(arena)
            stages.append(a)
            return a.x_ready

        def experts1(name, first):
            with ExitStack() as arena:
                ln = norm()
                h2 = k.sb(name + "_h2", [P, NT, P], F32, arena)
                h2t = k.sb(name + "_h2t", [P, 1 + T], F32, arena)
                if first:
                    stages.append(PerturbedRows(perturb))
                inner = LayerNorm(k, k.H, h2, h2t, lambda c: [(k.ln_mem.normed, ln.chunk_ready(c))],
                                  gamma=k.vec[:, 9:10], beta=k.vec[:, 10:11], banks=(4, 5, 6, 7))
                r = Router(k, name + "_router", h2t, inner, k.wr[:, :], k.br, False)
                e = Experts(k, name, k.HT, ln, r, lambda e, m: k.w1[:, e, m * P:(m + 1) * P],
                            lambda e, m: k.w1b[:, e, m, :], lambda e, m: k.b1[:, e, m:m + 1], k.seed1,
                            ACT.Gelu_apprx_tanh, 2, 4, needs=[(perturb.rows_split, 8), (perturb.ready, 16)])
                e.alloc(arena)
            stages.extend([inner, r, e])
            return e.x_ready

        def latent_attention():
            ln = norm()
            qb = [(0, 0, [0], 2, 32), (0, 64, [1], 1, 32), (1, 0, [1], 1, 32), (1, 32, [0], 1, 32), (1, 64, [2], 1, 32)]
            kb = [(0, 0, [0], 1, 32), (0, 32, [1], 1, 32), (0, 64, [0], 1, 32),
                  (1, 0, [1], 1, 32), (1, 32, [2], 1, 32), (1, 64, [0], 1, 32)]
            sources = [(k.wc[:, 4 * g:4 * g + 4, :].rearrange("p h l -> p (h l)"), None, P) for g in range(2)]
            a = CausalHeads(k, "latent", ln, 2, sources + [(k.wkv[:, :, :].rearrange("p a l -> p (a l)"), None, P)], (qb, kb), 96, 1,
                            k.wkv[:, 1, :], 2, 32, float(P ** -0.5), k.den_latent, k.wy, 2, d["latent_parts"], False)
            with ExitStack() as arena:
                a.alloc(arena)
            stages.append(a)
            return a.x_ready

        makers = [rwkv, lambda: experts0("moe1"), rope_attention, lambda: experts0("moe2"), full_attention,
                  lambda: experts1("ffn1", True), latent_attention, lambda: experts1("ffn2", int(start) == 7)]
        for make in makers[start:int(upto)]:
            x_ready = make()
        stored = k.sem("stored")
        block = ctx.enter_context(nc.Block())
        out = d["out"][0].rearrange("(n p) d -> p n d", p=P)

        @block.sync
        def _(sp):
            k.setup.sync(sp)
            for s in stages:
                s.sync(sp)
            for c in range(NC):
                for sem, val in x_ready(c):
                    sp.wait_ge(sem, val)
                sp.dma_start(out[:, c * TPC:(c + 1) * TPC, :], k.X[:, c * TPC:(c + 1) * TPC, :]) \
                    .then_inc(stored, 16)
            sp.wait_ge(stored, 16 * NC)

        @block.gpsimd
        def _(g):
            k.setup.gpsimd(g)
            for s in stages:
                s.gpsimd(g)
            perturb.gpsimd(g)
            g.wait_ge(perturb.ready, 16)

        @block.tensor
        def _(pe):
            k.setup.tensor(pe)
            for s in stages:
                s.tensor(pe)

        @block.scalar
        def _(act):
            for s in stages:
                s.scalar(act)

        @block.vector
        def _(v):
            k.setup.vector(v)
            for s in stages:
                s.vector(v)


def scratch(nc, d):
    d["b2_scratch"] = nc.dram_tensor("b2_scratch", (2 * P,), F32).ap()
    d["rope_parts"] = nc.dram_tensor("rope_parts", (2, 3, P, T), BF16).ap()
    d["latent_parts"] = nc.dram_tensor("latent_parts", (3, 3, P, T), BF16).ap()


def kernel(**inputs):
    import concourse.bacc as bacc
    from concourse.bass_utils import run_bass_kernel_spmd

    nc = bacc.Bacc("TRN2", target_bir_lowering=False, num_devices=1)
    arrays = {f"in_{n}": np.ascontiguousarray(inputs[n]) for n in INPUTS}
    arrays["in_const"] = constants()
    arrays["in_rotation"] = rotation()
    d = {n[3:]: nc.dram_tensor(n, a.shape, F32, kind="ExternalInput").ap() for n, a in arrays.items()}
    d["out"] = nc.dram_tensor("out", (1, T, P), F32, kind="ExternalOutput").ap()
    scratch(nc, d)
    build(nc, d)
    r = run_bass_kernel_spmd(nc, [arrays], core_ids=[0])
    return r.results[0]["out"]
```

```python
from contextlib import ExitStack

import numpy as np
import concourse.bass as bass
from concourse import mybir

F32 = mybir.dt.float32
BF16 = mybir.dt.bfloat16
I32 = mybir.dt.int32
ALU = mybir.AluOpType
ACT = mybir.ActivationFunctionType
AX = mybir.AxisListType
RADD = bass.bass_isa.ReduceOp.add

P = 128
T = 2048
NT = T // P
CH = 512
NC = T // CH
TPC = CH // P
MASKED = -1.0e30
LOWEST = -3.0e38


class Stage:

    def sync(self, sp):
        pass

    def gpsimd(self, g):
        pass

    def tensor(self, pe):
        pass

    def scalar(self, s):
        pass

    def vector(self, v):
        pass


def each(eng, turns, body):
    body(0)
    with eng.Fori(1, turns) as turn:
        body(turn)


class Chain:

    def __init__(self, eng, sem, base=0):
        self.eng, self.sem, self.base, self.n = eng, sem, base, 0

    def mark(self, ins):
        self.n += 1
        return ins.then_inc(self.sem, 1)

    def wait(self):
        self.eng.wait_ge(self.sem, self.base + self.n)

    def __call__(self, ins):
        self.mark(ins)
        self.wait()


class Kernel:

    def __init__(self, nc, ctx, dram):
        self.nc, self.ctx, self.d = nc, ctx, dram
        self.n_sem = 0
        sb = self.sb
        self.X = sb("X", [P, NT, P])
        self.H = sb("H", [P, NT, P])
        self.HT = sb("HT", [P, 1 + T])
        self.cst = sb("cst", [P, CST_COLS])
        self.gates = sb("gates", [P, NT, 8])
        self.experts_mem = ExpertsMemory(self)
        self.router_mem = RouterMemory(self)
        self.ident = self.cst[:, 0:P]
        self.group_sum = self.cst[:, P:2 * P]
        self.group_mean = self.cst[:, 2 * P:3 * P]
        self.den_rope = self.cst[:, 3 * P:4 * P]
        self.ones_col = self.cst[:, 4 * P:4 * P + 32]
        self.mask_qk = sb("mask_qk", [P, P], BF16)
        self.mask_kq = sb("mask_kq", [P, P], BF16)
        self.identb = sb("identb", [P, P], BF16)
        self.onesb = sb("onesb", [P, P], BF16)
        self.eps = sb("eps", [P, 1])
        self.PS = ctx.enter_context(nc.psum_tensor("PS", [P, 8, CH], F32))

    def sb(self, name, shape, dt=F32, ctx=None):
        return (ctx or self.ctx).enter_context(self.nc.sbuf_tensor("sb_" + name, shape, dt))

    def sem(self, name):
        self.n_sem += 1
        return self.ctx.enter_context(self.nc.semaphore(name))

    def bank(self, b, cols=CH):
        return self.PS[:, b, 0:cols]


N_CST = 5 + 8 + 2


class NormMemory:

    def __init__(self, k):
        self.stats = k.sb("stats", [P, NT, 6])
        self.mv = k.sb("mv", [P, NT, 2])
        self.sd = k.sb("sd", [P, NT])
        self.rstd = k.sb("rstd", [P, NT])
        self.uses = 0
        self.moments = k.sem("ln_moments")
        self.deviation = k.sem("ln_deviation")
        self.normed = k.sem("ln_normed")
        self.turned = k.sem("ln_turned")
        self.ready = k.sem("ln_ready")
        self.steps = k.sem("ln_steps")


class ExpertsMemory:

    def __init__(self, k):
        self.hid = [k.sem(f"hid{b}") for b in range(4)]
        self.hid_used = [k.sem(f"hid_used{b}") for b in range(4)]
        self.out = [k.sem(f"expert{b}") for b in range(2)]
        self.out_used = [k.sem(f"expert_used{b}") for b in range(2)]
        self.ready = k.sem("experts_ready")
        self.hid_count = self.out_count = self.ready_count = 0


class RouterMemory:

    def __init__(self, k):
        self.logits = k.sem("logits")
        self.read = k.sem("logits_read")
        self.shifted = k.sem("logits_shifted")
        self.exps = k.sem("router_exps")
        self.steps = k.sem("router_steps")
        self.uses = self.step_count = 0
        self.p = k.sb("rt_p", [P, NT, 8])
        self.a = k.sb("rt_a", [P, NT, 1])
        self.left = k.sb("rt_left", [P, NT, 8])
        self.sel = k.sb("rt_sel", [P, 2, NT, 8])


class LayerNorm(Stage):

    def __init__(self, k, src, dst, dst_t, src_ready, gamma=None, beta=None, banks=(0, 1, 2, 3)):
        self.k, self.src, self.dst, self.dst_t = k, src, dst, dst_t
        self.src_ready, self.gamma, self.beta, self.banks = src_ready, gamma, beta, banks
        self.mem = k.ln_mem
        self.use = self.mem.uses
        self.mem.uses += 1
        self.ready = self.mem.ready

    def chunk_ready(self, c):
        return self.use * NC + c + 1

    @property
    def all_ready(self):
        return self.use * NC + NC

    def vector(self, v):
        m, first = self.mem, self.use * (NT + 1)
        for c in range(NC):
            for sem, val in self.src_ready(c):
                v.wait_ge(sem, val)
            for n in range(c * TPC, (c + 1) * TPC):
                v.bn_stats(m.stats[:, n, :], self.src[:, n, :]).then_inc(m.steps, 1)
        for n in range(NT):
            v.wait_ge(m.steps, first + n + 1)
            ins = v.bn_aggr(m.mv[:, n, :], m.stats[:, n, :])
        ins.then_inc(m.moments, 1)
        v.wait_ge(m.deviation, self.use + 1)
        v.reciprocal(m.rstd[:, :], m.sd[:, :]).then_inc(m.steps, 1)
        v.wait_ge(m.steps, first + NT + 1)
        for n in range(NT):
            ins = v.tensor_scalar(self.dst[:, n, :], self.src[:, n, :], m.mv[:, n, 0:1], m.rstd[:, n:n + 1],
                                  ALU.subtract, ALU.mult)
            if n % TPC == TPC - 1:
                ins.then_inc(m.normed, 1)

    def tensor(self, pe):
        for c in range(NC):
            pe.wait_ge(self.mem.normed, self.chunk_ready(c))
            for i in range(TPC):
                ins = pe.transpose(self.k.PS[:, self.banks[c], i * P:(i + 1) * P], self.dst[:, c * TPC + i, :],
                                   self.k.ident)
            ins.then_inc(self.mem.turned, 1)

    def scalar(self, s):
        m = self.mem
        s.wait_ge(m.moments, self.use + 1)
        s.activation(m.sd[:, :], m.mv[:, :, 1], ACT.Sqrt, bias=self.k.eps[:, :]).then_inc(m.deviation, 1)
        for c in range(NC):
            s.wait_ge(m.turned, self.chunk_ready(c))
            out = self.dst_t[:, 1 + c * CH:1 + (c + 1) * CH]
            if self.gamma is None:
                s.activation(out, self.k.bank(self.banks[c]), ACT.Copy).then_inc(m.ready, 1)
            else:
                s.activation(out, self.k.bank(self.banks[c]), ACT.Identity, bias=self.beta,
                             scale=self.gamma).then_inc(m.ready, 1)


class Setup:

    def __init__(self, k):
        self.k = k
        sb = k.sb
        nc = k.nc
        self.loaded = k.sem("loaded")
        self.loaded_x = k.sem("loaded_x")
        self.turned = [k.sem(f"weights_turned{i}") for i in range(2)]
        self.copied = [k.sem(f"weights_copied{i}") for i in range(2)]
        self.steps = k.sem("setup_steps")
        self.ready = k.sem("setup_ready")
        self.zeroed = k.sem("setup_zeroed")
        self.pool = k.sem("setup_pool")
        k.ln_mem = NormMemory(k)
        k.w0 = sb("w0", [P, 8, 256])
        k.w0b = sb("w0b", [P, 8, 2, P])
        k.wg = sb("wg", [P, 8])
        k.bg = sb("bg", [P, 8])
        k.w1 = sb("w1", [P, 2, CH])
        k.w1b = sb("w1b", [P, 2, 4, P])
        k.b1 = sb("b1", [P, 2, 4])
        k.b1col = sb("b1col", [P, 2])
        k.wr = sb("wr", [P, 8])
        k.br = sb("br", [P, 8])
        k.vec = sb("vec", [P, 32])
        k.b0 = k.vec[:, 16:32].rearrange("p (e m) -> p e m", m=2)
        k.seed0 = sb("seed0", [3, 8, P], BF16)
        k.seed1 = sb("seed1", [3, 2, P], BF16)
        k.wqkvT = sb("wqkvT", [P, 5, P])
        k.woutT = sb("woutT", [P, 4, P])
        k.bv = sb("bv", [P, P])
        k.w3 = sb("w3", [P, 3, P])
        k.wkv = sb("wkv", [P, 2, 64])
        k.wc = sb("wc", [P, 8, 32])
        k.wy = sb("wy", [P, 2, P])

        self.n_zeroed = 4

    def alloc(self, ctx):
        sb = lambda n, sh, dt=F32: self.k.sb(n, sh, dt, ctx)
        self.k.wT = sb("wT", [P, 5, P])
        self.k.wvrep = sb("wvrep", [P, 8, P])
        self.rows = sb("rows", [32, P])
        self.wraw = sb("wraw", [P, 9, P])
        self.wpad = sb("wpad", [P, 4, 4, 32])
        self.wq = sb("wq", [P, 8, P])
        self.wqT = sb("wqT", [P, 8, P])
        self.wup = sb("wup", [32, 2, P])
        self.wkupT = sb("wkupT", [P, 32])
        self.wvupT = sb("wvupT", [P, 32])
        self.wo = sb("wo", [P, 8, P])
        self.row0 = sb("row0", [3, 8, P])
        self.rowr = sb("rowr", [3, 8, P])
        self.rowb = sb("rowb", [3, 8, P], BF16)
        self.n_loaded = 16 * len(self.loads())

    def loads(self):
        k, d = self.k, self.k.d
        out = []

        def load(dst, src):
            out.append((dst, src))

        load(k.cst[:, :], d["const"])
        for i, w in enumerate((d["L0_attn_a_W_r"], d["L0_attn_a_W_k"], d["L0_attn_a_W_v"], d["L0_attn_a_W_w"], d["L0_attn_a_W_o"])):
            load(self.wraw[:, i, :], w)
        load(self.wraw[:, 5:8, :], d["L0_attn_b_W_qkv"].rearrange("(n p) d -> p n d", p=P))
        load(self.wraw[:, 8, :], d["L0_attn_b_W_out"])
        load(self.wq[:, :, :], d["L1_attn_b_wq"].rearrange("p (h d) -> p h d", h=8))
        load(self.wup[:, 0, :], d["L1_attn_b_wk_up"])
        load(self.wup[:, 1, :], d["L1_attn_b_wv_up"])
        load(self.wo[:, :, :], d["L1_attn_b_wo"].rearrange("(h p) n -> p h n", p=P))
        load(k.wkv[:, 0, :], d["L1_attn_b_wk_down"])
        load(k.wkv[:, 1, :], d["L1_attn_b_wv_down"])
        for i, w in enumerate((d["L0_attn_a_tm_r"], d["L0_attn_a_tm_k"], d["L0_attn_a_tm_v"], d["L0_attn_a_tm_w"],
                               d["L0_attn_a_u"].rearrange("h d -> (h d)"))):
            load(self.rows[i:i + 1, :], w.rearrange("(a p) -> a p", a=1))
        for i, w in ((5, d["L0_attn_a_ln_w"]), (6, d["L0_attn_a_ln_b"])):
            load(self.rows[i:i + 1, :].rearrange("a (h d) -> a h d", h=16),
                 w.rearrange("(a b d) -> a b d", a=1, b=1).broadcast_to([1, 16, 8]))
        for i, w in ((7, d["L1_attn_a_b_q"]), (8, d["L1_attn_a_b_k"]), (9, d["L1_ffn_ln_gamma"]), (10, d["L1_ffn_ln_beta"]),
                     (11, d["L1_ffn_b2"])):
            load(self.rows[i:i + 1, :], w.rearrange("(a p) -> a p", a=1))
        load(self.rows[12:16, :], d["L1_ffn_b1"].rearrange("(m p) -> m p", p=P))
        load(self.rows[16:32, :], d["L0_ffn_b1"].rearrange("e (m p) -> (e m) p", p=P))
        for i, w in enumerate((d["L1_attn_a_W_q"], d["L1_attn_a_W_k"], d["L1_attn_a_W_v"])):
            load(k.w3[:, i, :], w)
        load(k.bv[:, :], d["L1_attn_a_b_v"].rearrange("(a p) -> a p", a=1).broadcast_to([P, P]))
        load(k.w0[:, :, :], d["L0_ffn_W1"].rearrange("e d h -> d e h"))
        for e in range(8):
            load(k.w0b[:, e, :, :], d["L0_ffn_W2"][e].rearrange("(m p) d -> p m d", p=P))
        load(k.wg[:, :], d["L0_ffn_Wg"])
        load(k.bg[:, :], d["L0_ffn_bg"].rearrange("(a e) -> a e", a=1).broadcast_to([P, 8]))
        load(self.row0[:, :, :], d["L0_ffn_b2"].rearrange("(a e) d -> a e d", a=1).broadcast_to([3, 8, P]))
        load(k.w1[:, 0, :], d["L1_ffn_W1"])
        load(k.w1b[:, 0, :, :], d["L1_ffn_W2"].rearrange("(m p) d -> p m d", p=P))
        load(k.wr[:, :], d["L1_ffn_Wr"])
        load(k.br[:, :], d["L1_ffn_br"].rearrange("(a e) -> a e", a=1).broadcast_to([P, 8]))
        return out

    def sync(self, sp):
        sp.dma_start(self.k.X[:, :, :], self.k.d["L0_attn_a_x"][0].rearrange("(n p) d -> p n d", p=P)) \
            .then_inc(self.loaded_x, 16)
        for dst, src in self.loads():
            sp.dma_start(dst, src).then_inc(self.loaded, 16)

    def gpsimd(self, g):
        k = self.k
        g.memset(k.eps[:, :], 1e-5).then_inc(self.zeroed, 1)
        g.memset(k.onesb[:, :], 1.0).then_inc(self.zeroed, 1)
        g.memset(self.wpad[:, :, :, :], 0.0).then_inc(self.zeroed, 1)
        g.memset(k.HT[:, 0:1], 0.0).then_inc(self.zeroed, 1)

    def groups(self):
        k = self.k
        raw = [self.wraw[:, i, :] for i in range(8)]
        pads = [self.wpad[:, g, :, :].rearrange("p j c -> p (j c)") for g in range(4)]
        return [(raw[0:4], k.wT[:, 0:4, :]), (raw[4:5], k.wT[:, 4:5, :]), (raw[5:8], k.wqkvT[:, 0:3, :]),
                (pads, k.woutT[:, :, :]), ([self.wq[:, i, :] for i in range(4)], self.wqT[:, 0:4, :]),
                ([self.wq[:, i, :] for i in range(4, 8)], self.wqT[:, 4:8, :])]

    def tensor(self, pe):
        k = self.k
        pe.wait_ge(self.loaded, self.n_loaded)
        pe.wait_ge(self.steps, 1)
        n = 0
        for ins_, _ in self.groups():
            pe.wait_ge(self.copied[n % 2], n // 2)
            for i, a in enumerate(ins_):
                ins = pe.transpose(k.PS[:, n % 2, i * P:(i + 1) * P], a, k.ident)
            ins.then_inc(self.turned[n % 2], 1)
            n += 1
        pe.wait_ge(self.copied[n % 2], n // 2)
        for i in range(2):
            pe.transpose(k.PS[:, n % 2, i * 32:(i + 1) * 32], self.wup[:, i, :], k.cst[0:32, 0:32])
        ins = pe.transpose(k.PS[:, n % 2, 64:96], self.rows[:, :], k.cst[0:32, 0:32])
        ins.then_inc(self.turned[n % 2], 1)
        n += 1
        pe.wait_ge(self.copied[(n - 1) % 2], (n - 1) // 2 + 1)
        pe.wait_ge(self.copied[n % 2], n // 2)
        for h in range(8):
            ins = pe.matmul(k.PS[:, n % 2, h * 32:(h + 1) * 32], self.wqT[:, h, :], self.wkupT[:, :],
                            start=True, stop=True)
        ins.then_inc(self.turned[n % 2], 1)
        n += 1
        pe.wait_ge(self.copied[n % 2], n // 2)
        for h in range(8):
            g, j = h // 4, h % 4
            ins = pe.matmul(k.PS[32 * j:32 * j + 32, n % 2, g * P:(g + 1) * P], self.wvupT[:, :], self.wo[:, h, :],
                            start=True, stop=True)
        ins.then_inc(self.turned[n % 2], 1)

    def vector(self, v):
        k, ch = self.k, Chain(v, self.steps)
        v.wait_ge(self.loaded, self.n_loaded)
        v.wait_ge(self.zeroed, self.n_zeroed)
        ch(v.tensor_copy(self.wpad[:, :, :, 0:8], self.wraw[:, 8, :].rearrange("p (g j d) -> p g j d", g=4, j=4)))
        ch(v.tensor_copy(k.identb[:, :], k.ident))
        ch(v.tensor_copy(k.mask_qk[:, :], k.cst[:, (5 + 8) * P:(6 + 8) * P]))
        ch(v.tensor_copy(k.mask_kq[:, :], k.cst[:, (6 + 8) * P:(7 + 8) * P]))
        n = 0
        for _, out in self.groups():
            v.wait_ge(self.turned[n % 2], n // 2 + 1)
            w = out.shape[1]
            v.tensor_copy(out, k.PS[:, n % 2, 0:w * P].rearrange("p (n d) -> p n d", n=w)) \
                .then_inc(self.copied[n % 2], 1)
            n += 1
        v.wait_ge(self.turned[n % 2], n // 2 + 1)
        ch(v.tensor_copy(self.wkupT[:, :], k.PS[:, n % 2, 0:32]))
        ch(v.tensor_copy(k.vec[:, :], k.PS[:, n % 2, 64:96]))
        ch(v.tensor_copy(k.b1[:, 0, :], k.vec[:, 12:16]))
        ch(v.tensor_copy(k.b1col[:, 0:1], k.vec[:, 11:12]))
        v.tensor_copy(self.wvupT[:, :], k.PS[:, n % 2, 32:64]).then_inc(self.copied[n % 2], 1)
        n += 1
        v.wait_ge(self.turned[n % 2], n // 2 + 1)
        v.tensor_copy(k.wc[:, :, :], k.PS[:, n % 2, 0:256].rearrange("p (h l) -> p h l", h=8)) \
            .then_inc(self.copied[n % 2], 1)
        n += 1
        v.wait_ge(self.turned[n % 2], n // 2 + 1)
        v.tensor_copy(k.wy[:, :, :], k.PS[:, n % 2, 0:2 * P].rearrange("p (h l) -> p h l", h=2)) \
            .then_inc(self.copied[n % 2], 1)
        n += 1
        v.wait_ge(self.copied[0], 5)
        v.wait_ge(self.copied[1], 4)
        for j in range(8):
            ch(v.tensor_copy(k.wvrep[:, j, :].rearrange("p (h i) -> p h i", h=16),
                             k.wT[:, 2, :].rearrange("p (h i) -> p h i", h=16)[:, :, j:j + 1]
                             .broadcast_to([P, 16, 8])))
        for i in range(2):
            for a in range(2):
                ch(v.tensor_copy(k.wqkvT[:, 3 + i, :].rearrange("p (m a) -> p m a", a=2)[:, :, a:a + 1],
                                 k.wqkvT[:, i, :].rearrange("p (m a) -> p m a", a=2)[:, :, 1 - a:2 - a]))
        split_rows(ch, v, self.row0[:, :, :], self.rowr[:, :, :], self.rowb[:, :, :], k.seed0[:, :, :], k)
        v.tensor_copy(self.rowb[:, 0, :], self.rowb[:, 0, :]).then_inc(self.ready, 1)


def split_rows(ch, v, full, rest, part, out, k):
    for r in range(3):
        src = full if r == 0 else rest
        ch(v.tensor_copy(part, src))
        if r == 0:
            ch(v.tensor_scalar(out, part, k.cst[0:3, 0:1], None, ALU.mult))
        else:
            ch(v.scalar_tensor_tensor(out, part, k.cst[0:3, r:r + 1], out, ALU.mult, ALU.add))
        if r < 2:
            ch(v.tensor_tensor(rest, src, part, ALU.subtract))


class Perturb:

    def __init__(self, k):
        self.k = k
        sb = k.sb
        self.steps = k.sem("perturb_steps")
        self.ready = k.sem("perturb_ready")
        self.b2_out = k.sem("perturb_b2_out")
        self.rows_split = k.sem("perturb_rows_split")
        self.a = sb("pa", [P, 2, CH])
        self.ab = sb("pab", [P, 4])
        self.ac = sb("pac", [P, 1])
        self.below = sb("pbelow", [P, 2, 2, CH])
        self.belowb = sb("pbelowb", [P, 2, 4])
        self.cnt = sb("pcnt", [P, 8])
        self.tot = sb("ptot", [P, 8])
        self.rank = sb("prank", [P, 8])
        self.found = sb("pfound", [P, 8], I32)
        self.trial = sb("ptrial", [P, 8], I32)
        self.keep = sb("pkeep", [P, 8], I32)
        self.bit = sb("pbit", [P, 8], I32)
        self.bitf = sb("pbitf", [P, 8])
        self.row1 = sb("prow1", [3, 2, P])
        self.rowr = sb("prowr", [3, 2, P])
        self.rowb = sb("prowb", [3, 2, P], BF16)

    def gpsimd(self, g):
        k = self.k
        ch = Chain(g, self.steps)
        g.wait_ge(k.setup.ready, 1)
        w2 = k.w1b[:, 0, :, :].rearrange("p m d -> p (m d)")
        for i, n in enumerate((P * CH, P * CH, CH, P)):
            kth = max(1, int(n * 0.1 / 2))
            ch(g.memset(self.rank[:, 2 * i:2 * i + 1], float(kth - 1)))
            ch(g.memset(self.rank[:, 2 * i + 1:2 * i + 2], float(n - kth)))
        ch(g.memset(self.found[:, :], 0))
        ch(g.memset(self.bitf[:, :], float(1 << 30)))
        for out, src in ((self.a[:, 0, :], k.w1[:, 0, :]), (self.a[:, 1, :], w2), (self.ab[:, :], k.b1[:, 0, :]),
                         (self.ac[:, :], k.b1col[:, 0:1])):
            low = self.below[:, 0, 0, 0:src.shape[-1]]
            ch(g.tensor_scalar(low, src, -1.0, 0.0, ALU.mult, ALU.max))
            ch(g.tensor_scalar(out, src, 0.0, None, ALU.max))
            ch(g.tensor_tensor(out, out, low, ALU.add))
        g.sem_clear(self.steps)
        with g.Fori(0, 31):
            ch = Chain(g, self.steps)
            tr = self.trial[:, :].bitcast(F32)
            ch(g.tensor_scalar(self.bit[:, :], self.bitf[:, :], 1.0, None, ALU.mult))
            ch(g.tensor_tensor(self.trial[:, :], self.found[:, :], self.bit[:, :], ALU.add))
            for s in range(2):
                for w in range(2):
                    ch.mark(g.tensor_scalar(self.below[:, w, s, :], self.a[:, w, :], tr[:, 2 * w + s:2 * w + s + 1],
                                            None, ALU.is_lt))
                ch.mark(g.tensor_scalar(self.belowb[:, s, :], self.ab[:, :], tr[:, 4 + s:5 + s], None, ALU.is_lt))
                ch(g.tensor_scalar(self.cnt[:, 6 + s:7 + s], self.ac[:, :], tr[:, 6 + s:7 + s], None, ALU.is_lt))
            bl = self.below[:, :, :, :].rearrange("p w s n -> p (w s) n")
            n = CH // 2
            while n > 1:
                ch(g.tensor_tensor(bl[:, :, 0:n], bl[:, :, 0:n], bl[:, :, n:2 * n], ALU.add))
                n //= 2
            ch.mark(g.tensor_tensor(self.cnt[:, 0:4], bl[:, :, 0], bl[:, :, 1], ALU.add))
            ch(g.tensor_tensor(self.belowb[:, :, 0:2], self.belowb[:, :, 0:2], self.belowb[:, :, 2:4], ALU.add))
            ch(g.tensor_tensor(self.cnt[:, 4:6], self.belowb[:, :, 0], self.belowb[:, :, 1], ALU.add))
            ch(g.partition_all_reduce(self.tot[:, :], self.cnt[:, :], P, RADD))
            ch(g.tensor_tensor(self.tot[:, :], self.tot[:, :], self.rank[:, :], ALU.subtract))
            ch(g.tensor_scalar(self.keep[:, :], self.tot[:, :], 0.0, self.bitf[:, 0:1], ALU.is_le, ALU.mult))
            ch(g.tensor_tensor(self.found[:, :], self.found[:, :], self.keep[:, :], ALU.add))
            ch(g.tensor_scalar(self.bitf[:, :], self.bitf[:, :], 0.5, None, ALU.mult))
            g.sem_clear(self.steps)
        ch = Chain(g, self.steps)
        th = self.found[:, :].bitcast(F32)
        for i, (a, src, out) in enumerate(((self.a[:, 0, :], k.w1[:, 0, :], k.w1[:, 1, :]),
                                           (self.a[:, 1, :], w2, k.w1b[:, 1, :, :].rearrange("p m d -> p (m d)")),
                                           (self.ab[:, :], k.b1[:, 0, :], k.b1[:, 1, :]),
                                           (self.ac[:, :], k.b1col[:, 0:1], k.b1col[:, 1:2]))):
            w = a.shape[-1]
            low = self.below[:, 0, 0, 0:w]
            top = self.below[:, 0, 1, 0:w]
            one = self.below[:, 1, 0, 0:w]
            ch(g.tensor_scalar(low, a, th[:, 2 * i:2 * i + 1], None, ALU.is_le))
            ch(g.tensor_scalar(top, a, th[:, 2 * i + 1:2 * i + 2], None, ALU.is_ge))
            ch(g.tensor_scalar(one, low, 1.0, None, ALU.add))
            ch(g.tensor_tensor(top, top, one, ALU.mult))
            ch(g.tensor_tensor(low, low, top, ALU.subtract))
            ch(g.tensor_scalar(one, src, 0.8, None, ALU.mult))
            ch(g.tensor_tensor(one, one, low, ALU.mult))
            ch(g.tensor_tensor(out, src, one, ALU.add))
        g.dma_start(k.d["b2_scratch"].rearrange("(v p) -> p v", v=2), k.b1col[:, :],
                    allow_slow_non_contiguous=True).then_inc(self.b2_out, 16)
        g.wait_ge(self.b2_out, 16)
        g.dma_start(self.row1[:, :, :], k.d["b2_scratch"].rearrange("(a v p) -> a v p", a=1, v=2)
                    .broadcast_to([3, 2, P])).then_inc(self.ready, 16)

    def split_b2(self, v):
        ch = Chain(v, self.rows_split)
        v.wait_ge(self.ready, 16)
        split_rows(ch, v, self.row1[:, :, :], self.rowr[:, :, :], self.rowb[:, :, :], self.k.seed1[:, :, :], self.k)



class PerturbedRows(Stage):

    def __init__(self, perturb):
        self.perturb = perturb

    def gpsimd(self, g):
        self.perturb.gpsimd(g)
        g.wait_ge(self.perturb.ready, 16)

    def vector(self, v):
        self.perturb.split_b2(v)


class Rwkv(Stage):

    STEPS = 15
    def __init__(self, k, ht, ln):
        self.k, self.ht, self.ln = k, ht, ln
        s = lambda n: k.sem("rwkv_" + n)
        self.mixed = s("mixed")
        self.projected = s("projected")
        self.taken = s("taken")
        self.rk_ready = s("rk_ready")
        self.bonus = s("bonus")
        self.vrep = [s(f"vrep{b}") for b in range(2)]
        self.vrep_used = [s(f"vrep_used{b}") for b in range(2)]
        self.kv = [s(f"kv{b}") for b in range(2)]
        self.kv_used = [s(f"kv_used{b}") for b in range(2)]
        self.rs = [s(f"rs{b}") for b in range(2)]
        self.rs_used = [s(f"rs_used{b}") for b in range(2)]
        self.o_sb = s("o_sb")
        self.mean = s("mean")
        self.centred = s("centred")
        self.squared = s("squared")
        self.var = s("var")
        self.dev = s("dev")
        self.gated = s("gated")
        self.y = s("y")
        self.ready = s("ready")
        self.steps = s("steps")
        self.zeroed = s("zeroed")

    def alloc(self, ctx):
        sb = lambda n, sh: self.k.sb("rw_" + n, sh, ctx=ctx)
        self.diff = sb("diff", [P, CH])
        self.mix = sb("mix", [P, 4, CH])
        self.r, self.kk, self.v, self.w, self.ek = (sb(n, [P, CH]) for n in ("r", "k", "v", "w", "ek"))
        self.rk = sb("rk", [P, CH])
        self.vj = sb("vj", [P, 2, CH])
        self.kvj = sb("kvj", [P, 2, CH])
        self.state = sb("state", [P, 8, 1 + CH])
        self.rsj = sb("rsj", [P, 2, CH])
        self.o = sb("o", [P, CH])
        self.oc = sb("oc", [P, CH])
        self.sq = sb("sq", [P, CH])
        self.sd = sb("sd", [P, CH])
        self.z = sb("z", [P, CH])

    def vector(self, v):
        k = self.k
        v.wait_ge(k.setup.ready, 1)
        v.memset(self.state[:, :, CH:CH + 1], 0.0).then_inc(self.zeroed, 1)
        v.wait_ge(self.zeroed, 1)
        def turn(c):
            ch = Chain(v, self.steps, c * self.STEPS)
            v.wait_ge(self.ln.ready, self.ln.chunk_ready(c))
            v.wait_ge(self.projected, c * 4)
            ch(v.tensor_copy(self.state[:, :, 0:1], self.state[:, :, CH:CH + 1]))
            now = self.ht[:, bass.ds(1 + c * CH, CH)]
            before = self.ht[:, bass.ds(c * CH, CH)]
            ch(v.tensor_tensor(self.diff[:, :], now, before, ALU.subtract))
            for i in range(4):
                v.scalar_tensor_tensor(self.mix[:, i, :], self.diff[:, :], k.vec[:, i:i + 1], before,
                                       ALU.mult, ALU.add).then_inc(self.mixed, 1)
            v.wait_ge(self.taken, c * 5 + 5)
            v.tensor_tensor(self.rk[:, :], self.r[:, :], self.ek[:, :], ALU.mult).then_inc(self.rk_ready, 1)
            ch(v.tensor_scalar(self.w[:, :], self.w[:, :], float(np.exp(-1e-4)), None, ALU.mult))
            for j in range(8):
                b = j % 2
                v.wait_ge(self.kv[b], c * 4 + j // 2 + 1)
                ch(v.tensor_tensor_scan(self.state[:, j, 1:1 + CH], self.w[:, :], self.kvj[:, b, :],
                                        self.state[:, j, 0:1], ALU.mult, ALU.add))
                v.wait_ge(self.rs_used[b], c * 4 + j // 2)
                v.tensor_tensor(self.rsj[:, b, :], self.r[:, :], self.state[:, j, 0:CH], ALU.mult) \
                    .then_inc(self.rs[b], 1)
            v.wait_ge(self.bonus, c + 1)
            ch(v.tensor_tensor(self.o[:, :], k.bank(0), self.v[:, :], ALU.mult))
            v.wait_ge(self.rs_used[1], c * 4 + 4)
            v.tensor_tensor(self.o[:, :], self.o[:, :], k.bank(6), ALU.add).then_inc(self.o_sb, 1)
            v.wait_ge(self.mean, c + 1)
            v.tensor_tensor(self.oc[:, :], self.o[:, :], k.bank(1), ALU.subtract).then_inc(self.centred, 1)
            v.wait_ge(self.dev, c + 1)
            ch(v.reciprocal(self.sd[:, :], self.sd[:, :]))
            ch(v.tensor_tensor(self.oc[:, :], self.oc[:, :], self.sd[:, :], ALU.mult))
            ch(v.tensor_scalar(self.oc[:, :], self.oc[:, :], k.vec[:, 5:6], k.vec[:, 6:7], ALU.mult, ALU.add))
            v.tensor_tensor(self.z[:, :], self.oc[:, :], self.r[:, :], ALU.mult).then_inc(self.gated, 1)
            v.wait_ge(self.y, c + 1)
            xc = k.X[:, bass.ds(c * TPC, TPC), :]
            v.tensor_tensor(xc, xc, k.bank(3).rearrange("p (n d) -> p n d", n=TPC), ALU.add) \
                .then_inc(self.ready, 1)
            assert ch.n == self.STEPS, ch.n

        each(v, NC, turn)

    def scalar(self, s):
        k = self.k
        s.wait_ge(k.setup.ready, 1)
        def turn(c):
            s.wait_ge(self.gated, c)
            for i, (out, f, kw) in enumerate(((self.r, ACT.Sigmoid, {}), (self.kk, ACT.Copy, {}),
                                              (self.v, ACT.Copy, {}), (self.w, ACT.Sigmoid, {}))):
                s.wait_ge(self.projected, c * 4 + i + 1)
                s.activation(out[:, :], k.bank(i), f, **kw).then_inc(self.taken, 1)
            s.activation(self.ek[:, :], k.bank(1), ACT.Exp, bias=k.vec[:, 4:5]).then_inc(self.taken, 1)
            for j in range(8):
                b = j % 2
                s.wait_ge(self.vrep[b], c * 4 + j // 2 + 1)
                s.wait_ge(self.kv[b], c * 4 + j // 2)
                s.activation(self.vj[:, b, :], k.bank(4 + b), ACT.Copy).then_inc(self.vrep_used[b], 1)
            s.wait_ge(self.centred, c + 1)
            s.activation(self.sq[:, :], self.oc[:, :], ACT.Square).then_inc(self.squared, 1)
            s.wait_ge(self.var, c + 1)
            s.activation(self.sd[:, :], k.bank(2), ACT.Sqrt, bias=k.eps[:, :]).then_inc(self.dev, 1)

        each(s, NC, turn)

    def gpsimd(self, g):
        def turn(c):
            for j in range(8):
                b = j % 2
                g.wait_ge(self.taken, c * 5 + 2)
                g.wait_ge(self.vrep_used[b], c * 4 + j // 2 + 1)
                g.wait_ge(self.steps, c * self.STEPS + (3 + j - 1 if j >= 2 else 0))
                g.tensor_tensor(self.kvj[:, b, :], self.kk[:, :], self.vj[:, b, :], ALU.mult).then_inc(self.kv[b], 1)

        each(g, NC, turn)

    def tensor(self, pe):
        k = self.k
        pe.wait_ge(self.ln.ready, self.ln.all_ready)
        def turn(c):
            pe.wait_ge(self.ready, c)
            for i in range(4):
                pe.wait_ge(self.mixed, c * 4 + i + 1)
                pe.matmul(k.bank(i), k.wT[:, i, :], self.mix[:, i, :], start=True, stop=True) \
                    .then_inc(self.projected, 1)

            def values(j):
                b = j % 2
                pe.wait_ge(self.vrep_used[b], c * 4 + j // 2)
                pe.matmul(k.bank(4 + b), k.wvrep[:, j, :], self.mix[:, 2, :], start=True, stop=True) \
                    .then_inc(self.vrep[b], 1)

            values(0)
            values(1)
            pe.wait_ge(self.rk_ready, c + 1)
            pe.wait_ge(self.taken, c * 5 + 5)
            pe.matmul(k.bank(0), k.group_sum, self.rk[:, :], start=True, stop=True).then_inc(self.bonus, 1)
            for j in range(8):
                b = j % 2
                if j + 2 < 8:
                    values(j + 2)
                pe.wait_ge(self.rs[b], c * 4 + j // 2 + 1)
                pe.matmul(k.bank(6), k.cst[:, (5 + j) * P:(6 + j) * P], self.rsj[:, b, :],
                          start=(j == 0), stop=(j == 7)).then_inc(self.rs_used[b], 1)
            pe.wait_ge(self.o_sb, c + 1)
            pe.matmul(k.bank(1), k.group_mean, self.o[:, :], start=True, stop=True).then_inc(self.mean, 1)
            pe.wait_ge(self.squared, c + 1)
            pe.matmul(k.bank(2), k.group_mean, self.sq[:, :], start=True, stop=True).then_inc(self.var, 1)
            pe.wait_ge(self.gated, c + 1)
            for n in range(TPC):
                ins = pe.matmul(k.PS[:, 3, n * P:(n + 1) * P], self.z[:, n * P:(n + 1) * P], k.wT[:, 4, :],
                                start=True, stop=True)
            ins.then_inc(self.y, 1)

        each(pe, NC, turn)


class Experts(Stage):

    def __init__(self, k, name, ht, ln, router, w1, w2, b1, seed, func, experts, tiles,
                 needs=()):
        self.k, self.name, self.ht, self.ln, self.router = k, name, ht, ln, router
        self.w1, self.w2, self.b1, self.seed, self.func = w1, w2, b1, seed, func
        self.E, self.M, self.needs = experts, tiles, needs
        m = k.experts_mem
        self.hid, self.hid_used, self.out, self.out_used, self.ready = m.hid, m.hid_used, m.out, m.out_used, m.ready
        self.hid0, self.out0, self.ready0 = m.hid_count, m.out_count, m.ready_count
        m.hid_count += NC * experts * tiles // 4
        m.out_count += NC * experts // 2
        m.ready_count += NC

    def alloc(self, ctx):
        self.g = self.k.sb(self.name + "_hidden", [P, 2, self.M, CH], ctx=ctx)

    def tensor(self, pe):
        k, E, M = self.k, self.E, self.M
        uses = E * M // 4
        for sem, val in [*self.router.banks_free(), *self.needs]:
            pe.wait_ge(sem, val)
        def turn(c):
            x = self.ht[:, bass.ds(1 + c * CH, CH)]

            def hidden(e):
                for m in range(M):
                    b, n = (e * M + m) % 4, (e * M + m) // 4
                    pe.wait_ge(self.hid_used[b], self.hid0 + c * uses + n)
                    pe.matmul(k.bank(b), self.w1(e, m), x, start=True, stop=True).then_inc(self.hid[b], 1)

            def output(e):
                b = e % 2
                pe.wait_ge(self.out_used[b], self.out0 + c * (E // 2) + e // 2)
                pe.matmul(k.bank(4 + b), k.onesb[0:3, :],
                          self.seed[:, e:e + 1, :].broadcast_to([3, TPC, P]), start=True, stop=False,
                          skip_group_check=True)
                for m in range(M):
                    q, n = (e * M + m) % 4, (e * M + m) // 4
                    pe.wait_ge(self.hid_used[q], self.hid0 + c * uses + n + 1)
                    for i in range(TPC):
                        ins = pe.matmul(k.PS[:, 4 + b, i * P:(i + 1) * P], self.g[:, b, m, i * P:(i + 1) * P],
                                        self.w2(e, m), start=False, stop=(m == M - 1),
                                        skip_group_check=True)
                ins.then_inc(self.out[b], 1)

            for e in range(E):
                hidden(e)
                if e:
                    output(e - 1)
            output(E - 1)

        each(pe, NC, turn)

    def scalar(self, s):
        k, E, M = self.k, self.E, self.M
        uses = E * M // 4
        for sem, val in self.needs:
            s.wait_ge(sem, val)
        def turn(c):
            for e in range(E):
                s.wait_ge(self.out[e % 2], self.out0 + c * (E // 2) + e // 2)
                for m in range(M):
                    b, n = (e * M + m) % 4, (e * M + m) // 4
                    s.wait_ge(self.hid[b], self.hid0 + c * uses + n + 1)
                    s.activation(self.g[:, e % 2, m, :], k.bank(b), self.func, bias=self.b1(e, m)) \
                        .then_inc(self.hid_used[b], 1)

        each(s, NC, turn)

    def vector(self, v):
        k, E = self.k, self.E
        def turn(c):
            for e in range(E):
                b = e % 2
                v.wait_ge(self.out[b], self.out0 + c * (E // 2) + e // 2 + 1)
                if e:
                    v.wait_ge(self.out_used[1 - b], self.out0 + c * (E // 2) + (e - 1) // 2 + 1)
                for i in range(TPC):
                    xi = k.X[:, bass.ds(c * TPC + i, 1), :]
                    gate = k.gates[:, bass.ds(c * TPC + i, 1), e:e + 1].rearrange("p a b -> p (a b)")
                    ins = v.scalar_tensor_tensor(xi, k.PS[:, 4 + b:5 + b, i * P:(i + 1) * P], gate, xi,
                                                 ALU.mult, ALU.add)
                ins.then_inc(self.out_used[b], 1)
            v.wait_ge(self.out_used[1], self.out0 + c * (E // 2) + E // 2)
            v.sem_inc(self.ready, 1)

        each(v, NC, turn)

    def x_ready(self, c):
        return [(self.ready, self.ready0 + c + 1)]


class Router(Stage):

    def __init__(self, k, name, ht, ln, w, bias, top2):
        self.k, self.ht, self.ln, self.w, self.bias, self.top2 = k, ht, ln, w, bias, top2
        m = k.router_mem
        self.logits, self.shifted, self.exps, self.steps, self.read = m.logits, m.shifted, m.exps, m.steps, m.read
        self.nth, self.step0 = m.uses + 1, m.step_count
        m.uses += 1
        m.step_count += 22 if top2 else 6

    def tensor(self, pe):
        k = self.k
        pe.wait_ge(self.ln.ready, self.ln.all_ready)
        for n in range(NT):
            ins = pe.matmul(k.PS[:, 7, n * 8:(n + 1) * 8], self.ht[:, 1 + n * P:1 + (n + 1) * P], self.w,
                            start=True, stop=True)
        ins.then_inc(self.logits, 1)

    def scalar(self, s):
        m = self.k.router_mem
        s.wait_ge(self.shifted, self.nth)
        s.activation(m.p[:, :, :], m.p[:, :, :], ACT.Exp, scale=0.2 if self.top2 else 1.0).then_inc(self.exps, 1)

    def banks_free(self):
        return [(self.read, self.nth)]

    def vector(self, v):
        k, m, ch = self.k, self.k.router_mem, Chain(v, self.steps, self.step0)
        full = [P, NT, 8]
        col = lambda a: a.broadcast_to(full)
        v.wait_ge(self.logits, self.nth)
        v.tensor_tensor(m.p[:, :, :], k.PS[:, 7, 0:NT * 8].rearrange("p (n e) -> p n e", n=NT),
                        self.bias[:, :].rearrange("p (a e) -> p a e", a=1).broadcast_to(full), ALU.add) \
            .then_inc(self.read, 1)
        v.wait_ge(self.read, self.nth)
        ch(v.tensor_reduce(m.a[:, :, :], m.p[:, :, :], AX.X, ALU.max))
        v.tensor_tensor(m.p[:, :, :], m.p[:, :, :], col(m.a[:, :, :]), ALU.subtract).then_inc(self.shifted, 1)
        v.wait_ge(self.exps, self.nth)
        ch(v.tensor_reduce(m.a[:, :, :], m.p[:, :, :], AX.X, ALU.add))
        ch(v.reciprocal(m.a[:, :, :], m.a[:, :, :]))
        ch(v.tensor_tensor(m.p[:, :, :], m.p[:, :, :], col(m.a[:, :, :]), ALU.mult))
        if not self.top2:
            ch(v.tensor_copy(k.gates[:, :, 0:1], m.p[:, :, 0:1]))
            ch(v.tensor_reduce(k.gates[:, :, 1:2], m.p[:, :, 1:8], AX.X, ALU.add))
            assert ch.n == 6
            return
        order = k.cst[:, CST_ORDER:CST_ORDER + 8].rearrange("p (a e) -> p a e", a=1).broadcast_to(full)
        ch(v.tensor_copy(m.left[:, :, :], m.p[:, :, :]))
        for r in range(2):
            sel = m.sel[:, r, :, :]
            ch(v.tensor_reduce(m.a[:, :, :], m.left[:, :, :], AX.X, ALU.max))
            ch(v.tensor_tensor(sel, m.left[:, :, :], col(m.a[:, :, :]), ALU.is_equal))
            ch(v.tensor_tensor(sel, sel, order, ALU.mult))
            ch(v.tensor_reduce(m.a[:, :, :], sel, AX.X, ALU.max))
            ch(v.tensor_tensor(sel, sel, col(m.a[:, :, :]), ALU.is_equal))
            if r == 0:
                ch(v.scalar_tensor_tensor(m.left[:, :, :], sel, -2.0, m.left[:, :, :], ALU.mult, ALU.add))
        ch(v.tensor_tensor(m.sel[:, 0, :, :], m.sel[:, 0, :, :], m.sel[:, 1, :, :], ALU.add))
        ch(v.tensor_tensor(m.p[:, :, :], m.p[:, :, :], m.sel[:, 0, :, :], ALU.mult))
        ch(v.tensor_reduce(m.a[:, :, :], m.p[:, :, :], AX.X, ALU.add))
        ch(v.tensor_scalar(m.a[:, :, :], m.a[:, :, :], 1e-9, None, ALU.add))
        ch(v.reciprocal(m.a[:, :, :], m.a[:, :, :]))
        ch(v.tensor_tensor(k.gates[:, :, :], m.p[:, :, :], col(m.a[:, :, :]), ALU.mult))
        assert ch.n == 22, ch.n


class CausalHeads(Stage):

    R = 3

    AHEAD = 3
    RATE = 4.5

    def __init__(self, k, name, ln, quads, sources, blocks, rows, kheads, value_w, vheads, vdim, scale, wout,
                 scratch, rotate, summed):
        self.k, self.name, self.ln, self.NQ = k, name, ln, quads
        self.sources, self.blocks, self.rows, self.kheads = sources, blocks, rows, kheads
        self.value_w, self.vheads, self.vdim, self.scale = value_w, vheads, vdim, scale
        self.wout, self.scratch, self.rotate, self.summed = wout, scratch, rotate, summed
        self.NP = 1 + max(b[0] for b in blocks[0])
        s = lambda n: k.sem(name + "_" + n)
        self.filled = s("filled")
        self.ones = s("ones")
        self.table = s("table")
        self.projected = s("projected")
        self.split = s("split")
        self.stored = [s(f"stored{i}") for i in range(len(sources))]
        self.steps = s("steps")
        self.vproj = s("vproj")
        self.values = s("values")
        self.first = [s(f"first{c}") for c in range(NC)]
        self.stacked = [s(f"stacked{b}") for b in range(2)]
        self.added = [s("added_g"), s("added_v")]
        self.ring_full = [s(f"ring_full{b}") for b in range(self.R)]
        self.ring_free = [s(f"ring_free{b}") for b in range(self.R)]
        self.maxima = s("maxima")
        self.max_rows = [s(f"max_rows{b}") for b in range(2)]
        self.scores = [s(f"scores{p}") for p in range(2)]
        self.exps = [s(f"exps{p}") for p in range(2)]
        self.weighted = s("weighted")
        self.moved = s("moved")
        self.normed = s("normed")
        self.ready = s("ready")
        self.units = [(c, kj) for c in range(NC) for kj in range((c + 1) * TPC)]
        self.plan = self.make_plan()

    def alloc(self, ctx):
        sb = lambda n, sh, dt=F32: self.k.sb(self.name + "_" + n, sh, dt, ctx)
        self.Q = sb("Q", [P, 2, 4, self.NP, T], BF16)
        self.K = sb("K", [P, 2, self.kheads, self.NP, T], BF16)
        self.vcols = self.vdim + (0 if self.summed else 1)
        self.V = sb("V", [P, NT, self.vheads, self.vcols])
        self.acc = sb("acc", [P, 4, CH]) if self.summed else None
        self.mp = sb("mp", [P, 2, NC, 4, TPC])
        self.neg = sb("neg", [P, 2, 4, TPC])
        self.negp = sb("negp", [P, 2, 4, 3, TPC], BF16)
        self.negT = sb("negT", [3 * 4 * TPC, 2, P], BF16)
        self.O = sb("O", [P, 2, CH])
        self.On = sb("On", [P, 2, CH])
        self.rec = sb("rec", [P, CH])
        with ExitStack() as c:
            self.PT = self.k.sb(self.name + "_PT", [P, 2, 4, CH], F32, c)
        with ExitStack() as c:
            self.parts = self.k.sb(self.name + "_parts", [P, 2, 3, CH], BF16, c)
            self.x = self.k.sb(self.name + "_x", [P, CH], F32, c)
            self.y = self.k.sb(self.name + "_y", [P, CH], F32, c)
            if self.rotate:
                self.tab = self.k.sb(self.name + "_tab", [P, 2, T], F32, c)

    def chunk_maxima(self, g, c):
        items = []
        for i in range(TPC):
            for kc in range(c + 1):
                share = 1 if kc < c else TPC // (i + 1)
                items += [("max", g, c, i, kc, tuple(range(j, j + share))) for j in range(0, 4, share)]
        return items

    def make_plan(self):
        n = len(self.units)
        total = self.NQ * n
        items, due = [], []
        for g in range(self.NQ):
            for c in range(NC):
                items += self.chunk_maxima(g, c)
                due.append((g * n + self.units.index((c, 0)), len(items)))

        def wanted(u):
            late = max(min(d, np.ceil(d - self.RATE * max(0, first - self.AHEAD - u))) for first, d in due)
            steady = (due[-1][1] - start) * u / (due[-1][0] - self.AHEAD)
            return int(min(len(items), max(late, start + steady)))

        start = 0
        start = wanted(0)
        steps = [[] for _ in range(total + 5)]
        turn_at = dict((d, (i // NC, i % NC)) for i, (u, d) in enumerate(due))
        up_front, pending = [], []
        done = 0
        for u in range(-1, total):
            mine = steps[u] if u >= 0 else up_front
            for i in range(max(2, wanted(u + 1) - done)):
                if pending and (i > pending[0][0] or done == len(items)):
                    mine.append(("turn",) + pending.pop(0)[1])
                if done < wanted(u + 1):
                    mine.append(items[done])
                    done += 1
                    if done in turn_at:
                        pending.append((i + 2, turn_at[done]))
            pending = [(0, at) for _, at in pending]
        for g in range(self.NQ):
            for c in range(NC):
                end = g * n + self.units.index((c, (c + 1) * TPC - 1))
                steps[end + 2].append(("sum", g, c))
                steps[end + 3].append(("out", g, c))
        plan = [(None, it) for it in up_front]
        for u, mine in enumerate(steps):
            a, b = (len(mine) + 3) // 4, (len(mine) + 1) // 2
            ring = lambda part: [(None, it) for it in part]
            if u < total:
                plan.append((u, "scores0"))
            plan += ring(mine[:a])
            if u < total:
                plan.append((u, "scores1"))
            plan += ring(mine[a:b])
            if 1 <= u <= total:
                plan.append((u - 1, "weighted"))
            plan += ring(mine[b:])
        return plan

    def ring_bank(self, ring):
        return ring % self.R, ring // self.R

    def unit(self, u):
        g, i = divmod(u, len(self.units))
        c, kj = self.units[i]
        q0 = max(0, kj - c * TPC) * P
        return g, c, kj, q0

    def chunk(self, g, c):
        return g * NC + c

    def tensor(self, pe):
        k, ns = self.k, len(self.sources)
        pe.wait_ge(self.ln.ready, self.ln.all_ready)
        def turn(c):
            for i, (w, partner, m) in enumerate(self.sources):
                if i >= 2:
                    pe.wait_ge(self.split, c * ns + i - 1)
                else:
                    pe.wait_ge(self.split, c * ns)
                h = self.k.HT[:, bass.ds(1 + c * CH, CH)]
                b = 2 * (i % 2)
                ins = pe.matmul(k.PS[0:m, b, :], w, h, start=True, stop=True)
                if partner is not None:
                    ins = pe.matmul(k.PS[0:m, b + 1, :], partner, h, start=True, stop=True)
                ins.then_inc(self.projected, 1)

        each(pe, NC, turn)
        pe.wait_ge(self.filled, 1)
        for c in range(NC):
            pe.wait_ge(self.values, max(0, c - 1))
            for i in range(TPC):
                n = c * TPC + i
                ins = pe.matmul(k.PS[:, 4 + c % 2, i * P:i * P + self.value_w.shape[-1]],
                                k.HT[:, 1 + n * P:1 + (n + 1) * P], self.value_w, start=True, stop=True)
            ins.then_inc(self.vproj, 1)
        pe.wait_ge(self.values, NC)
        ring = 0
        for u, item in self.plan:
            if item == "scores0":
                self.pe_scores(pe, u, 0)
            elif item == "scores1":
                self.pe_scores(pe, u, 1)
            elif item == "weighted":
                self.pe_weighted(pe, u)
            else:
                b, uses = self.ring_bank(ring)
                pe.wait_ge(self.ring_free[b], uses)
                self.pe_item(pe, item, 5 + b).then_inc(self.ring_full[b], 1)
                ring += 1

    def pe_item(self, pe, item, bank):
        k, kind = self.k, item[0]
        if kind == "max":
            _, g, c, i, kc, heads = item
            if g == 0:
                pe.wait_ge(self.first[c], 16 * self.stack_dmas)
            else:
                pe.wait_ge(self.stacked[g % 2], 16 * self.stack_dmas * ((g + 1) // 2))
            w = CH if kc < c else (i + 1) * P
            q0 = c * CH + i * P
            for x, j in enumerate(heads):
                at = x * w
                ins = pe.matmul(k.PS[:, bank, at:at + w], self.Q[0:self.rows, g % 2, j, 0, q0:q0 + P],
                                self.K[0:self.rows, g % 2, j % self.kheads, 0, kc * CH:kc * CH + w],
                                start=True, stop=kc < c)
                if kc == c:
                    ins = pe.matmul(k.PS[:, bank, at + w - P:at + w], k.identb[:, :], k.mask_qk[:, :],
                                    start=False, stop=True)
            return ins
        if kind == "turn":
            _, g, c = item
            n = self.chunk(g, c)
            pe.wait_ge(self.maxima, n + 1)
            return pe.transpose(k.PS[:, bank, :].bitcast(BF16)[0:3 * 4 * TPC, 0:P],
                                self.negp[:, n % 2, :, :, :].rearrange("p j r i -> p (j r i)"), k.identb[:, :])
        if kind == "sum":
            _, g, c = item
            n = self.chunk(g, c)
            if self.summed:
                pe.wait_ge(self.added[0], self.first_unit(n + 1))
                pe.wait_ge(self.added[1], self.first_unit(n + 1))
                for j in range(4):
                    ins = pe.matmul(k.PS[32 * j:32 * j + 32, bank, :], k.ones_col, self.acc[:, j, :],
                                    start=True, stop=True)
                return ins
            pe.wait_ge(self.moved, n + 1)
            return pe.matmul(k.bank(bank), k.den_rope, self.O[:, n % 2, :], start=True, stop=True)
        _, g, c = item
        n = self.chunk(g, c)
        pe.wait_ge(self.normed, n + 1)
        for i in range(TPC):
            ins = pe.matmul(k.PS[:, bank, i * P:(i + 1) * P], self.On[:, n % 2, i * P:(i + 1) * P],
                            self.wout[:, g, :], start=True, stop=True)
        return ins

    def first_unit(self, n):
        g, c = divmod(n, NC)
        return g * len(self.units) + self.units.index((c, 0))

    def pe_scores(self, pe, u, p):
        k = self.k
        g, c, kj, q0 = self.unit(u)
        n = self.chunk(g, c)
        if p == 0 and kj == 0:
            pe.wait_ge(self.max_rows[n % 2], 16 * 4 * (n // 2 + 1))
        if u == 0:
            pe.wait_ge(self.split, NC * len(self.sources))
        pe.wait_ge(self.exps[p], u)
        for j in (2 * p, 2 * p + 1):
            diag = kj >= c * TPC
            for m in range(self.NP):
                r = self.rows + (3 if m == 0 else 0)
                ins = pe.matmul(k.PS[:, j, q0:CH], self.K[0:r, g % 2, j % self.kheads, m, kj * P:(kj + 1) * P],
                                self.Q[0:r, g % 2, j, m, c * CH + q0:(c + 1) * CH],
                                start=(m == 0), stop=(m == self.NP - 1 and not diag))
            if diag:
                ins = pe.matmul(k.PS[:, j, q0:q0 + P], k.identb[:, :], k.mask_kq[:, :], start=False, stop=True)
        ins.then_inc(self.scores[p], 1)

    def pe_weighted(self, pe, u):
        k = self.k
        g, c, kj, q0 = self.unit(u)
        n = self.chunk(g, c)
        last = (c + 1) * TPC - 1
        if kj == 0:
            if n > 0:
                pe.wait_ge(self.moved, n)
        for p in range(2):
            pe.wait_ge(self.exps[p], u + 1)
        for j in range(4):
            v = self.V[:, kj, (4 * g + j) if self.vheads > 4 else g, :]
            ins = pe.matmul(k.PS[32 * j:32 * j + self.vcols, 4, q0:CH], v, self.PT[:, u % 2, j, q0:CH],
                            start=(kj == 0), stop=(kj == last))
        ins.then_inc(self.weighted, 1)

    def scalar(self, s):
        k, v = self.k, self.vdim
        s.activation(self.K[:, :, :, 0, :], k.onesb[:, None, None, 0:1].broadcast_to([P, 2, self.kheads, T]),
                     ACT.Copy).then_inc(self.ones, 1)
        s.wait_ge(self.filled, 1)
        for c in range(NC):
            s.wait_ge(self.vproj, c + 1)
            s.activation(self.V[:, c * TPC:(c + 1) * TPC, :, 0:v],
                         k.PS[:, 4 + c % 2, :].rearrange("p (n d) -> p n d", n=TPC)[:, :, 0:self.vheads * v]
                         .rearrange("p n (h d) -> p n h d", h=self.vheads), ACT.Copy).then_inc(self.values, 1)
        total = self.NQ * len(self.units)
        for sem in self.stored:
            s.wait_ge(sem, 16 * self.split_dmas * NC)
        for u in range(total + 1):
            if u < total:
                _, _, _, q0 = self.unit(u)
                if u >= 2:
                    s.wait_ge(self.weighted, u - 1)
                    if self.summed:
                        s.wait_ge(self.added[0], u - 1)
                        s.wait_ge(self.added[1], u - 1)
                for p in range(2):
                    s.wait_ge(self.scores[p], u + 1)
                    s.activation(self.PT[:, u % 2, 2 * p:2 * p + 2, q0:CH], k.PS[:, 2 * p:2 * p + 2, q0:CH],
                                 ACT.Exp, scale=self.scale).then_inc(self.exps[p], 1)
            if u:
                g, c, kj, _ = self.unit(u - 1)
                if kj == (c + 1) * TPC - 1:
                    n = self.chunk(g, c)
                    s.wait_ge(self.weighted, u)
                    if n >= 2:
                        s.wait_ge(self.normed, n - 1)
                    s.activation(self.O[:, n % 2, :], k.bank(4), ACT.Copy).then_inc(self.moved, 1)

    def gpsimd(self, g):
        if not self.summed:
            return
        for u in range(self.NQ * len(self.units)):
            self.add_weights(g, u, 0, slice(0, 3))

    def add_weights(self, eng, u, who, heads):
        quad, c, kj, q0 = self.unit(u)
        n = self.chunk(quad, c)
        if kj == 0 and n:
            b, uses = self.ring_bank(self.ring_items().index(("sum", (n - 1) // NC, (n - 1) % NC)))
            eng.wait_ge(self.ring_full[b], uses + 1)
        if u:
            eng.wait_ge(self.added[who], u)
        for p in range(who, 2):
            eng.wait_ge(self.exps[p], u + 1)
        new, acc = self.PT[:, u % 2, heads, q0:CH], self.acc[:, heads, q0:CH]
        if kj == 0:
            eng.tensor_copy(acc, new).then_inc(self.added[who], 1)
        else:
            eng.tensor_tensor(acc, acc, new, ALU.add).then_inc(self.added[who], 1)

    def vector(self, v):
        k, ch, ns = self.k, Chain(v, self.steps), len(self.sources)
        if self.rotate:
            v.memset(self.Q[64:self.rows, :, :, 0, :].bitcast(F32), 0.0)
        if not self.summed:
            v.memset(self.V[:, :, :, self.vdim:self.vdim + 1], 1.0)
        v.wait_ge(self.ln.ready, self.ln.all_ready)
        v.memset(k.PS[:, 4, :], 0.0).then_inc(self.filled, 1)
        per = sum((3 if partner is not None else 1) + 3 for _, partner, _ in self.sources)
        def turn(c):
            ch = Chain(v, self.steps, c * per)
            for i, (w, partner, m) in enumerate(self.sources):
                b = 2 * (i % 2)
                x, y, part = self.x[0:m, :], self.y[0:m, :], self.parts[0:m, i % 2, :, :]
                v.wait_ge(self.projected, c * ns + i + 1)
                if partner is not None:
                    ch.mark(v.tensor_tensor(x, k.PS[0:m, b, :], self.tab[0:m, 0, bass.ds(c * CH, CH)], ALU.mult))
                    ch(v.tensor_tensor(y, k.PS[0:m, b + 1, :], self.tab[0:m, 1, bass.ds(c * CH, CH)], ALU.mult))
                    ch(v.tensor_tensor(x, x, y, ALU.add))
                else:
                    ch(v.tensor_copy(x, k.PS[0:m, b, :]))
                if i >= 2:
                    v.wait_ge(self.stored[i - 2], 16 * self.split_dmas * (c + 1))
                else:
                    v.wait_ge(self.stored[ns - 1 - (ns - 1 - i) % 2], 16 * self.split_dmas * c)
                ch(v.tensor_copy(part[:, 0, :], x))
                ch(v.tensor_tensor(x, x, part[:, 0, :], ALU.subtract))
                ch(v.tensor_copy(part[:, 1, :], x))
                v.tensor_tensor(part[:, 2, :], x, part[:, 1, :], ALU.subtract).then_inc(self.split, 1)
                v.wait_ge(self.split, c * ns + i + 1)
            assert ch.n == per, ch.n

        if self.rotate:
            v.wait_ge(self.table, 16)
        each(v, NC, turn)
        ch = Chain(v, self.steps, NC * per)
        ring = 0
        for u, item in self.plan:
            if u is not None:
                if item == "weighted" and self.summed:
                    self.add_weights(v, u, 1, slice(3, 4))
                continue
            b, uses = self.ring_bank(ring)
            v.wait_ge(self.ring_full[b], uses + 1)
            self.dve_item(v, ch, item, 5 + b, ring)
            ring += 1

    def turned_at(self, g, c):
        return self.ring_items().index(("turn", g, c))

    def ring_items(self):
        return [it for u, it in self.plan if u is None]

    def dve_item(self, v, ch, item, bank, ring):
        k, kind = self.k, item[0]
        b, uses = self.ring_bank(ring)
        free = self.ring_free[b]
        if kind == "max":
            _, g, c, i, kc, heads = item
            n = self.chunk(g, c)
            w = CH if kc < c else (i + 1) * P
            v.tensor_reduce(self.mp[:, n % 2, kc, heads[0]:heads[-1] + 1, i],
                            k.PS[:, bank, 0:len(heads) * w].rearrange("p (h k) -> p h k", h=len(heads)), AX.X, ALU.max) \
                .then_inc(free, 1)
            if (i, kc, heads[-1]) == (TPC - 1, c, 3):
                neg, part = self.neg[:, n % 2, :, :], self.negp[:, n % 2, :, :, :]
                for back in range(self.R):
                    if ring >= back:
                        b, uses = self.ring_bank(ring - back)
                        v.wait_ge(self.ring_free[b], uses + 1)
                ch(v.tensor_reduce(neg, self.mp[:, n % 2, 0:c + 1, :, :].rearrange("p k j i -> p j i k"), AX.X, ALU.max,
                                   negate=True))
                if n >= 2:
                    v.wait_ge(self.max_rows[n % 2], 16 * 4 * (n // 2))
                ch(v.tensor_copy(part[:, :, 0, :], neg))
                ch(v.tensor_tensor(neg, neg, part[:, :, 0, :], ALU.subtract))
                ch(v.tensor_copy(part[:, :, 1, :], neg))
                v.tensor_tensor(part[:, :, 2, :], neg, part[:, :, 1, :], ALU.subtract).then_inc(self.maxima, 1)
        elif kind == "turn":
            _, g, c = item
            n = self.chunk(g, c)
            if n >= 2:
                v.wait_ge(self.max_rows[n % 2], 16 * 4 * (n // 2))
            v.tensor_copy(self.negT[:, n % 2, :], k.PS[:, bank, :].bitcast(BF16)[0:3 * 4 * TPC, 0:P]).then_inc(free, 1)
        elif kind == "sum":
            _, g, c = item
            n = self.chunk(g, c)
            if n:
                v.wait_ge(self.normed, n)
            if self.summed:
                v.wait_ge(self.moved, n + 1)
            v.reciprocal(self.rec[:, :], k.bank(bank)).then_inc(free, 1)
            v.wait_ge(free, uses + 1)
            v.tensor_tensor(self.On[:, n % 2, :], self.O[:, n % 2, :], self.rec[:, :], ALU.mult) \
                .then_inc(self.normed, 1)
        else:
            _, g, c = item
            xc = k.X[:, c * TPC:(c + 1) * TPC, :]
            v.tensor_tensor(xc, xc, k.bank(bank).rearrange("p (n d) -> p n d", n=TPC), ALU.add).then_inc(free, 1)
            if g == self.NQ - 1:
                v.wait_ge(free, uses + 1)
                v.sem_inc(self.ready, 1)

    def x_ready(self, c):
        return [(self.ready, c + 1)]

    split_dmas = 3

    def load_stacks(self, sp, g, cols, done):
        d = P // self.shape[0]
        for operand, heads, (src, h), blocks in ((self.Q, 4, self.q_source(g), self.blocks[0]),
                                                 (self.K, self.kheads, self.k_source(g), self.blocks[1])):
            for m, row, first, parts in blocks:
                sp.dma_start(operand[row:row + parts * d, g % 2, 0:heads, m, cols],
                             self.scratch[src, h:h + heads, first * d:(first + parts) * d, cols]
                             .rearrange("h r t -> r h t")).then_inc(done, 16)

    def q_source(self, g):
        return (0, 4 * g) if self.rotate else (g, 0)

    def k_source(self, g):
        return (1, 4 * g) if self.rotate else (2, g)

    @property
    def shape(self):
        return self.scratch.shape[1], self.scratch.shape[2]

    @property
    def stack_dmas(self):
        return len(self.blocks[0]) + len(self.blocks[1])

    def sync(self, sp):
        ns = len(self.sources)
        heads, rows = self.shape
        sp.wait_ge(self.ln.mem.moments, self.ln.use + 1)
        if self.rotate:
            sp.dma_start(self.tab[:, :, :], self.k.d["rotation"]).then_inc(self.table, 16)
        sp.wait_ge(self.ones, 1)
        sp.wait_ge(self.filled, 1)
        for c in range(NC):
            cols = slice(c * CH, (c + 1) * CH)
            for i, (w, partner, m) in enumerate(self.sources):
                sp.wait_ge(self.split, c * ns + i + 1)
                for part in range(3):
                    d = rows // 3
                    sp.dma_start(self.scratch[i, 0:m // d, part * d:(part + 1) * d, cols],
                                 self.parts[0:m, i % 2, part, :]).then_inc(self.stored[i], 16)
            for sem in self.stored:
                sp.wait_ge(sem, 16 * self.split_dmas * (c + 1))
            self.load_stacks(sp, 0, cols, self.first[c])
        self.load_stacks(sp, 1, slice(0, T), self.stacked[1])
        for g in range(self.NQ):
            for c in range(NC):
                if c == NC - 1 and 2 <= g + 1 < self.NQ:
                    sp.wait_ge(self.weighted, g * len(self.units))
                    self.load_stacks(sp, g + 1, slice(0, T), self.stacked[(g + 1) % 2])
                n = self.chunk(g, c)
                b, uses = self.ring_bank(self.turned_at(g, c))
                sp.wait_ge(self.ring_free[b], uses + 1)
                for j in range(4):
                    sp.dma_start(self.Q[self.rows:self.rows + 3, g % 2, j, 0, c * CH:(c + 1) * CH],
                                 self.negT[3 * TPC * j:3 * TPC * (j + 1), n % 2, :]).then_inc(self.max_rows[n % 2], 16)


class FullHead(Stage):

    def __init__(self, k, name, ln):
        self.k, self.name, self.ln = k, name, ln
        s = lambda n: k.sem(name + "_" + n)
        self.projected = s("projected")
        self.q_ready = s("q_ready")
        self.k_ready = s("k_ready")
        self.vproj = s("vproj")
        self.values = s("values")
        self.tile = s("tile")
        self.scores = s("scores")
        self.maxima = s("maxima")
        self.exps = s("exps")
        self.turned = s("turned")
        self.moved = s("moved")
        self.weighted = s("weighted")
        self.added = s("added")
        self.steps = s("steps")
        self.scale = float(P ** -0.5)

    def alloc(self, ctx):
        sb = lambda n, sh, dt=F32: self.k.sb(self.name + "_" + n, sh, dt, ctx)
        self.qT = sb("qT", [P, T])
        self.kT = sb("kT", [P, T])
        self.v = sb("v", [P, NT, P])
        self.qi = sb("qi", [P, 2, P])
        self.pr = sb("pr", [P, 2, T])
        self.pT = sb("pT", [P, NT, P])
        self.neg = sb("neg", [P, 2])
        self.sum = sb("sum", [P, 2])
        self.rec = sb("rec", [P, 2])

    def tensor(self, pe):
        k = self.k
        pe.wait_ge(self.ln.ready, self.ln.all_ready)
        def turn(c):
            pe.wait_ge(self.q_ready, c)
            pe.wait_ge(self.k_ready, c)
            for i in range(2):
                ins = pe.matmul(k.bank(i), k.w3[:, i, :], k.HT[:, bass.ds(1 + c * CH, CH)], start=True, stop=True)
            ins.then_inc(self.projected, 1)

        each(pe, NC, turn)
        for c in range(NC):
            if c >= 2:
                pe.wait_ge(self.values, c - 1)
            for i in range(TPC):
                n = c * TPC + i
                ins = pe.matmul(k.PS[:, 4 + c % 2, i * P:(i + 1) * P], k.HT[:, 1 + n * P:1 + (n + 1) * P],
                                k.w3[:, 2, :], start=True, stop=True)
            ins.then_inc(self.vproj, 1)
        pe.wait_ge(self.q_ready, NC)
        pe.wait_ge(self.k_ready, NC)
        pe.wait_ge(self.values, NC)

        def scores(i, b):
            pe.wait_ge(self.tile, i + 1)
            pe.wait_ge(self.exps, i)
            for c in range(NC):
                ins = pe.matmul(k.bank(c), self.qi[:, b, :], self.kT[:, c * CH:(c + 1) * CH], start=True, stop=True)
            ins.then_inc(self.scores, 1)

        def weigh(i, b):
            pe.wait_ge(self.exps, i + 1)
            for q in range(NC):
                if q < 2:
                    pe.wait_ge(self.moved, i * NC)
                else:
                    pe.wait_ge(self.moved, i * NC + q - 1)
                for m in range(TPC):
                    n = q * TPC + m
                    ins = pe.transpose(k.PS[:, 4 + q % 2, m * P:(m + 1) * P], self.pr[:, b, n * P:(n + 1) * P],
                                       k.ident)
                ins.then_inc(self.turned, 1)
            for n in range(NT):
                if n % TPC == 0:
                    pe.wait_ge(self.moved, i * NC + n // TPC + 1)
                ins = pe.matmul(k.PS[:, 6 + b, 0:P], self.pT[:, n, :], self.v[:, n, :],
                                start=(n == 0), stop=(n == NT - 1))
            ins.then_inc(self.weighted, 1)

        scores(0, 0)
        def turn(t):
            scores(2 * t + 1, 1)
            weigh(2 * t, 0)
            scores(2 * t + 2, 0)
            weigh(2 * t + 1, 1)

        each(pe, NT // 2 - 1, turn)
        scores(NT - 1, 1)
        weigh(NT - 2, 0)
        weigh(NT - 1, 1)

    def scalar(self, s):
        k = self.k
        def turn(c):
            s.wait_ge(self.projected, c + 1)
            s.activation(self.qT[:, bass.ds(c * CH, CH)], k.bank(0), ACT.Identity, bias=k.vec[:, 7:8]) \
                .then_inc(self.q_ready, 1)

        each(s, NC, turn)
        s.wait_ge(self.q_ready, NC)

        def tile(i, b):
            s.activation(self.qi[:, b, :], self.qT[:, bass.ds(i * P, P)], ACT.Copy).then_inc(self.tile, 1)

        def exps(i, b):
            s.wait_ge(self.maxima, i + 1)
            s.activation(self.pr[:, b, :], k.PS[:, 0:NC, :].rearrange("p c n -> p (c n)"), ACT.Exp,
                         bias=self.neg[:, b:b + 1], scale=self.scale, accum_out=self.sum[:, b:b + 1]) \
                .then_inc(self.exps, 1)

        def move(i, b):
            for q in range(NC):
                s.wait_ge(self.turned, i * NC + q + 1)
                if q == 0:
                    s.wait_ge(self.weighted, i)
                s.activation(self.pT[:, q * TPC:(q + 1) * TPC, :],
                             k.bank(4 + q % 2).rearrange("p (n d) -> p n d", n=TPC), ACT.Copy) \
                    .then_inc(self.moved, 1)

        tile(0, 0)
        tile(1, 1)
        exps(0, 0)
        def turn(t):
            move(2 * t, 0)
            tile(2 * t + 2, 0)
            exps(2 * t + 1, 1)
            move(2 * t + 1, 1)
            tile(2 * t + 3, 1)
            exps(2 * t + 2, 0)

        each(s, NT // 2 - 1, turn)
        move(NT - 2, 0)
        exps(NT - 1, 1)
        move(NT - 1, 1)

    def vector(self, v):
        k = self.k
        def turn(c):
            v.wait_ge(self.projected, c + 1)
            v.tensor_scalar(self.kT[:, bass.ds(c * CH, CH)], k.bank(1), k.vec[:, 8:9], None, ALU.add) \
                .then_inc(self.k_ready, 1)

        each(v, NC, turn)
        for c in range(NC):
            v.wait_ge(self.vproj, c + 1)
            v.tensor_tensor(self.v[:, c * TPC:(c + 1) * TPC, :],
                            k.bank(4 + c % 2).rearrange("p (n d) -> p n d", n=TPC),
                            k.bv[:, :].rearrange("p (a d) -> p a d", a=1).broadcast_to([P, TPC, P]), ALU.add) \
                .then_inc(self.values, 1)

        def maxima(i, b, first=0):
            v.wait_ge(self.scores, i + 1)
            v.tensor_reduce(self.neg[:, b:b + 1], k.PS[:, 0:NC, :].rearrange("p c n -> p (c n)"), AX.X, ALU.max,
                            negate=True).then_inc(self.steps, 1)
            v.wait_ge(self.steps, first + 2 * i)
            v.tensor_scalar(self.neg[:, b:b + 1], self.neg[:, b:b + 1], self.scale, None, ALU.mult) \
                .then_inc(self.maxima, 1)

        def add(i, b):
            v.wait_ge(self.weighted, i + 1)
            v.reciprocal(self.rec[:, b:b + 1], self.sum[:, b:b + 1]).then_inc(self.steps, 1)
            v.wait_ge(self.steps, 2 * i + 3)
            xi = k.X[:, bass.ds(i, 1), :].rearrange("p a d -> p (a d)")
            v.scalar_tensor_tensor(xi, k.PS[:, 6 + b, 0:P], self.rec[:, b:b + 1], xi, ALU.mult, ALU.add) \
                .then_inc(self.added, 1)

        maxima(0, 0, first=1)
        def turn(t):
            maxima(2 * t + 1, 1)
            add(2 * t, 0)
            maxima(2 * t + 2, 0)
            add(2 * t + 1, 1)

        each(v, NT // 2 - 1, turn)
        maxima(NT - 1, 1)
        add(NT - 2, 0)
        i = NT - 1
        v.wait_ge(self.weighted, i + 1)
        v.reciprocal(self.rec[:, 1:2], self.sum[:, 1:2]).then_inc(self.steps, 1)
        v.wait_ge(self.steps, 2 * NT)
        v.scalar_tensor_tensor(k.X[:, i, :], k.PS[:, 7, 0:P], self.rec[:, 1:2], k.X[:, i, :], ALU.mult, ALU.add) \
            .then_inc(self.added, 1)

    def x_ready(self, c):
        return [(self.added, (c + 1) * TPC)]


CST_ORDER = N_CST * P
CST_COLS = N_CST * P + 8


def constants():
    c = np.zeros((P, CST_COLS), np.float32)
    r = np.arange(P)
    c[:, 0:P] = np.eye(P)
    same = (r[:, None] // 8 == r[None, :] // 8).astype(np.float32)
    c[:, P:2 * P] = same
    c[:, 2 * P:3 * P] = same / 8
    c[:, 3 * P:4 * P] = (r[:, None] // 32 == r[None, :] // 32) & (r[:, None] % 32 == 8)
    c[:, 4 * P:5 * P] = 1.0
    for j in range(8):
        c[:, (5 + j) * P:(6 + j) * P] = same * (r[None, :] % 8 == j)
    c[:, 13 * P:14 * P] = np.where(r[None, :] > r[:, None], MASKED, 0.0)
    c[:, 14 * P:15 * P] = np.where(r[:, None] > r[None, :], MASKED, 0.0)
    c[:, CST_ORDER:] = 8 - np.arange(8)
    return c


def rotation():
    freqs = (np.float32(1.0) / np.float32(10000.0) ** (np.arange(0, 8, 2, dtype=np.float32) / np.float32(8))) \
        .astype(np.float32)
    ang = np.outer(freqs, np.arange(T, dtype=np.float32)).astype(np.float32)
    p = np.arange(P)
    a = ang[(p % 8) // 2]
    sign = np.where(p % 2 == 0, -1.0, 1.0).astype(np.float32)[:, None]
    return np.ascontiguousarray(np.stack([np.cos(a), sign * np.sin(a)], axis=1).astype(np.float32))


INPUTS = ["L0_attn_a_x", "L0_attn_a_W_r", "L0_attn_a_W_k", "L0_attn_a_W_v", "L0_attn_a_W_w", "L0_attn_a_W_o",
          "L0_attn_a_u", "L0_attn_a_tm_r", "L0_attn_a_tm_k", "L0_attn_a_tm_v", "L0_attn_a_tm_w", "L0_attn_a_ln_w",
          "L0_attn_a_ln_b", "L0_attn_b_W_qkv", "L0_attn_b_W_out", "L0_ffn_Wg", "L0_ffn_bg", "L0_ffn_W1", "L0_ffn_b1",
          "L0_ffn_W2", "L0_ffn_b2", "L1_attn_a_W_q", "L1_attn_a_W_k", "L1_attn_a_W_v", "L1_attn_a_b_q",
          "L1_attn_a_b_k", "L1_attn_a_b_v", "L1_attn_b_wq", "L1_attn_b_wk_down", "L1_attn_b_wv_down",
          "L1_attn_b_wk_up", "L1_attn_b_wv_up", "L1_attn_b_wo", "L1_ffn_W1", "L1_ffn_b1", "L1_ffn_W2", "L1_ffn_b2",
          "L1_ffn_ln_gamma", "L1_ffn_ln_beta", "L1_ffn_Wr", "L1_ffn_br"]


def build(nc, d, upto=8, start=0):
    with ExitStack() as ctx:
        k = Kernel(nc, ctx, d)
        k.setup = Setup(k)
        perturb = Perturb(k)
        stages = []
        x_ready = lambda c: [(k.setup.loaded_x, 16), (k.setup.ready, 1)]

        def norm():
            ln = LayerNorm(k, k.X, k.H, k.HT, x_ready)
            stages.append(ln)
            return ln

        def experts0(name):
            ln = norm()
            r = Router(k, name + "_router", ln.dst_t, ln, k.wg[:, :], k.bg, True)
            e = Experts(k, name, ln.dst_t, ln, r, lambda e, m: k.w0[:, e, m * P:(m + 1) * P],
                        lambda e, m: k.w0b[:, e, m, :], lambda e, m: k.b0[:, e, m:m + 1], k.seed0, ACT.Gelu, 8, 2)
            with ExitStack() as arena:
                e.alloc(arena)
            stages.extend([r, e])
            return e.x_ready

        def rope_attention():
            ln = norm()
            blocks = ([(0, 24 * a, 0, 3) for a in range(3)],
                      [(0, 0, 0, 3), (0, 24, 1, 2), (0, 40, 0, 1), (0, 48, 2, 1), (0, 56, 0, 2)])
            a = CausalHeads(k, "rope", ln, 4, [(k.wqkvT[:, i, :], k.wqkvT[:, 3 + i, :], P) for i in range(2)],
                            blocks, 96, 4, k.wqkvT[:, 2, :], 16, 8, float(8 ** -0.5), k.woutT,
                            d["rope_parts"], True, False)
            with ExitStack() as arena:
                a.alloc(arena)
            stages.append(a)
            return a.x_ready

        def rwkv():
            ln = norm()
            rw = Rwkv(k, ln.dst_t, ln)
            with ExitStack() as arena:
                k.setup.alloc(arena)
                rw.alloc(arena)
            stages.append(rw)
            return lambda c: [(rw.ready, c + 1)]

        if start:
            with ExitStack() as arena:
                k.setup.alloc(arena)
        def full_attention():
            ln = norm()
            a = FullHead(k, "full", ln)
            with ExitStack() as arena:
                a.alloc(arena)
            stages.append(a)
            return a.x_ready

        def experts1(name, first):
            with ExitStack() as arena:
                ln = norm()
                h2 = k.sb(name + "_h2", [P, NT, P], F32, arena)
                h2t = k.sb(name + "_h2t", [P, 1 + T], F32, arena)
                if first:
                    stages.append(PerturbedRows(perturb))
                inner = LayerNorm(k, k.H, h2, h2t, lambda c: [(k.ln_mem.normed, ln.chunk_ready(c))],
                                  gamma=k.vec[:, 9:10], beta=k.vec[:, 10:11], banks=(4, 5, 6, 7))
                r = Router(k, name + "_router", h2t, inner, k.wr[:, :], k.br, False)
                e = Experts(k, name, k.HT, ln, r, lambda e, m: k.w1[:, e, m * P:(m + 1) * P],
                            lambda e, m: k.w1b[:, e, m, :], lambda e, m: k.b1[:, e, m:m + 1], k.seed1,
                            ACT.Gelu_apprx_tanh, 2, 4, needs=[(perturb.rows_split, 8), (perturb.ready, 16)])
                e.alloc(arena)
            stages.extend([inner, r, e])
            return e.x_ready

        def latent_attention():
            ln = norm()
            qb = [(0, 0, 0, 2), (0, 64, 0, 1), (1, 0, 0, 3)]
            kb = [(0, 0, 0, 1), (0, 32, 0, 2), (1, 0, 2, 1), (1, 32, 1, 1), (1, 64, 0, 1)]
            sources = [(k.wc[:, 4 * g:4 * g + 4, :].rearrange("p h l -> p (h l)"), None, P) for g in range(2)]
            a = CausalHeads(k, "latent", ln, 2, sources + [(k.wkv[:, :, :].rearrange("p a l -> p (a l)"), None, P)], (qb, kb), 96, 1,
                            k.wkv[:, 1, :], 2, 32, float(P ** -0.5), k.wy, d["latent_parts"], False, True)
            with ExitStack() as arena:
                a.alloc(arena)
            stages.append(a)
            return a.x_ready

        makers = [rwkv, lambda: experts0("moe1"), rope_attention, lambda: experts0("moe2"), full_attention,
                  lambda: experts1("ffn1", True), latent_attention, lambda: experts1("ffn2", int(start) == 7)]
        for make in makers[start:int(upto)]:
            x_ready = make()
        stored = k.sem("stored")
        block = ctx.enter_context(nc.Block())
        out = d["out"][0].rearrange("(n p) d -> p n d", p=P)

        @block.sync
        def _(sp):
            k.setup.sync(sp)
            for s in stages:
                s.sync(sp)
            for c in range(NC):
                for sem, val in x_ready(c):
                    sp.wait_ge(sem, val)
                sp.dma_start(out[:, c * TPC:(c + 1) * TPC, :], k.X[:, c * TPC:(c + 1) * TPC, :]) \
                    .then_inc(stored, 16)
            sp.wait_ge(stored, 16 * NC)

        @block.gpsimd
        def _(g):
            k.setup.gpsimd(g)
            for s in stages:
                s.gpsimd(g)

        @block.tensor
        def _(pe):
            k.setup.tensor(pe)
            for s in stages:
                s.tensor(pe)

        @block.scalar
        def _(act):
            for s in stages:
                s.scalar(act)

        @block.vector
        def _(v):
            k.setup.vector(v)
            for s in stages:
                s.vector(v)


def scratch(nc, d):
    d["b2_scratch"] = nc.dram_tensor("b2_scratch", (2 * P,), F32).ap()
    d["rope_parts"] = nc.dram_tensor("rope_parts", (2, 16, 3 * 8, T), BF16).ap()
    d["latent_parts"] = nc.dram_tensor("latent_parts", (3, 4, 3 * 32, T), BF16).ap()


def kernel(**inputs):
    import concourse.bacc as bacc
    from concourse.bass_utils import run_bass_kernel_spmd

    nc = bacc.Bacc("TRN2", target_bir_lowering=False, num_devices=1)
    arrays = {f"in_{n}": np.ascontiguousarray(inputs[n]) for n in INPUTS}
    arrays["in_const"] = constants()
    arrays["in_rotation"] = rotation()
    d = {n[3:]: nc.dram_tensor(n, a.shape, F32, kind="ExternalInput").ap() for n, a in arrays.items()}
    d["out"] = nc.dram_tensor("out", (1, T, P), F32, kind="ExternalOutput").ap()
    scratch(nc, d)
    build(nc, d)
    r = run_bass_kernel_spmd(nc, [arrays], core_ids=[0])
    return r.results[0]["out"]
```

```python
from contextlib import ExitStack

import numpy as np
import concourse.bass as bass
from concourse import mybir

F32 = mybir.dt.float32
BF16 = mybir.dt.bfloat16
I32 = mybir.dt.int32
ALU = mybir.AluOpType
ACT = mybir.ActivationFunctionType
AX = mybir.AxisListType
RADD = bass.bass_isa.ReduceOp.add

P = 128
T = 2048
NT = T // P
CH = 512
NC = T // CH
TPC = CH // P
MASKED = -1.0e30
LOWEST = -3.0e38


class Stage:

    next_ln = None
    tiles_ahead = 0

    def sync(self, sp):
        pass

    def gpsimd(self, g):
        pass

    def tensor(self, pe):
        pass

    def scalar(self, s):
        pass

    def vector(self, v):
        pass


def each(eng, turns, body):
    body(0)
    with eng.Fori(1, turns) as turn:
        body(turn)


class Chain:

    def __init__(self, eng, sem, base=0):
        self.eng, self.sem, self.base, self.n = eng, sem, base, 0

    def mark(self, ins):
        self.n += 1
        return ins.then_inc(self.sem, 1)

    def wait(self):
        self.eng.wait_ge(self.sem, self.base + self.n)

    def __call__(self, ins):
        self.mark(ins)
        self.wait()


class Kernel:

    def __init__(self, nc, ctx, dram):
        self.nc, self.ctx, self.d = nc, ctx, dram
        self.n_sem = 0
        sb = self.sb
        self.X = sb("X", [P, NT, P])
        self.H = sb("H", [P, NT, P])
        self.HT = sb("HT", [P, 1 + T])
        self.cst = sb("cst", [P, CST_COLS])
        self.gates = sb("gates", [P, NT, 8])
        self.experts_mem = ExpertsMemory(self)
        self.causal_mem = CausalMemory(self)
        self.router_mem = RouterMemory(self)
        self.ident = self.cst[:, 0:P]
        self.group_sum = self.cst[:, P:2 * P]
        self.group_mean = self.cst[:, 2 * P:3 * P]
        self.den_rope = self.cst[:, 3 * P:4 * P]
        self.ones_col = self.cst[:, 4 * P:4 * P + 32]
        self.mask_qk = sb("mask_qk", [P, P], BF16)
        self.mask_kq = sb("mask_kq", [P, P], BF16)
        self.identb = sb("identb", [P, P], BF16)
        self.onesb = sb("onesb", [P, P], BF16)
        self.zerosb = sb("zerosb", [P, 2], BF16)
        self.eps = sb("eps", [P, 1])
        self.PS = ctx.enter_context(nc.psum_tensor("PS", [P, 8, CH], F32))

    def sb(self, name, shape, dt=F32, ctx=None):
        return (ctx or self.ctx).enter_context(self.nc.sbuf_tensor("sb_" + name, shape, dt))

    def sem(self, name):
        self.n_sem += 1
        return self.ctx.enter_context(self.nc.semaphore(name))

    def bank(self, b, cols=CH):
        return self.PS[:, b, 0:cols]


N_CST = 5 + 8 + 2


class NormMemory:

    def __init__(self, k):
        self.stats = k.sb("stats", [P, NT, 6])
        self.mv = k.sb("mv", [P, NT, 2])
        self.sd = k.sb("sd", [P, NT])
        self.rstd = k.sb("rstd", [P, NT])
        self.uses = 0
        self.moments = k.sem("ln_moments")
        self.deviation = k.sem("ln_deviation")
        self.normed = k.sem("ln_normed")
        self.turned = k.sem("ln_turned")
        self.ready = k.sem("ln_ready")
        self.steps = k.sem("ln_steps")


class ExpertsMemory:

    def __init__(self, k):
        self.hid = [k.sem(f"hid{b}") for b in range(4)]
        self.hid_used = [k.sem(f"hid_used{b}") for b in range(4)]
        self.out = [k.sem(f"expert{b}") for b in range(2)]
        self.out_used = [k.sem(f"expert_used{b}") for b in range(2)]
        self.ready = k.sem("experts_ready")
        self.hid_count = self.out_count = self.ready_count = 0


class CausalMemory:

    def __init__(self, k):
        self.first = [k.sem(f"first{h}") for h in range(2)]
        self.filled = k.sem("filled")
        self.constants = k.sem("constants")
        self.vproj = k.sem("vproj")
        self.values = k.sem("values")
        self.rests = k.sem("rests")
        self.rounded = k.sem("rounded")
        self.uses = self.first_count = self.constant_count = self.rest_count = self.rounded_count = 0


class RouterMemory:

    def __init__(self, k):
        self.logits = k.sem("logits")
        self.read = k.sem("logits_read")
        self.shifted = k.sem("logits_shifted")
        self.exps = k.sem("router_exps")
        self.steps = k.sem("router_steps")
        self.uses = self.step_count = 0
        self.p = k.sb("rt_p", [P, NT, 8])
        self.a = k.sb("rt_a", [P, NT, 1])
        self.left = k.sb("rt_left", [P, NT, 8])
        self.sel = k.sb("rt_sel", [P, 2, NT, 8])


class LayerNorm(Stage):

    def __init__(self, k, src, dst, dst_t, src_ready, gamma=None, beta=None, banks=(0, 1, 2, 3)):
        self.k, self.src, self.dst, self.dst_t = k, src, dst, dst_t
        self.src_ready, self.gamma, self.beta, self.banks = src_ready, gamma, beta, banks
        self.mem = k.ln_mem
        self.use = self.mem.uses
        self.mem.uses += 1
        self.ready = self.mem.ready
        self.ahead = 0

    def statistics(self, v, n, tiles):
        for i in range(tiles):
            v.bn_stats(self.mem.stats[:, bass.ds(n + i, 1), :], self.src[:, bass.ds(n + i, 1), :]) \
                .then_inc(self.mem.steps, 1)

    def chunk_ready(self, c):
        return self.use * NC + c + 1

    @property
    def all_ready(self):
        return self.use * NC + NC

    def vector(self, v):
        m, first = self.mem, self.use * (NT + 1)
        for c in range(NC):
            for sem, val in self.src_ready(c):
                v.wait_ge(sem, val)
        self.statistics(v, self.ahead, NT - self.ahead)
        for n in range(NT):
            v.wait_ge(m.steps, first + n + 1)
            ins = v.bn_aggr(m.mv[:, n, :], m.stats[:, n, :])
        ins.then_inc(m.moments, 1)
        v.wait_ge(m.deviation, self.use + 1)
        v.reciprocal(m.rstd[:, :], m.sd[:, :]).then_inc(m.steps, 1)
        v.wait_ge(m.steps, first + NT + 1)
        for n in range(NT):
            ins = v.tensor_scalar(self.dst[:, n, :], self.src[:, n, :], m.mv[:, n, 0:1], m.rstd[:, n:n + 1],
                                  ALU.subtract, ALU.mult)
            if n % TPC == TPC - 1:
                ins.then_inc(m.normed, 1)

    def tensor(self, pe):
        for c in range(NC):
            if self.banks[c] in self.banks[:c]:
                pe.wait_ge(self.ready, self.chunk_ready(c - 2))
            pe.wait_ge(self.mem.normed, self.chunk_ready(c))
            for i in range(TPC):
                ins = pe.transpose(self.k.PS[:, self.banks[c], i * P:(i + 1) * P], self.dst[:, c * TPC + i, :],
                                   self.k.ident)
            ins.then_inc(self.mem.turned, 1)

    def scalar(self, s):
        m = self.mem
        s.wait_ge(m.moments, self.use + 1)
        s.activation(m.sd[:, :], m.mv[:, :, 1], ACT.Sqrt, bias=self.k.eps[:, :]).then_inc(m.deviation, 1)
        for c in range(NC):
            s.wait_ge(m.turned, self.chunk_ready(c))
            out = self.dst_t[:, 1 + c * CH:1 + (c + 1) * CH]
            if self.gamma is None:
                s.activation(out, self.k.bank(self.banks[c]), ACT.Copy).then_inc(m.ready, 1)
            else:
                s.activation(out, self.k.bank(self.banks[c]), ACT.Identity, bias=self.beta,
                             scale=self.gamma).then_inc(m.ready, 1)


class Setup(Stage):

    STEPS = 13

    def __init__(self, k):
        self.k = k
        sb = k.sb
        nc = k.nc
        self.loaded = k.sem("loaded")
        self.loaded_rest = k.sem("loaded_rest")
        self.loaded_x = k.sem("loaded_x")
        self.turned = [k.sem(f"weights_turned{i}") for i in range(2)]
        self.steps = k.sem("setup_steps")
        self.ready = k.sem("setup_ready")
        self.zeroed = k.sem("setup_zeroed")
        self.pool = k.sem("setup_pool")
        k.ln_mem = NormMemory(k)
        k.w0 = sb("w0", [P, 8, 256])
        k.w0b = sb("w0b", [P, 8, 2, P])
        k.wg = sb("wg", [P, 8])
        k.bg = sb("bg", [P, 8])
        k.w1 = sb("w1", [P, 2, CH])
        k.w1b = sb("w1b", [P, 2, 4, P])
        k.b1 = sb("b1", [P, 2, 4])
        k.b1col = sb("b1col", [P, 2])
        k.wr = sb("wr", [P, 8])
        k.br = sb("br", [P, 8])
        k.vec = sb("vec", [P, 32])
        k.b0 = k.vec[:, 16:32].rearrange("p (e m) -> p e m", m=2)
        k.seed0 = sb("seed0", [3, 8, P], BF16)
        k.seed1 = sb("seed1", [3, 2, P], BF16)
        k.wqkvT = sb("wqkvT", [P, 5, P])
        k.woutT = sb("woutT", [P, 4, P])
        k.bv = sb("bv", [P, P])
        k.w3 = sb("w3", [P, 3, P])
        k.wkv = sb("wkv", [P, 2, 64])
        k.wc = sb("wc", [P, 8, 32])
        k.wy = sb("wy", [P, 2, P])

        self.n_zeroed = 5

    def alloc(self, ctx):
        sb = lambda n, sh, dt=F32: self.k.sb(n, sh, dt, ctx)
        self.k.wT = sb("wT", [P, 5, P])
        self.k.wvrep = sb("wvrep", [P, 8, P])
        self.rows = sb("rows", [32, P])
        self.wraw = sb("wraw", [P, 9, P])
        self.wpad = sb("wpad", [P, 4, 4, 32])
        self.wq = sb("wq", [P, 8, P])
        self.wqT = sb("wqT", [P, 8, P])
        self.wup = sb("wup", [32, 2, P])
        self.wkupT = sb("wkupT", [P, 32])
        self.wvupT = sb("wvupT", [P, 32])
        self.wo = sb("wo", [P, 8, P])
        self.row0 = sb("row0", [3, 8, P])
        self.rowr = sb("rowr", [3, 8, P])
        self.rowb = sb("rowb", [3, 8, P], BF16)
        self.n_loaded, self.n_rest = (16 * len(x) for x in self.loads())

    def loads(self):
        k, d = self.k, self.k.d
        out = []

        def load(dst, src):
            out.append((dst, src))

        load(k.cst[:, :], d["const"])
        for i, w in enumerate((d["L0_attn_a_W_r"], d["L0_attn_a_W_k"], d["L0_attn_a_W_v"], d["L0_attn_a_W_w"], d["L0_attn_a_W_o"])):
            load(self.wraw[:, i, :], w)
        for i, w in enumerate((d["L0_attn_a_tm_r"], d["L0_attn_a_tm_k"], d["L0_attn_a_tm_v"], d["L0_attn_a_tm_w"],
                               d["L0_attn_a_u"].rearrange("h d -> (h d)"))):
            load(self.rows[i:i + 1, :], w.rearrange("(a p) -> a p", a=1))
        for i, w in ((5, d["L0_attn_a_ln_w"]), (6, d["L0_attn_a_ln_b"])):
            load(self.rows[i:i + 1, :].rearrange("a (h d) -> a h d", h=16),
                 w.rearrange("(a b d) -> a b d", a=1, b=1).broadcast_to([1, 16, 8]))
        for i, w in ((7, d["L1_attn_a_b_q"]), (8, d["L1_attn_a_b_k"]), (9, d["L1_ffn_ln_gamma"]), (10, d["L1_ffn_ln_beta"]),
                     (11, d["L1_ffn_b2"])):
            load(self.rows[i:i + 1, :], w.rearrange("(a p) -> a p", a=1))
        load(self.rows[12:16, :], d["L1_ffn_b1"].rearrange("(m p) -> m p", p=P))
        load(self.rows[16:32, :], d["L0_ffn_b1"].rearrange("e (m p) -> (e m) p", p=P))
        early, out = out, []
        for i, w in enumerate((d["L1_attn_a_W_q"], d["L1_attn_a_W_k"], d["L1_attn_a_W_v"])):
            load(k.w3[:, i, :], w)
        load(k.bv[:, :], d["L1_attn_a_b_v"].rearrange("(a p) -> a p", a=1).broadcast_to([P, P]))
        load(k.w0[:, :, :], d["L0_ffn_W1"].rearrange("e d h -> d e h"))
        for e in range(8):
            load(k.w0b[:, e, :, :], d["L0_ffn_W2"][e].rearrange("(m p) d -> p m d", p=P))
        load(k.wg[:, :], d["L0_ffn_Wg"])
        load(k.bg[:, :], d["L0_ffn_bg"].rearrange("(a e) -> a e", a=1).broadcast_to([P, 8]))
        load(self.row0[:, :, :], d["L0_ffn_b2"].rearrange("(a e) d -> a e d", a=1).broadcast_to([3, 8, P]))
        load(k.w1[:, 0, :], d["L1_ffn_W1"])
        load(k.w1b[:, 0, :, :], d["L1_ffn_W2"].rearrange("(m p) d -> p m d", p=P))
        load(k.wr[:, :], d["L1_ffn_Wr"])
        load(k.br[:, :], d["L1_ffn_br"].rearrange("(a e) -> a e", a=1).broadcast_to([P, 8]))
        load(self.wraw[:, 5:8, :], d["L0_attn_b_W_qkv"].rearrange("(n p) d -> p n d", p=P))
        load(self.wraw[:, 8, :], d["L0_attn_b_W_out"])
        load(self.wq[:, :, :], d["L1_attn_b_wq"].rearrange("p (h d) -> p h d", h=8))
        load(self.wup[:, 0, :], d["L1_attn_b_wk_up"])
        load(self.wup[:, 1, :], d["L1_attn_b_wv_up"])
        load(self.wo[:, :, :], d["L1_attn_b_wo"].rearrange("(h p) n -> p h n", p=P))
        load(k.wkv[:, 0, :], d["L1_attn_b_wk_down"])
        load(k.wkv[:, 1, :], d["L1_attn_b_wv_down"])
        return early, out

    def sync(self, sp):
        sp.dma_start(self.k.X[:, :, :], self.k.d["L0_attn_a_x"][0].rearrange("(n p) d -> p n d", p=P)) \
            .then_inc(self.loaded_x, 16)
        early, rest = self.loads()
        for dst, src in early:
            sp.dma_start(dst, src).then_inc(self.loaded, 16)
        for dst, src in rest:
            sp.dma_start(dst, src).then_inc(self.loaded_rest, 16)

    def gpsimd(self, g):
        k = self.k
        g.memset(k.eps[:, :], 1e-5).then_inc(self.zeroed, 1)
        g.memset(k.onesb[:, :], 1.0).then_inc(self.zeroed, 1)
        g.memset(k.zerosb[:, :], 0.0).then_inc(self.zeroed, 1)
        g.memset(self.wpad[:, :, :, :], 0.0).then_inc(self.zeroed, 1)
        g.memset(k.HT[:, 0:1], 0.0).then_inc(self.zeroed, 1)

    def tensor(self, pe):
        k = self.k
        pe.wait_ge(self.loaded, self.n_loaded)
        for i in range(4):
            ins = pe.transpose(k.PS[:, 4, i * P:(i + 1) * P], self.wraw[:, i, :], k.ident)
        ins.then_inc(self.turned[0], 1)
        pe.transpose(k.PS[:, 5, 0:P], self.wraw[:, 4, :], k.ident)
        pe.transpose(k.PS[:, 5, P:P + 32], self.rows[:, :], k.cst[0:32, 0:32]).then_inc(self.turned[1], 1)

    def scalar(self, s):
        s.wait_ge(self.zeroed, self.n_zeroed)

    def copies(self, v):
        k, ch = self.k, Chain(v, self.steps)
        v.wait_ge(self.zeroed, self.n_zeroed)
        v.wait_ge(self.turned[0], 1)
        ch(v.tensor_copy(k.wT[:, 0:4, :], k.PS[:, 4, :].rearrange("p (n d) -> p n d", n=4)))
        v.wait_ge(self.turned[1], 1)
        ch(v.tensor_copy(k.wT[:, 4, :], k.PS[:, 5, 0:P]))
        ch(v.tensor_copy(k.vec[:, :], k.PS[:, 5, P:P + 32]))
        ch(v.tensor_copy(k.b1[:, 0, :], k.vec[:, 12:16]))
        ch(v.tensor_copy(k.b1col[:, 0:1], k.vec[:, 11:12]))
        for j in range(8):
            ch(v.tensor_copy(k.wvrep[:, j, :].rearrange("p (h i) -> p h i", h=16),
                             k.wT[:, 2, :].rearrange("p (h i) -> p h i", h=16)[:, :, j:j + 1]
                             .broadcast_to([P, 16, 8])))
        assert ch.n == self.STEPS, ch.n
        v.sem_inc(self.ready, 1)


class SetupCopies(Stage):

    def __init__(self, k):
        self.k = k

    def vector(self, v):
        self.k.setup.copies(v)


class LaterWeights(Stage):

    def __init__(self, k):
        self.k, self.setup = k, k.setup
        self.turned = self.setup.turned
        self.copied = [k.sem(f"later_copied{i}") for i in range(2)]
        self.ready = k.sem("later_ready")

    def groups(self):
        k, s = self.k, self.setup
        pads = [s.wpad[:, g, :, :].rearrange("p j c -> p (j c)") for g in range(4)]
        return [([s.wraw[:, i, :] for i in range(5, 8)], k.wqkvT[:, 0:3, :]),
                (pads, k.woutT[:, :, :]), ([s.wq[:, i, :] for i in range(4)], s.wqT[:, 0:4, :]),
                ([s.wq[:, i, :] for i in range(4, 8)], s.wqT[:, 4:8, :])]

    def gpsimd(self, g):
        k, s = self.k, self.setup
        g.wait_ge(s.loaded_rest, s.n_rest)
        g.wait_ge(s.loaded, s.n_loaded)
        g.wait_ge(s.zeroed, s.n_zeroed)
        g.tensor_copy(s.wpad[:, :, :, 0:8], s.wraw[:, 8, :].rearrange("p (g j d) -> p g j d", g=4, j=4)) \
            .then_inc(self.ready, 1)
        g.tensor_copy(k.identb[:, :], k.ident).then_inc(self.ready, 1)
        g.tensor_copy(k.mask_qk[:, :], k.cst[:, (5 + 8) * P:(6 + 8) * P]).then_inc(self.ready, 1)
        g.tensor_copy(k.mask_kq[:, :], k.cst[:, (6 + 8) * P:(7 + 8) * P]).then_inc(self.ready, 1)

    def tensor(self, pe):
        k, s = self.k, self.setup
        pe.wait_ge(s.loaded_rest, s.n_rest)
        pe.wait_ge(s.ready, 1)
        pe.wait_ge(self.ready, 4)
        n = 0
        for ins_, _ in self.groups():
            if n >= 2:
                pe.wait_ge(self.copied[n % 2], n // 2)
            for i, a in enumerate(ins_):
                ins = pe.transpose(k.PS[:, 4 + n % 2, i * P:(i + 1) * P], a, k.ident)
            ins.then_inc(self.turned[n % 2], 1)
            n += 1
        pe.wait_ge(self.copied[0], 2)
        for i in range(2):
            ins = pe.transpose(k.PS[:, 4, i * 32:(i + 1) * 32], s.wup[:, i, :], k.cst[0:32, 0:32])
        ins.then_inc(self.turned[0], 1)
        pe.wait_ge(self.copied[0], 4)
        pe.wait_ge(self.copied[1], 2)
        for h in range(8):
            ins = pe.matmul(k.PS[:, 5, h * 32:(h + 1) * 32], s.wqT[:, h, :], s.wkupT[:, :], start=True, stop=True)
        ins.then_inc(self.turned[1], 1)
        for h in range(8):
            g, j = h // 4, h % 4
            ins = pe.matmul(k.PS[32 * j:32 * j + 32, 4, g * P:(g + 1) * P], s.wvupT[:, :], s.wo[:, h, :],
                            start=True, stop=True)
        ins.then_inc(self.turned[0], 1)

    def scalar(self, act):
        k, s = self.k, self.setup
        n = 0
        for _, out in self.groups():
            act.wait_ge(self.turned[n % 2], n // 2 + 2)
            w = out.shape[1]
            act.activation(out, k.PS[:, 4 + n % 2, 0:w * P].rearrange("p (n d) -> p n d", n=w), ACT.Copy) \
                .then_inc(self.copied[n % 2], 1)
            n += 1
        act.wait_ge(self.turned[0], 4)
        act.activation(s.wkupT[:, :], k.PS[:, 4, 0:32], ACT.Copy).then_inc(self.copied[0], 1)
        act.activation(s.wvupT[:, :], k.PS[:, 4, 32:64], ACT.Copy).then_inc(self.copied[0], 1)
        act.wait_ge(self.turned[1], 4)
        act.activation(k.wc[:, :, :], k.PS[:, 5, 0:256].rearrange("p (h l) -> p h l", h=8), ACT.Copy) \
            .then_inc(self.copied[1], 1)
        act.wait_ge(self.turned[0], 5)
        act.activation(k.wy[:, :, :], k.PS[:, 4, 0:2 * P].rearrange("p (h l) -> p h l", h=2), ACT.Copy) \
            .then_inc(self.copied[0], 1)

    def vector(self, v):
        k, s, ch = self.k, self.setup, Chain(v, self.setup.steps, self.setup.STEPS)
        v.wait_ge(s.loaded_rest, s.n_rest)
        split_rows(ch, v, s.row0[:, :, :], s.rowr[:, :, :], s.rowb[:, :, :], k.seed0[:, :, :], k)
        v.wait_ge(self.copied[0], 1)
        for i in range(2):
            for a in range(2):
                ch(v.tensor_copy(k.wqkvT[:, 3 + i, :].rearrange("p (m a) -> p m a", a=2)[:, :, a:a + 1],
                                 k.wqkvT[:, i, :].rearrange("p (m a) -> p m a", a=2)[:, :, 1 - a:2 - a]))


def split_rows(ch, v, full, rest, part, out, k):
    for r in range(3):
        src = full if r == 0 else rest
        ch(v.tensor_copy(part, src))
        if r == 0:
            ch(v.tensor_scalar(out, part, k.cst[0:3, 0:1], None, ALU.mult))
        else:
            ch(v.scalar_tensor_tensor(out, part, k.cst[0:3, r:r + 1], out, ALU.mult, ALU.add))
        if r < 2:
            ch(v.tensor_tensor(rest, src, part, ALU.subtract))


class Perturb:

    def __init__(self, k):
        self.k = k
        sb = k.sb
        self.steps = k.sem("perturb_steps")
        self.ready = k.sem("perturb_ready")
        self.b2_out = k.sem("perturb_b2_out")
        self.rows_split = k.sem("perturb_rows_split")
        self.a = sb("pa", [P, 2, CH])
        self.ab = sb("pab", [P, 4])
        self.ac = sb("pac", [P, 1])
        self.below = sb("pbelow", [P, 2, 2, CH])
        self.belowb = sb("pbelowb", [P, 2, 4])
        self.cnt = sb("pcnt", [P, 8])
        self.tot = sb("ptot", [P, 8])
        self.rank = sb("prank", [P, 8])
        self.found = sb("pfound", [P, 8], I32)
        self.trial = sb("ptrial", [P, 8], I32)
        self.keep = sb("pkeep", [P, 8], I32)
        self.bit = sb("pbit", [P, 8], I32)
        self.bitf = sb("pbitf", [P, 8])
        self.row1 = sb("prow1", [3, 2, P])
        self.rowr = sb("prowr", [3, 2, P])
        self.rowb = sb("prowb", [3, 2, P], BF16)

    def gpsimd(self, g):
        k = self.k
        ch = Chain(g, self.steps)
        g.wait_ge(k.setup.ready, 1)
        g.wait_ge(k.setup.loaded_rest, k.setup.n_rest)
        w2 = k.w1b[:, 0, :, :].rearrange("p m d -> p (m d)")
        for i, n in enumerate((P * CH, P * CH, CH, P)):
            kth = max(1, int(n * 0.1 / 2))
            ch(g.memset(self.rank[:, 2 * i:2 * i + 1], float(kth - 1)))
            ch(g.memset(self.rank[:, 2 * i + 1:2 * i + 2], float(n - kth)))
        ch(g.memset(self.found[:, :], 0))
        ch(g.memset(self.bitf[:, :], float(1 << 30)))
        for out, src in ((self.a[:, 0, :], k.w1[:, 0, :]), (self.a[:, 1, :], w2), (self.ab[:, :], k.b1[:, 0, :]),
                         (self.ac[:, :], k.b1col[:, 0:1])):
            low = self.below[:, 0, 0, 0:src.shape[-1]]
            ch(g.tensor_scalar(low, src, -1.0, 0.0, ALU.mult, ALU.max))
            ch(g.tensor_scalar(out, src, 0.0, None, ALU.max))
            ch(g.tensor_tensor(out, out, low, ALU.add))
        g.sem_clear(self.steps)
        with g.Fori(0, 31):
            ch = Chain(g, self.steps)
            tr = self.trial[:, :].bitcast(F32)
            ch(g.tensor_scalar(self.bit[:, :], self.bitf[:, :], 1.0, None, ALU.mult))
            ch(g.tensor_tensor(self.trial[:, :], self.found[:, :], self.bit[:, :], ALU.add))
            for s in range(2):
                for w in range(2):
                    ch.mark(g.tensor_scalar(self.below[:, w, s, :], self.a[:, w, :], tr[:, 2 * w + s:2 * w + s + 1],
                                            None, ALU.is_lt))
                ch.mark(g.tensor_scalar(self.belowb[:, s, :], self.ab[:, :], tr[:, 4 + s:5 + s], None, ALU.is_lt))
                ch(g.tensor_scalar(self.cnt[:, 6 + s:7 + s], self.ac[:, :], tr[:, 6 + s:7 + s], None, ALU.is_lt))
            bl = self.below[:, :, :, :].rearrange("p w s n -> p (w s) n")
            n = CH // 2
            while n > 1:
                ch(g.tensor_tensor(bl[:, :, 0:n], bl[:, :, 0:n], bl[:, :, n:2 * n], ALU.add))
                n //= 2
            ch.mark(g.tensor_tensor(self.cnt[:, 0:4], bl[:, :, 0], bl[:, :, 1], ALU.add))
            ch(g.tensor_tensor(self.belowb[:, :, 0:2], self.belowb[:, :, 0:2], self.belowb[:, :, 2:4], ALU.add))
            ch(g.tensor_tensor(self.cnt[:, 4:6], self.belowb[:, :, 0], self.belowb[:, :, 1], ALU.add))
            ch(g.partition_all_reduce(self.tot[:, :], self.cnt[:, :], P, RADD))
            ch(g.tensor_tensor(self.tot[:, :], self.tot[:, :], self.rank[:, :], ALU.subtract))
            ch(g.tensor_scalar(self.keep[:, :], self.tot[:, :], 0.0, self.bitf[:, 0:1], ALU.is_le, ALU.mult))
            ch(g.tensor_tensor(self.found[:, :], self.found[:, :], self.keep[:, :], ALU.add))
            ch(g.tensor_scalar(self.bitf[:, :], self.bitf[:, :], 0.5, None, ALU.mult))
            g.sem_clear(self.steps)
        ch = Chain(g, self.steps)
        th = self.found[:, :].bitcast(F32)
        for i, (a, src, out) in enumerate(((self.a[:, 0, :], k.w1[:, 0, :], k.w1[:, 1, :]),
                                           (self.a[:, 1, :], w2, k.w1b[:, 1, :, :].rearrange("p m d -> p (m d)")),
                                           (self.ab[:, :], k.b1[:, 0, :], k.b1[:, 1, :]),
                                           (self.ac[:, :], k.b1col[:, 0:1], k.b1col[:, 1:2]))):
            w = a.shape[-1]
            low = self.below[:, 0, 0, 0:w]
            top = self.below[:, 0, 1, 0:w]
            one = self.below[:, 1, 0, 0:w]
            ch(g.tensor_scalar(low, a, th[:, 2 * i:2 * i + 1], None, ALU.is_le))
            ch(g.tensor_scalar(top, a, th[:, 2 * i + 1:2 * i + 2], None, ALU.is_ge))
            ch(g.tensor_scalar(one, low, 1.0, None, ALU.add))
            ch(g.tensor_tensor(top, top, one, ALU.mult))
            ch(g.tensor_tensor(low, low, top, ALU.subtract))
            ch(g.tensor_scalar(one, src, 0.8, None, ALU.mult))
            ch(g.tensor_tensor(one, one, low, ALU.mult))
            ch(g.tensor_tensor(out, src, one, ALU.add))
        g.dma_start(k.d["b2_scratch"].rearrange("(v p) -> p v", v=2), k.b1col[:, :],
                    allow_slow_non_contiguous=True).then_inc(self.b2_out, 16)
        g.wait_ge(self.b2_out, 16)
        g.dma_start(self.row1[:, :, :], k.d["b2_scratch"].rearrange("(a v p) -> a v p", a=1, v=2)
                    .broadcast_to([3, 2, P])).then_inc(self.ready, 16)

    def split_b2(self, v):
        ch = Chain(v, self.rows_split)
        v.wait_ge(self.ready, 16)
        split_rows(ch, v, self.row1[:, :, :], self.rowr[:, :, :], self.rowb[:, :, :], self.k.seed1[:, :, :], self.k)



class PerturbedRows(Stage):

    def __init__(self, perturb):
        self.perturb = perturb

    def gpsimd(self, g):
        self.perturb.gpsimd(g)
        g.wait_ge(self.perturb.ready, 16)

    def vector(self, v):
        self.perturb.split_b2(v)


class Rwkv(Stage):

    STEPS0, STEPS = 4, 7
    tiles_ahead = NT - TPC

    def __init__(self, k, ht, ln):
        self.k, self.ht, self.ln = k, ht, ln
        s = lambda n: k.sem("rwkv_" + n)
        self.mixed = s("mixed")
        self.projected = s("projected")
        self.taken = s("taken")
        self.r_copied = s("r_copied")
        self.rk_ready = s("rk_ready")
        self.bonus = s("bonus")
        self.vrep = [s(f"vrep{b}") for b in range(2)]
        self.vrep_used = [s(f"vrep_used{b}") for b in range(2)]
        self.kv = [s(f"kv{b}") for b in range(2)]
        self.kv_used = [s(f"kv_used{b}") for b in range(2)]
        self.rs = [s(f"rs{b}") for b in range(2)]
        self.rs_used = [s(f"rs_used{b}") for b in range(2)]
        self.o_sb = s("o_sb")
        self.mean = s("mean")
        self.centred = s("centred")
        self.squared = s("squared")
        self.var = s("var")
        self.dev = s("dev")
        self.gated = s("gated")
        self.y = s("y")
        self.ready = s("ready")
        self.steps = s("steps")
        self.zeroed = s("zeroed")

    def alloc(self, ctx):
        sb = lambda n, sh: self.k.sb("rw_" + n, sh, ctx=ctx)
        self.diff = sb("diff", [P, CH])
        self.mix = sb("mix", [P, 4, CH])
        self.r, self.kk, self.v, self.w, self.ek = (sb(n, [P, CH]) for n in ("r", "k", "v", "w", "ek"))
        self.rk = sb("rk", [P, CH])
        self.r_last = sb("r_last", [P, CH])
        self.vj = sb("vj", [P, 2, CH])
        self.kvj = sb("kvj", [P, 2, CH])
        self.state = sb("state", [P, 8, 1 + CH])
        self.rsj = sb("rsj", [P, 2, CH])
        self.o = sb("o", [P, CH])
        self.oc = sb("oc", [P, CH])
        self.sq = sb("sq", [P, CH])
        self.sd = sb("sd", [P, CH])
        self.z = sb("z", [P, CH])

    def vector(self, v):
        k = self.k
        v.wait_ge(k.setup.ready, 1)
        v.memset(self.state[:, :, CH:CH + 1], 0.0).then_inc(self.zeroed, 1)
        v.wait_ge(self.zeroed, 1)

        def output(m):
            v.wait_ge(self.rs_used[1], m * 4)
            v.tensor_tensor(self.o[:, :], self.o[:, :], k.bank(6), ALU.add).then_inc(self.o_sb, 1)

        def centre(m):
            v.wait_ge(self.mean, m)
            v.tensor_tensor(self.oc[:, :], self.o[:, :], k.bank(7), ALU.subtract).then_inc(self.centred, 1)

        def invert(ch, m):
            v.wait_ge(self.dev, m)
            ch(v.reciprocal(self.sd[:, :], self.sd[:, :]))

        def normalise(ch, m):
            v.wait_ge(self.centred, m)
            ch(v.tensor_tensor(self.oc[:, :], self.oc[:, :], self.sd[:, :], ALU.mult))

        def gate(ch, m):
            ch(v.tensor_scalar(self.oc[:, :], self.oc[:, :], k.vec[:, 5:6], k.vec[:, 6:7], ALU.mult, ALU.add))
            v.wait_ge(self.r_copied, m)
            v.tensor_tensor(self.z[:, :], self.oc[:, :], self.r_last[:, :], ALU.mult).then_inc(self.gated, 1)

        def add(m):
            v.wait_ge(self.y, m)
            xc = k.X[:, bass.ds(m * TPC - TPC, TPC), :]
            v.tensor_tensor(xc, xc, k.bank(7).rearrange("p (n d) -> p n d", n=TPC), ALU.add) \
                .then_inc(self.ready, 1)

        def turn(c, ch, tail):
            if tail:
                output(c)
            v.wait_ge(self.ln.ready, self.ln.chunk_ready(c))
            v.wait_ge(self.vrep[1], c * 4)
            v.wait_ge(self.mixed, c * 4)
            v.wait_ge(self.rs[1], c * 4)
            ch(v.tensor_copy(self.state[:, :, 0:1], self.state[:, :, CH:CH + 1]))
            now = self.ht[:, bass.ds(1 + c * CH, CH)]
            before = self.ht[:, bass.ds(c * CH, CH)]
            ch(v.tensor_tensor(self.diff[:, :], now, before, ALU.subtract))
            for i in range(4):
                v.scalar_tensor_tensor(self.mix[:, i, :], self.diff[:, :], k.vec[:, i:i + 1], before,
                                       ALU.mult, ALU.add).then_inc(self.mixed, 1)
            if tail:
                centre(c)
            v.wait_ge(self.taken, c * 5 + 5)
            v.tensor_tensor(self.rk[:, :], self.r[:, :], self.ek[:, :], ALU.mult).then_inc(self.rk_ready, 1)
            ch(v.tensor_scalar(self.w[:, :], self.w[:, :], float(np.exp(-1e-4)), None, ALU.mult))
            for j in range(8):
                b = j % 2
                v.wait_ge(self.kv[b], c * 4 + j // 2 + 1)
                v.tensor_tensor_scan(self.state[:, j, 1:1 + CH], self.w[:, :], self.kvj[:, b, :],
                                     self.state[:, j, 0:1], ALU.mult, ALU.add).then_inc(self.kv_used[b], 1)
                if j == 0:
                    v.wait_ge(self.bonus, c + 1)
                    v.wait_ge(self.centred, c)
                    ch(v.tensor_tensor(self.o[:, :], k.bank(0), self.v[:, :], ALU.mult))
                if tail and j == 1:
                    invert(ch, c)
                if tail and j == 2:
                    normalise(ch, c)
                if tail and j == 3:
                    gate(ch, c)
                if tail and j == 6:
                    add(c)
                v.wait_ge(self.kv_used[b], c * 4 + j // 2 + 1)
                v.wait_ge(self.rs_used[b], c * 4 + j // 2)
                v.tensor_tensor(self.rsj[:, b, :], self.r[:, :], self.state[:, j, 0:CH], ALU.mult) \
                    .then_inc(self.rs[b], 1)
            if tail:
                v.wait_ge(self.ready, c)
                self.next_ln.statistics(v, c * TPC - TPC, TPC)
            v.wait_ge(self.gated, c)
            v.tensor_copy(self.r_last[:, :], self.r[:, :]).then_inc(self.r_copied, 1)
            assert ch.n == (self.STEPS if tail else self.STEPS0), ch.n

        turn(0, Chain(v, self.steps), False)
        with v.Fori(1, NC) as c:
            turn(c, Chain(v, self.steps, c * self.STEPS + self.STEPS0 - self.STEPS), True)
        ch = Chain(v, self.steps, (NC - 1) * self.STEPS + self.STEPS0)
        output(NC)
        centre(NC)
        invert(ch, NC)
        normalise(ch, NC)
        gate(ch, NC)
        add(NC)

    def scalar(self, s):
        k = self.k
        s.wait_ge(k.setup.ready, 1)

        def square(m):
            s.wait_ge(self.centred, m)
            s.activation(self.sq[:, :], self.oc[:, :], ACT.Square).then_inc(self.squared, 1)

        def deviation(m):
            s.wait_ge(self.var, m)
            s.activation(self.sd[:, :], k.bank(7), ACT.Sqrt, bias=k.eps[:, :]).then_inc(self.dev, 1)

        def turn(c, tail):
            s.wait_ge(self.r_copied, c)
            for b in range(2):
                s.wait_ge(self.kv[b], c * 4)
            for i, (out, f, kw) in enumerate(((self.r, ACT.Sigmoid, {}), (self.kk, ACT.Copy, {}),
                                              (self.v, ACT.Copy, {}), (self.w, ACT.Sigmoid, {}))):
                s.wait_ge(self.projected, c * 4 + i + 1)
                s.activation(out[:, :], k.bank(i), f, **kw).then_inc(self.taken, 1)
            s.activation(self.ek[:, :], k.bank(1), ACT.Exp, bias=k.vec[:, 4:5]).then_inc(self.taken, 1)
            if tail:
                square(c)
            for j in range(8):
                b = j % 2
                s.wait_ge(self.vrep[b], c * 4 + j // 2 + 1)
                s.wait_ge(self.kv[b], c * 4 + j // 2)
                s.activation(self.vj[:, b, :], k.bank(4 + b), ACT.Copy).then_inc(self.vrep_used[b], 1)
                if tail and j == 1:
                    deviation(c)

        turn(0, False)
        with s.Fori(1, NC) as c:
            turn(c, True)
        square(NC)
        deviation(NC)

    def gpsimd(self, g):
        def turn(c):
            for j in range(8):
                b = j % 2
                g.wait_ge(self.taken, c * 5 + 2)
                g.wait_ge(self.vrep_used[b], c * 4 + j // 2 + 1)
                g.wait_ge(self.kv_used[b], c * 4 + j // 2)
                g.tensor_tensor(self.kvj[:, b, :], self.kk[:, :], self.vj[:, b, :], ALU.mult).then_inc(self.kv[b], 1)

        each(g, NC, turn)

    def tensor(self, pe):
        k = self.k
        pe.wait_ge(self.ln.ready, self.ln.all_ready)

        def mean(m):
            pe.wait_ge(self.o_sb, m)
            pe.matmul(k.bank(7), k.group_mean, self.o[:, :], start=True, stop=True).then_inc(self.mean, 1)

        def variance(m):
            pe.wait_ge(self.squared, m)
            pe.matmul(k.bank(7), k.group_mean, self.sq[:, :], start=True, stop=True).then_inc(self.var, 1)

        def output(m):
            pe.wait_ge(self.gated, m)
            for n in range(TPC):
                ins = pe.matmul(k.PS[:, 7, n * P:(n + 1) * P], self.z[:, n * P:(n + 1) * P], k.wT[:, 4, :],
                                start=True, stop=True)
            ins.then_inc(self.y, 1)

        def turn(c, tail):
            if tail:
                mean(c)
            pe.wait_ge(self.taken, c * 5)
            for i in range(4):
                pe.wait_ge(self.mixed, c * 4 + i + 1)
                pe.matmul(k.bank(i), k.wT[:, i, :], self.mix[:, i, :], start=True, stop=True) \
                    .then_inc(self.projected, 1)

            def values(j):
                b = j % 2
                pe.wait_ge(self.vrep_used[b], c * 4 + j // 2)
                pe.matmul(k.bank(4 + b), k.wvrep[:, j, :], self.mix[:, 2, :], start=True, stop=True) \
                    .then_inc(self.vrep[b], 1)

            values(0)
            values(1)
            if tail:
                variance(c)
            pe.wait_ge(self.rk_ready, c + 1)
            pe.wait_ge(self.taken, c * 5 + 5)
            pe.matmul(k.bank(0), k.group_sum, self.rk[:, :], start=True, stop=True).then_inc(self.bonus, 1)
            for j in range(8):
                b = j % 2
                if j + 2 < 8:
                    values(j + 2)
                pe.wait_ge(self.rs[b], c * 4 + j // 2 + 1)
                pe.matmul(k.bank(6), k.cst[:, (5 + j) * P:(6 + j) * P], self.rsj[:, b, :],
                          start=(j == 0), stop=(j == 7)).then_inc(self.rs_used[b], 1)
                if tail and j == 4:
                    output(c)

        turn(0, False)
        with pe.Fori(1, NC) as c:
            turn(c, True)
        mean(NC)
        variance(NC)
        output(NC)


class Experts(Stage):

    tiles_ahead = NT - TPC

    def __init__(self, k, name, ht, ln, router, w1, w2, b1, seed, func, experts, tiles,
                 needs=(), between=()):
        self.k, self.name, self.ht, self.ln, self.router = k, name, ht, ln, router
        self.w1, self.w2, self.b1, self.seed, self.func = w1, w2, b1, seed, func
        self.E, self.M, self.needs = experts, tiles, needs
        self.between = between
        m = k.experts_mem
        self.hid, self.hid_used, self.out, self.out_used, self.ready = m.hid, m.hid_used, m.out, m.out_used, m.ready
        self.hid0, self.out0, self.ready0 = m.hid_count, m.out_count, m.ready_count
        m.hid_count += NC * experts * tiles // 4
        m.out_count += NC * experts // 2
        m.ready_count += NC

    def alloc(self, ctx):
        self.g = self.k.sb(self.name + "_hidden", [P, 2, self.M, CH], ctx=ctx)

    def tensor(self, pe):
        k, E, M = self.k, self.E, self.M
        uses = E * M // 4
        if not self.between:
            for sem, val in self.router.banks_free():
                pe.wait_ge(sem, val)
        for sem, val in self.needs:
            pe.wait_ge(sem, val)
        pe.wait_ge(self.ln.ready, self.ln.all_ready)
        def turn(c, first):
            x = self.ht[:, bass.ds(1 + c * CH, CH)]

            def hidden(e):
                for m in range(M):
                    b, n = (e * M + m) % 4, (e * M + m) // 4
                    pe.wait_ge(self.hid_used[b], self.hid0 + c * uses + n)
                    pe.matmul(k.bank(b), self.w1(e, m), x, start=True, stop=True).then_inc(self.hid[b], 1)

            def output(e):
                b = e % 2
                pe.wait_ge(self.out_used[b], self.out0 + c * (E // 2) + e // 2)
                pe.matmul(k.bank(4 + b), k.onesb[0:3, :],
                          self.seed[:, e:e + 1, :].broadcast_to([3, TPC, P]), start=True, stop=False,
                          skip_group_check=True)
                for m in range(M):
                    q, n = (e * M + m) % 4, (e * M + m) // 4
                    pe.wait_ge(self.hid_used[q], self.hid0 + c * uses + n + 1)
                    for i in range(TPC):
                        ins = pe.matmul(k.PS[:, 4 + b, i * P:(i + 1) * P], self.g[:, b, m, i * P:(i + 1) * P],
                                        self.w2(e, m), start=False, stop=(m == M - 1),
                                        skip_group_check=True)
                ins.then_inc(self.out[b], 1)

            for e in range(E):
                hidden(e)
                if e:
                    output(e - 1)
            if first:
                for stage in self.between:
                    stage.tensor(pe)
            output(E - 1)

        turn(0, True)
        with pe.Fori(1, NC) as c:
            turn(c, False)

    def scalar(self, s):
        k, E, M = self.k, self.E, self.M
        uses = E * M // 4
        for sem, val in self.needs:
            s.wait_ge(sem, val)
        def turn(c):
            for e in range(E):
                s.wait_ge(self.out[e % 2], self.out0 + c * (E // 2) + e // 2)
                for m in range(M):
                    b, n = (e * M + m) % 4, (e * M + m) // 4
                    s.wait_ge(self.hid[b], self.hid0 + c * uses + n + 1)
                    s.activation(self.g[:, e % 2, m, :], k.bank(b), self.func, bias=self.b1(e, m)) \
                        .then_inc(self.hid_used[b], 1)

        turn(0)
        for stage in self.between:
            stage.scalar(s)
        with s.Fori(1, NC) as c:
            turn(c)

    def vector(self, v):
        k, E = self.k, self.E
        def turn(c, later):
            if later and self.next_ln:
                v.wait_ge(self.ready, self.ready0 + c)
                self.next_ln.statistics(v, c * TPC - TPC, TPC)
            for e in range(E):
                b = e % 2
                v.wait_ge(self.out[b], self.out0 + c * (E // 2) + e // 2 + 1)
                if e:
                    v.wait_ge(self.out_used[1 - b], self.out0 + c * (E // 2) + (e - 1) // 2 + 1)
                for i in range(TPC):
                    xi = k.X[:, bass.ds(c * TPC + i, 1), :]
                    gate = k.gates[:, bass.ds(c * TPC + i, 1), e:e + 1].rearrange("p a b -> p (a b)")
                    ins = v.scalar_tensor_tensor(xi, k.PS[:, 4 + b:5 + b, i * P:(i + 1) * P], gate, xi,
                                                 ALU.mult, ALU.add)
                ins.then_inc(self.out_used[b], 1)
            v.wait_ge(self.out_used[1], self.out0 + c * (E // 2) + E // 2)
            v.sem_inc(self.ready, 1)

        for stage in self.between:
            stage.vector(v)
        turn(0, False)
        with v.Fori(1, NC) as c:
            turn(c, True)

    def x_ready(self, c):
        return [(self.ready, self.ready0 + c + 1)]


class Router(Stage):

    def __init__(self, k, name, ht, ln, w, bias, top2):
        self.k, self.ht, self.ln, self.w, self.bias, self.top2 = k, ht, ln, w, bias, top2
        m = k.router_mem
        self.logits, self.shifted, self.exps, self.steps, self.read = m.logits, m.shifted, m.exps, m.steps, m.read
        self.nth, self.step0 = m.uses + 1, m.step_count
        m.uses += 1
        m.step_count += 22 if top2 else 6

    def tensor(self, pe):
        k = self.k
        pe.wait_ge(self.ln.ready, self.ln.all_ready)
        for n in range(NT):
            ins = pe.matmul(k.PS[:, 7, n * 8:(n + 1) * 8], self.ht[:, 1 + n * P:1 + (n + 1) * P], self.w,
                            start=True, stop=True)
        ins.then_inc(self.logits, 1)

    def scalar(self, s):
        m = self.k.router_mem
        s.wait_ge(self.shifted, self.nth)
        s.activation(m.p[:, :, :], m.p[:, :, :], ACT.Exp, scale=0.2 if self.top2 else 1.0).then_inc(self.exps, 1)

    def banks_free(self):
        return [(self.read, self.nth)]

    def vector(self, v):
        k, m, ch = self.k, self.k.router_mem, Chain(v, self.steps, self.step0)
        full = [P, NT, 8]
        col = lambda a: a.broadcast_to(full)
        v.wait_ge(self.logits, self.nth)
        v.tensor_tensor(m.p[:, :, :], k.PS[:, 7, 0:NT * 8].rearrange("p (n e) -> p n e", n=NT),
                        self.bias[:, :].rearrange("p (a e) -> p a e", a=1).broadcast_to(full), ALU.add) \
            .then_inc(self.read, 1)
        v.wait_ge(self.read, self.nth)
        ch(v.tensor_reduce(m.a[:, :, :], m.p[:, :, :], AX.X, ALU.max))
        v.tensor_tensor(m.p[:, :, :], m.p[:, :, :], col(m.a[:, :, :]), ALU.subtract).then_inc(self.shifted, 1)
        v.wait_ge(self.exps, self.nth)
        ch(v.tensor_reduce(m.a[:, :, :], m.p[:, :, :], AX.X, ALU.add))
        ch(v.reciprocal(m.a[:, :, :], m.a[:, :, :]))
        ch(v.tensor_tensor(m.p[:, :, :], m.p[:, :, :], col(m.a[:, :, :]), ALU.mult))
        if not self.top2:
            ch(v.tensor_copy(k.gates[:, :, 0:1], m.p[:, :, 0:1]))
            ch(v.tensor_reduce(k.gates[:, :, 1:2], m.p[:, :, 1:8], AX.X, ALU.add))
            assert ch.n == 6
            return
        order = k.cst[:, CST_ORDER:CST_ORDER + 8].rearrange("p (a e) -> p a e", a=1).broadcast_to(full)
        ch(v.tensor_copy(m.left[:, :, :], m.p[:, :, :]))
        for r in range(2):
            sel = m.sel[:, r, :, :]
            ch(v.tensor_reduce(m.a[:, :, :], m.left[:, :, :], AX.X, ALU.max))
            ch(v.tensor_tensor(sel, m.left[:, :, :], col(m.a[:, :, :]), ALU.is_equal))
            ch(v.tensor_tensor(sel, sel, order, ALU.mult))
            ch(v.tensor_reduce(m.a[:, :, :], sel, AX.X, ALU.max))
            ch(v.tensor_tensor(sel, sel, col(m.a[:, :, :]), ALU.is_equal))
            if r == 0:
                ch(v.scalar_tensor_tensor(m.left[:, :, :], sel, -2.0, m.left[:, :, :], ALU.mult, ALU.add))
        ch(v.tensor_tensor(m.sel[:, 0, :, :], m.sel[:, 0, :, :], m.sel[:, 1, :, :], ALU.add))
        ch(v.tensor_tensor(m.p[:, :, :], m.p[:, :, :], m.sel[:, 0, :, :], ALU.mult))
        ch(v.tensor_reduce(m.a[:, :, :], m.p[:, :, :], AX.X, ALU.add))
        ch(v.tensor_scalar(m.a[:, :, :], m.a[:, :, :], 1e-9, None, ALU.add))
        ch(v.reciprocal(m.a[:, :, :], m.a[:, :, :]))
        ch(v.tensor_tensor(k.gates[:, :, :], m.p[:, :, :], col(m.a[:, :, :]), ALU.mult))
        assert ch.n == 22, ch.n


class CausalHeads(Stage):

    tiles_ahead = NT - TPC
    R = 3

    AHEAD = 3

    def __init__(self, k, name, ln, quads, sources, blocks, rows, kheads, value_w, vheads, vdim, scale, wout,
                 scratch, rotate, summed, rate):
        self.k, self.name, self.ln, self.NQ = k, name, ln, quads
        self.sources, self.blocks, self.rows, self.kheads = sources, blocks, rows, kheads
        self.value_w, self.vheads, self.vdim, self.scale = value_w, vheads, vdim, scale
        self.wout, self.scratch, self.rotate, self.summed = wout, scratch, rotate, summed
        self.rate = rate
        self.NP = 1 + max(b[0] for b in blocks[0])
        s = lambda n: k.sem(name + "_" + n)
        if rotate:
            self.table = s("table")
        self.projected = s("projected")
        self.split = s("split")
        self.stored = [s(f"stored{i}") for i in range(len(sources))]
        self.steps = s("steps")
        m, ns = k.causal_mem, len(sources)
        self.first, self.filled, self.constants = m.first, m.filled, m.constants
        self.vproj, self.values, self.rests, self.rounded = m.vproj, m.values, m.rests, m.rounded
        self.use, self.first0, self.constants0 = m.uses, m.first_count, m.constant_count
        self.rests0, self.rounded0 = m.rest_count, m.rounded_count
        m.uses += 1
        m.first_count += 16 * self.stack_dmas
        self.n_constants = NC * (2 if rotate else 1)
        m.constant_count += self.n_constants
        m.rest_count += NC * ns * (2 if rotate else 1)
        m.rounded_count += NC * ns * 2
        self.stacked = [s(f"stacked{b}") for b in range(2)]
        if summed:
            self.added = [s("added_g"), s("added_v")]
        else:
            self.sums_in = s("sums_in")
            self.inverted = s("inverted")
            self.sums_out = s("sums_out")
        self.ring_full = [s(f"ring_full{b}") for b in range(self.R)]
        self.ring_free = [s(f"ring_free{b}") for b in range(self.R)]
        self.maxima = s("maxima")
        self.max_rows = [s(f"max_rows{b}") for b in range(2)]
        self.scores = [s(f"scores{p}") for p in range(2)]
        self.exps = [s(f"exps{p}") for p in range(2)]
        self.weighted = s("weighted")
        self.moved = s("moved")
        self.normed = s("normed")
        self.ready = s("ready")
        self.units = [(c, kj) for c in range(NC) for kj in range((c + 1) * TPC)]
        self.plan = self.make_plan()

    def alloc(self, ctx):
        sb = lambda n, sh, dt=F32: self.k.sb(self.name + "_" + n, sh, dt, ctx)
        self.Q = sb("Q", [P, 2, 4, self.NP, T], BF16)
        self.K = sb("K", [P, 2, self.kheads, self.NP, T], BF16)
        self.vcols = self.vdim + (0 if self.summed else 1)
        self.V = sb("V", [P, NT, self.vheads, self.vcols])
        self.acc = sb("acc", [P, 4, CH]) if self.summed else None
        self.mp = sb("mp", [P, 2, NC, 4, TPC])
        self.neg = sb("neg", [P, 2, 4, TPC])
        self.negp = sb("negp", [P, 2, 4, 3, TPC], BF16)
        self.negT = sb("negT", [3 * 4 * TPC, 2, P], BF16)
        self.O = sb("O", [P, 2, CH])
        self.On = sb("On", [P, 2, CH])
        self.rec = sb("rec", [P, CH])
        self.sums = None if self.summed else sb("sums", [P, 4 * CH // P])
        with ExitStack() as c:
            self.PT = self.k.sb(self.name + "_PT", [P, 2, 4, CH], F32, c)
        with ExitStack() as c:
            ns = len(self.sources)
            self.parts = self.k.sb(self.name + "_parts", [P, ns, 3, CH], BF16, c)
            self.x = self.k.sb(self.name + "_x", [P, ns, CH], F32, c)
            if self.rotate:
                self.y = self.k.sb(self.name + "_y", [P, CH], F32, c)
                self.tab = self.k.sb(self.name + "_tab", [P, 2, T], F32, c)

    def chunk_maxima(self, g, c):
        items = []
        for i in range(TPC):
            for kc in range(c + 1):
                share = 1 if kc < c else TPC // (i + 1)
                items += [("max", g, c, i, kc, tuple(range(j, j + share))) for j in range(0, 4, share)]
        return items

    def make_plan(self):
        n = len(self.units)
        total = self.NQ * n
        items, due = [], []
        for g in range(self.NQ):
            for c in range(NC):
                items += self.chunk_maxima(g, c)
                due.append((g * n + self.units.index((c, 0)), len(items)))

        def wanted(u):
            late = max(min(d, np.ceil(d - self.rate * max(0, first - self.AHEAD - u))) for first, d in due)
            steady = (due[-1][1] - start) * u / (due[-1][0] - self.AHEAD)
            return int(min(len(items), max(late, start + steady)))

        start = 0
        start = wanted(0)
        steps = [[] for _ in range(total + 7)]
        turn_at = dict((d, (i // NC, i % NC)) for i, (u, d) in enumerate(due))
        up_front, pending = [], []
        done = 0
        for u in range(-1, total):
            mine = steps[u] if u >= 0 else up_front
            for i in range(max(2, wanted(u + 1) - done)):
                if pending and (i > pending[0][0] or done == len(items)):
                    mine.append(("turn",) + pending.pop(0)[1])
                if done < wanted(u + 1):
                    mine.append(items[done])
                    done += 1
                    if done in turn_at:
                        pending.append((i + 2, turn_at[done]))
            pending = [(0, at) for _, at in pending]
        relays = []
        for g in range(self.NQ):
            for c in range(NC):
                end = g * n + self.units.index((c, (c + 1) * TPC - 1))
                if self.summed:
                    steps[end + 2].append(("sum", g, c))
                    steps[end + 3].append(("out", g, c))
                else:
                    relays.append((end + 2, "sums", g, c))
                    relays.append((end + 4, "reciprocals", g, c))
                    steps[end + 6].append(("sum", g, c))
                    steps[end + 7].append(("out", g, c))
        plan = [(None, it) for it in up_front]
        for u, mine in enumerate(steps):
            a, b = (len(mine) + 3) // 4, (len(mine) + 1) // 2
            ring = lambda part: [(None, it) for it in part]
            if u < total:
                plan.append((u, "scores0"))
            plan += ring(mine[:a])
            if u < total:
                plan.append((u, "scores1"))
            plan += ring(mine[a:b])
            if 1 <= u <= total:
                plan.append((u - 1, "weighted"))
            plan += [(u, relay[1:]) for relay in relays if relay[0] == u]
            plan += ring(mine[b:])
        return plan

    def ring_bank(self, ring):
        return ring % self.R, ring // self.R

    def unit(self, u):
        g, i = divmod(u, len(self.units))
        c, kj = self.units[i]
        q0 = max(0, kj - c * TPC) * P
        return g, c, kj, q0

    def chunk(self, g, c):
        return g * NC + c

    def tensor(self, pe):
        k, ns = self.k, len(self.sources)
        pe.wait_ge(self.ln.ready, self.ln.all_ready)
        for c in range(NC):
            for i, (w, partner) in enumerate(self.sources):
                if c:
                    pe.wait_ge(self.rests, self.rests0 + (c - 1) * ns * (2 if self.rotate else 1) + i + 1)
                h = k.HT[:, 1 + c * CH:1 + (c + 1) * CH]
                b = self.source_bank(i)
                ins = pe.matmul(k.bank(b), w, h, start=True, stop=True)
                if partner is not None:
                    ins = pe.matmul(k.bank(b + 1), partner, h, start=True, stop=True)
                ins.then_inc(self.projected, 1)
            if c == 0:
                pe.wait_ge(self.filled, self.use + 1)
                for n in range(NT):
                    at = n % TPC * P
                    ins = pe.matmul(k.PS[:, 4 + n // TPC, at:at + self.value_w.shape[-1]],
                                    k.HT[:, 1 + n * P:1 + (n + 1) * P], self.value_w, start=True, stop=True)
                    if n % TPC == TPC - 1:
                        ins.then_inc(self.vproj, 1)
        pe.wait_ge(self.values, (self.use + 1) * NC)
        ring = 0
        for u, item in self.plan:
            if item == "scores0":
                self.pe_scores(pe, u, 0)
            elif item == "scores1":
                self.pe_scores(pe, u, 1)
            elif item == "weighted":
                self.pe_weighted(pe, u)
            elif u is None:
                b, uses = self.ring_bank(ring)
                pe.wait_ge(self.ring_free[b], uses)
                self.pe_item(pe, item, 5 + b).then_inc(self.ring_full[b], 1)
                ring += 1

    def pe_item(self, pe, item, bank):
        k, kind = self.k, item[0]
        if kind == "max":
            _, g, c, i, kc, heads = item
            if g == 0:
                pe.wait_ge(self.first[2 * c // NC], self.first0 + 16 * self.stack_dmas)
            else:
                pe.wait_ge(self.stacked[g % 2], 16 * self.stack_dmas * ((g + 1) // 2))
            w = CH if kc < c else (i + 1) * P
            q0 = c * CH + i * P
            for x, j in enumerate(heads):
                at = x * w
                ins = pe.matmul(k.PS[:, bank, at:at + w], self.Q[0:self.rows, g % 2, j, 0, q0:q0 + P],
                                self.K[0:self.rows, g % 2, j % self.kheads, 0, kc * CH:kc * CH + w],
                                start=True, stop=kc < c)
                if kc == c:
                    ins = pe.matmul(k.PS[:, bank, at + w - P:at + w], k.identb[:, :], k.mask_qk[:, :],
                                    start=False, stop=True)
            return ins
        if kind == "turn":
            _, g, c = item
            n = self.chunk(g, c)
            pe.wait_ge(self.maxima, n + 1)
            return pe.transpose(k.PS[:, bank, :].bitcast(BF16)[0:3 * 4 * TPC, 0:P],
                                self.negp[:, n % 2, :, :, :].rearrange("p j r i -> p (j r i)"), k.identb[:, :])
        if kind == "sum":
            _, g, c = item
            n = self.chunk(g, c)
            if self.summed:
                pe.wait_ge(self.added[0], self.first_unit(n + 1))
                pe.wait_ge(self.added[1], self.first_unit(n + 1))
                for j in range(4):
                    ins = pe.matmul(k.PS[32 * j:32 * j + 32, bank, :], k.ones_col, self.acc[:, j, :],
                                    start=True, stop=True)
                return ins
            pe.wait_ge(self.sums_out, 16 * (n + 1))
            return pe.matmul(k.bank(bank), k.den_rope, self.O[:, n % 2, :], start=True, stop=True)
        _, g, c = item
        n = self.chunk(g, c)
        pe.wait_ge(self.normed, n + 1)
        for i in range(TPC):
            ins = pe.matmul(k.PS[:, bank, i * P:(i + 1) * P], self.On[:, n % 2, i * P:(i + 1) * P],
                            self.wout[:, g, :], start=True, stop=True)
        return ins

    def first_unit(self, n):
        g, c = divmod(n, NC)
        return g * len(self.units) + self.units.index((c, 0))

    def pe_scores(self, pe, u, p):
        k = self.k
        g, c, kj, q0 = self.unit(u)
        n = self.chunk(g, c)
        if p == 0 and kj == 0:
            pe.wait_ge(self.max_rows[n % 2], 16 * 4 * (n // 2 + 1))
        if u == 0:
            pe.wait_ge(self.split, NC * len(self.sources))
        pe.wait_ge(self.exps[p], u)
        for j in (2 * p, 2 * p + 1):
            diag = kj >= c * TPC
            for m in range(self.NP):
                r = self.rows + (3 if m == 0 else 0)
                ins = pe.matmul(k.PS[:, j, q0:CH], self.K[0:r, g % 2, j % self.kheads, m, kj * P:(kj + 1) * P],
                                self.Q[0:r, g % 2, j, m, c * CH + q0:(c + 1) * CH],
                                start=(m == 0), stop=(m == self.NP - 1 and not diag))
            if diag:
                ins = pe.matmul(k.PS[:, j, q0:q0 + P], k.identb[:, :], k.mask_kq[:, :], start=False, stop=True)
        ins.then_inc(self.scores[p], 1)

    def pe_weighted(self, pe, u):
        k = self.k
        g, c, kj, q0 = self.unit(u)
        n = self.chunk(g, c)
        last = (c + 1) * TPC - 1
        if kj == 0:
            if n > 0:
                pe.wait_ge(self.moved, n)
        for p in range(2):
            pe.wait_ge(self.exps[p], u + 1)
        for j in range(4):
            v = self.V[:, kj, (4 * g + j) if self.vheads > 4 else g, :]
            ins = pe.matmul(k.PS[32 * j:32 * j + self.vcols, 4, q0:CH], v, self.PT[:, u % 2, j, q0:CH],
                            start=(kj == 0), stop=(kj == last))
        ins.then_inc(self.weighted, 1)

    def scalar(self, s):
        k, v = self.k, self.vdim
        ns = len(self.sources)
        passes = 2 if self.rotate else 1
        for c in range(NC + 1):
            if c < NC:
                for i in range(ns):
                    if self.rotate:
                        s.wait_ge(self.rests, self.rests0 + 2 * c * ns + i + 1)
                    else:
                        s.wait_ge(self.projected, c * ns + i + 1)
                    if c:
                        s.wait_ge(self.stored[i], 16 * self.split_dmas * c)
                    s.activation(self.parts[:, i, 0, :], self.source(i), ACT.Copy).then_inc(self.rounded, 1)
                for i in range(ns):
                    s.wait_ge(self.rests, self.rests0 + (c + 1) * passes * ns - ns + i + 1)
                    s.activation(self.parts[:, i, 1, :], self.x[:, i, :], ACT.Copy).then_inc(self.rounded, 1)
                self.write_constants(s, c)
                s.wait_ge(self.filled, self.use + 1)
                s.wait_ge(self.vproj, self.use * NC + c + 1)
                s.activation(self.V[:, c * TPC:(c + 1) * TPC, :, 0:v],
                             k.PS[:, 4 + c, :].rearrange("p (n d) -> p n d", n=TPC)[:, :, 0:self.vheads * v]
                             .rearrange("p n (h d) -> p n h d", h=self.vheads), ACT.Copy).then_inc(self.values, 1)
            if c in (NC // 2, NC):
                for sem in self.stored:
                    s.wait_ge(sem, 16 * self.split_dmas * c)
                s.wait_ge(self.constants, self.constants0 + c * self.n_constants // NC)
                self.load_stacks(s, 0, slice((c - NC // 2) * CH, c * CH), self.first[2 * c // NC - 1])
        total = self.NQ * len(self.units)
        for u in range(total + 1):
            if u < total:
                _, _, _, q0 = self.unit(u)
                if u >= 2:
                    s.wait_ge(self.weighted, u - 1)
                    if self.summed:
                        s.wait_ge(self.added[0], u - 1)
                        s.wait_ge(self.added[1], u - 1)
                for p in range(2):
                    s.wait_ge(self.scores[p], u + 1)
                    s.activation(self.PT[:, u % 2, 2 * p:2 * p + 2, q0:CH], k.PS[:, 2 * p:2 * p + 2, q0:CH],
                                 ACT.Exp, scale=self.scale).then_inc(self.exps[p], 1)
            if u:
                g, c, kj, _ = self.unit(u - 1)
                if kj == (c + 1) * TPC - 1:
                    n = self.chunk(g, c)
                    s.wait_ge(self.weighted, u)
                    if n >= 2:
                        s.wait_ge(self.normed, n - 1)
                    s.activation(self.O[:, n % 2, :], k.bank(4), ACT.Copy).then_inc(self.moved, 1)

    def write_constants(self, s, c):
        k, cols = self.k, slice(c * CH, (c + 1) * CH)
        if self.rotate:
            zeros = k.zerosb[:, :].bitcast(F32)[64:self.rows, None, None, 0:1]
            s.activation(self.Q[64:self.rows, :, :, 0, cols].bitcast(F32),
                         zeros.broadcast_to([self.rows - 64, 2, 4, CH // 2]), ACT.Copy).then_inc(self.constants, 1)
        ones = k.onesb[:, :].bitcast(F32)[:, None, None, 0:1]
        s.activation(self.K[:, :, :, 0, cols].bitcast(F32), ones.broadcast_to([P, 2, self.kheads, CH // 2]),
                     ACT.Copy).then_inc(self.constants, 1)

    def gpsimd(self, g):
        if not self.summed:
            return
        for u in range(self.NQ * len(self.units)):
            self.add_weights(g, u, 0, slice(0, 3))

    def add_weights(self, eng, u, who, heads):
        quad, c, kj, q0 = self.unit(u)
        n = self.chunk(quad, c)
        if kj == 0 and n:
            b, uses = self.ring_bank(self.ring_items().index(("sum", (n - 1) // NC, (n - 1) % NC)))
            eng.wait_ge(self.ring_full[b], uses + 1)
        if u:
            eng.wait_ge(self.added[who], u)
        for p in range(who, 2):
            eng.wait_ge(self.exps[p], u + 1)
        new, acc = self.PT[:, u % 2, heads, q0:CH], self.acc[:, heads, q0:CH]
        if kj == 0:
            eng.tensor_copy(acc, new).then_inc(self.added[who], 1)
        else:
            eng.tensor_tensor(acc, acc, new, ALU.add).then_inc(self.added[who], 1)

    def source_bank(self, i):
        return 2 * i if self.rotate else i

    def source(self, i):
        return self.x[:, i, :] if self.rotate else self.k.bank(self.source_bank(i))

    def vector(self, v):
        k, ch, ns = self.k, Chain(v, self.steps), len(self.sources)
        if not self.summed:
            v.memset(self.V[:, :, :, self.vdim:self.vdim + 1], 1.0)
        v.wait_ge(self.ln.ready, self.ln.all_ready)
        v.memset(k.PS[:, 4, :], 0.0).then_inc(self.filled, 1)
        if self.rotate:
            v.wait_ge(self.table, 16)
        made, n = self.rests0, 0
        for c in range(NC):
            if self.rotate:
                for i in range(ns):
                    v.wait_ge(self.projected, c * ns + i + 1)
                    cols, b = slice(c * CH, (c + 1) * CH), self.source_bank(i)
                    if c:
                        v.wait_ge(self.split, (c - 1) * ns + i + 1)
                    ch.mark(v.tensor_tensor(self.x[:, i, :], k.bank(b), self.tab[:, 0, cols], ALU.mult))
                    ch(v.tensor_tensor(self.y[:, :], k.bank(b + 1), self.tab[:, 1, cols], ALU.mult))
                    v.tensor_tensor(self.x[:, i, :], self.x[:, i, :], self.y[:, :], ALU.add).then_inc(self.rests, 1)
                    made += 1
                    v.wait_ge(self.rests, made)
            for i in range(ns):
                v.wait_ge(self.rounded, self.rounded0 + 2 * c * ns + i + 1)
                if c:
                    v.wait_ge(self.split, (c - 1) * ns + i + 1)
                v.tensor_tensor(self.x[:, i, :], self.source(i), self.parts[:, i, 0, :], ALU.subtract) \
                    .then_inc(self.rests, 1)
                made += 1
            for i in range(ns):
                v.wait_ge(self.rests, made - ns + i + 1)
                v.wait_ge(self.rounded, self.rounded0 + (2 * c + 1) * ns + i + 1)
                v.tensor_tensor(self.parts[:, i, 2, :], self.x[:, i, :], self.parts[:, i, 1, :], ALU.subtract) \
                    .then_inc(self.split, 1)
        ring = 0
        for u, item in self.plan:
            if u is not None:
                if item == "weighted" and self.summed:
                    self.add_weights(v, u, 1, slice(3, 4))
                elif item[0] == "reciprocals":
                    n = self.chunk(*item[1:])
                    v.wait_ge(self.sums_in, 16 * (n + 1))
                    if n:
                        v.wait_ge(self.sums_out, 16 * n)
                    v.reciprocal(self.rec[:, 0:4 * CH // P], self.sums[:, :]).then_inc(self.inverted, 1)
                continue
            b, uses = self.ring_bank(ring)
            v.wait_ge(self.ring_full[b], uses + 1)
            self.dve_item(v, ch, item, 5 + b, ring)
            ring += 1

    def turned_at(self, g, c):
        return self.ring_items().index(("turn", g, c))

    def ring_items(self):
        return [it for u, it in self.plan if u is None]

    def dve_item(self, v, ch, item, bank, ring):
        k, kind = self.k, item[0]
        b, uses = self.ring_bank(ring)
        free = self.ring_free[b]
        if kind == "max":
            _, g, c, i, kc, heads = item
            n = self.chunk(g, c)
            w = CH if kc < c else (i + 1) * P
            v.tensor_reduce(self.mp[:, n % 2, kc, heads[0]:heads[-1] + 1, i],
                            k.PS[:, bank, 0:len(heads) * w].rearrange("p (h k) -> p h k", h=len(heads)), AX.X, ALU.max) \
                .then_inc(free, 1)
            if (i, kc, heads[-1]) == (TPC - 1, c, 3):
                neg, part = self.neg[:, n % 2, :, :], self.negp[:, n % 2, :, :, :]
                for back in range(self.R):
                    if ring >= back:
                        b, uses = self.ring_bank(ring - back)
                        v.wait_ge(self.ring_free[b], uses + 1)
                ch(v.tensor_reduce(neg, self.mp[:, n % 2, 0:c + 1, :, :].rearrange("p k j i -> p j i k"), AX.X, ALU.max,
                                   negate=True))
                if n >= 2:
                    v.wait_ge(self.max_rows[n % 2], 16 * 4 * (n // 2))
                ch(v.tensor_copy(part[:, :, 0, :], neg))
                ch(v.tensor_tensor(neg, neg, part[:, :, 0, :], ALU.subtract))
                ch(v.tensor_copy(part[:, :, 1, :], neg))
                v.tensor_tensor(part[:, :, 2, :], neg, part[:, :, 1, :], ALU.subtract).then_inc(self.maxima, 1)
        elif kind == "turn":
            _, g, c = item
            n = self.chunk(g, c)
            if n >= 2:
                v.wait_ge(self.max_rows[n % 2], 16 * 4 * (n // 2))
            v.tensor_copy(self.negT[:, n % 2, :], k.PS[:, bank, :].bitcast(BF16)[0:3 * 4 * TPC, 0:P]).then_inc(free, 1)
        elif kind == "sum":
            _, g, c = item
            n = self.chunk(g, c)
            if self.summed:
                if n:
                    v.wait_ge(self.normed, n)
                v.wait_ge(self.moved, n + 1)
                v.reciprocal(self.rec[:, :], k.bank(bank)).then_inc(free, 1)
                v.wait_ge(free, uses + 1)
                v.tensor_tensor(self.On[:, n % 2, :], self.O[:, n % 2, :], self.rec[:, :], ALU.mult) \
                    .then_inc(self.normed, 1)
            else:
                ch(v.tensor_tensor(self.On[:, n % 2, :], self.O[:, n % 2, :], k.bank(bank), ALU.mult))
                v.sem_inc(self.normed, 1)
                v.sem_inc(free, 1)
        else:
            _, g, c = item
            xc = k.X[:, c * TPC:(c + 1) * TPC, :]
            v.tensor_tensor(xc, xc, k.bank(bank).rearrange("p (n d) -> p n d", n=TPC), ALU.add).then_inc(free, 1)
            if g == self.NQ - 1:
                v.wait_ge(free, uses + 1)
                v.sem_inc(self.ready, 1)
                if c < NC - 1 and self.next_ln:
                    self.next_ln.statistics(v, c * TPC, TPC)

    def x_ready(self, c):
        return [(self.ready, c + 1)]

    split_dmas = 3

    def load_stacks(self, sp, g, cols, done):
        d = P // self.shape[0]
        for operand, heads, (src, h), blocks in ((self.Q, 4, self.q_source(g), self.blocks[0]),
                                                 (self.K, self.kheads, self.k_source(g), self.blocks[1])):
            for m, row, first, parts in blocks:
                sp.dma_start(operand[row:row + parts * d, g % 2, 0:heads, m, cols],
                             self.scratch[src, h:h + heads, first * d:(first + parts) * d, cols]
                             .rearrange("h r t -> r h t")).then_inc(done, 16)

    def q_source(self, g):
        return (0, 4 * g) if self.rotate else (g, 0)

    def k_source(self, g):
        return (1, 4 * g) if self.rotate else (2, g)

    @property
    def shape(self):
        return self.scratch.shape[1], self.scratch.shape[2]

    @property
    def stack_dmas(self):
        return len(self.blocks[0]) + len(self.blocks[1])

    def sync(self, sp):
        ns = len(self.sources)
        heads, rows = self.shape
        sp.wait_ge(self.ln.mem.moments, self.ln.use + 1)
        if self.rotate:
            sp.dma_start(self.tab[:, :, :], self.k.d["rotation"]).then_inc(self.table, 16)
        for c in range(NC):
            cols = slice(c * CH, (c + 1) * CH)
            for i, (w, partner) in enumerate(self.sources):
                sp.wait_ge(self.split, c * ns + i + 1)
                for part in range(3):
                    d = rows // 3
                    sp.dma_start(self.scratch[i, :, part * d:(part + 1) * d, cols],
                                 self.parts[:, i, part, :]).then_inc(self.stored[i], 16)
        for sem in self.stored:
            sp.wait_ge(sem, 16 * self.split_dmas * NC)
        sp.wait_ge(self.constants, self.constants0 + self.n_constants)
        self.load_stacks(sp, 1, slice(0, T), self.stacked[1])
        for u, item in self.plan:
            if item[0] == "turn":
                _, g, c = item
                if c == NC - 1 and 2 <= g + 1 < self.NQ:
                    sp.wait_ge(self.weighted, g * len(self.units))
                    self.load_stacks(sp, g + 1, slice(0, T), self.stacked[(g + 1) % 2])
                n = self.chunk(g, c)
                b, uses = self.ring_bank(self.turned_at(g, c))
                sp.wait_ge(self.ring_free[b], uses + 1)
                for j in range(4):
                    sp.dma_start(self.Q[self.rows:self.rows + 3, g % 2, j, 0, c * CH:(c + 1) * CH],
                                 self.negT[3 * TPC * j:3 * TPC * (j + 1), n % 2, :]).then_inc(self.max_rows[n % 2], 16)
            elif item[0] in ("sums", "reciprocals"):
                n = self.chunk(*item[1:])
                rows = self.O[self.vdim::32, n % 2, :]
                if item[0] == "sums":
                    sp.wait_ge(self.moved, n + 1)
                    sp.dma_start(self.sums[:, :], rows).then_inc(self.sums_in, 16)
                else:
                    sp.wait_ge(self.inverted, n + 1)
                    sp.dma_start(rows, self.rec[:, 0:4 * CH // P]).then_inc(self.sums_out, 16)


class FullHead(Stage):

    tiles_ahead = NT - 1

    def __init__(self, k, name, ln):
        self.k, self.name, self.ln = k, name, ln
        s = lambda n: k.sem(name + "_" + n)
        self.projected = s("projected")
        self.q_ready = s("q_ready")
        self.k_ready = s("k_ready")
        self.vproj = s("vproj")
        self.values = s("values")
        self.tile = s("tile")
        self.scores = s("scores")
        self.maxima = s("maxima")
        self.exps = s("exps")
        self.turned = s("turned")
        self.moved = s("moved")
        self.weighted = s("weighted")
        self.added = s("added")
        self.steps = s("steps")
        self.scale = float(P ** -0.5)

    def alloc(self, ctx):
        sb = lambda n, sh, dt=F32: self.k.sb(self.name + "_" + n, sh, dt, ctx)
        self.qT = sb("qT", [P, T])
        self.kT = sb("kT", [P, T])
        self.v = sb("v", [P, NT, P])
        self.qi = sb("qi", [P, 2, P])
        self.pr = sb("pr", [P, 2, T])
        self.pT = sb("pT", [P, NT, P])
        self.neg = sb("neg", [P, 2])
        self.sum = sb("sum", [P, 2])
        self.rec = sb("rec", [P, 2])

    def tensor(self, pe):
        k = self.k
        pe.wait_ge(self.ln.ready, self.ln.all_ready)
        def turn(c):
            pe.wait_ge(self.q_ready, c)
            pe.wait_ge(self.k_ready, c)
            for i in range(2):
                ins = pe.matmul(k.bank(i), k.w3[:, i, :], k.HT[:, bass.ds(1 + c * CH, CH)], start=True, stop=True)
            ins.then_inc(self.projected, 1)

        each(pe, NC, turn)
        for c in range(NC):
            if c >= 2:
                pe.wait_ge(self.values, c - 1)
            for i in range(TPC):
                n = c * TPC + i
                ins = pe.matmul(k.PS[:, 4 + c % 2, i * P:(i + 1) * P], k.HT[:, 1 + n * P:1 + (n + 1) * P],
                                k.w3[:, 2, :], start=True, stop=True)
            ins.then_inc(self.vproj, 1)
        pe.wait_ge(self.q_ready, NC)
        pe.wait_ge(self.k_ready, NC)
        pe.wait_ge(self.values, NC)

        def scores(i, b):
            pe.wait_ge(self.tile, i + 1)
            pe.wait_ge(self.exps, i)
            for c in range(NC):
                ins = pe.matmul(k.bank(c), self.qi[:, b, :], self.kT[:, c * CH:(c + 1) * CH], start=True, stop=True)
            ins.then_inc(self.scores, 1)

        def weigh(i, b):
            pe.wait_ge(self.exps, i + 1)
            for q in range(NC):
                if q < 2:
                    pe.wait_ge(self.moved, i * NC)
                else:
                    pe.wait_ge(self.moved, i * NC + q - 1)
                for m in range(TPC):
                    n = q * TPC + m
                    ins = pe.transpose(k.PS[:, 4 + q % 2, m * P:(m + 1) * P], self.pr[:, b, n * P:(n + 1) * P],
                                       k.ident)
                ins.then_inc(self.turned, 1)
            for n in range(NT):
                if n % TPC == 0:
                    pe.wait_ge(self.moved, i * NC + n // TPC + 1)
                ins = pe.matmul(k.PS[:, 6 + b, 0:P], self.pT[:, n, :], self.v[:, n, :],
                                start=(n == 0), stop=(n == NT - 1))
            ins.then_inc(self.weighted, 1)

        scores(0, 0)
        def turn(t):
            scores(2 * t + 1, 1)
            weigh(2 * t, 0)
            scores(2 * t + 2, 0)
            weigh(2 * t + 1, 1)

        each(pe, NT // 2 - 1, turn)
        scores(NT - 1, 1)
        weigh(NT - 2, 0)
        weigh(NT - 1, 1)

    def scalar(self, s):
        k = self.k
        def turn(c):
            s.wait_ge(self.projected, c + 1)
            s.activation(self.qT[:, bass.ds(c * CH, CH)], k.bank(0), ACT.Identity, bias=k.vec[:, 7:8]) \
                .then_inc(self.q_ready, 1)

        each(s, NC, turn)
        s.wait_ge(self.q_ready, NC)

        def tile(i, b):
            s.activation(self.qi[:, b, :], self.qT[:, bass.ds(i * P, P)], ACT.Copy).then_inc(self.tile, 1)

        def exps(i, b):
            s.wait_ge(self.maxima, i + 1)
            s.activation(self.pr[:, b, :], k.PS[:, 0:NC, :].rearrange("p c n -> p (c n)"), ACT.Exp,
                         bias=self.neg[:, b:b + 1], scale=self.scale, accum_out=self.sum[:, b:b + 1]) \
                .then_inc(self.exps, 1)

        def move(i, b):
            for q in range(NC):
                s.wait_ge(self.turned, i * NC + q + 1)
                if q == 0:
                    s.wait_ge(self.weighted, i)
                s.activation(self.pT[:, q * TPC:(q + 1) * TPC, :],
                             k.bank(4 + q % 2).rearrange("p (n d) -> p n d", n=TPC), ACT.Copy) \
                    .then_inc(self.moved, 1)

        tile(0, 0)
        tile(1, 1)
        exps(0, 0)
        def turn(t):
            move(2 * t, 0)
            tile(2 * t + 2, 0)
            exps(2 * t + 1, 1)
            move(2 * t + 1, 1)
            tile(2 * t + 3, 1)
            exps(2 * t + 2, 0)

        each(s, NT // 2 - 1, turn)
        move(NT - 2, 0)
        exps(NT - 1, 1)
        move(NT - 1, 1)

    def vector(self, v):
        k = self.k
        def turn(c):
            v.wait_ge(self.projected, c + 1)
            v.tensor_scalar(self.kT[:, bass.ds(c * CH, CH)], k.bank(1), k.vec[:, 8:9], None, ALU.add) \
                .then_inc(self.k_ready, 1)

        each(v, NC, turn)
        for c in range(NC):
            v.wait_ge(self.vproj, c + 1)
            v.tensor_tensor(self.v[:, c * TPC:(c + 1) * TPC, :],
                            k.bank(4 + c % 2).rearrange("p (n d) -> p n d", n=TPC),
                            k.bv[:, :].rearrange("p (a d) -> p a d", a=1).broadcast_to([P, TPC, P]), ALU.add) \
                .then_inc(self.values, 1)

        def maxima(i, b, first=0):
            v.wait_ge(self.scores, i + 1)
            v.tensor_reduce(self.neg[:, b:b + 1], k.PS[:, 0:NC, :].rearrange("p c n -> p (c n)"), AX.X, ALU.max,
                            negate=True).then_inc(self.steps, 1)
            v.wait_ge(self.steps, first + 2 * i)
            v.tensor_scalar(self.neg[:, b:b + 1], self.neg[:, b:b + 1], self.scale, None, ALU.mult) \
                .then_inc(self.maxima, 1)

        def add(i, b, later=True):
            if later and self.next_ln:
                v.wait_ge(self.added, i)
                self.next_ln.statistics(v, i - 1, 1)
            v.wait_ge(self.weighted, i + 1)
            v.reciprocal(self.rec[:, b:b + 1], self.sum[:, b:b + 1]).then_inc(self.steps, 1)
            v.wait_ge(self.steps, 2 * i + 3)
            xi = k.X[:, bass.ds(i, 1), :].rearrange("p a d -> p (a d)")
            v.scalar_tensor_tensor(xi, k.PS[:, 6 + b, 0:P], self.rec[:, b:b + 1], xi, ALU.mult, ALU.add) \
                .then_inc(self.added, 1)

        maxima(0, 0, first=1)
        def turn(t, later):
            maxima(2 * t + 1, 1)
            add(2 * t, 0, later)
            maxima(2 * t + 2, 0)
            add(2 * t + 1, 1)

        turn(0, False)
        with v.Fori(1, NT // 2 - 1) as t:
            turn(t, True)
        maxima(NT - 1, 1)
        add(NT - 2, 0)
        i = NT - 1
        if self.next_ln:
            v.wait_ge(self.added, i)
            self.next_ln.statistics(v, i - 1, 1)
        v.wait_ge(self.weighted, i + 1)
        v.reciprocal(self.rec[:, 1:2], self.sum[:, 1:2]).then_inc(self.steps, 1)
        v.wait_ge(self.steps, 2 * NT)
        v.scalar_tensor_tensor(k.X[:, i, :], k.PS[:, 7, 0:P], self.rec[:, 1:2], k.X[:, i, :], ALU.mult, ALU.add) \
            .then_inc(self.added, 1)

    def x_ready(self, c):
        return [(self.added, (c + 1) * TPC)]


CST_ORDER = N_CST * P
CST_COLS = N_CST * P + 8


def constants():
    c = np.zeros((P, CST_COLS), np.float32)
    r = np.arange(P)
    c[:, 0:P] = np.eye(P)
    same = (r[:, None] // 8 == r[None, :] // 8).astype(np.float32)
    c[:, P:2 * P] = same
    c[:, 2 * P:3 * P] = same / 8
    c[:, 3 * P:4 * P] = (r[:, None] // 32 == r[None, :] // 32) & (r[:, None] % 32 == 8)
    c[:, 4 * P:5 * P] = 1.0
    for j in range(8):
        c[:, (5 + j) * P:(6 + j) * P] = same * (r[None, :] % 8 == j)
    c[:, 13 * P:14 * P] = np.where(r[None, :] > r[:, None], MASKED, 0.0)
    c[:, 14 * P:15 * P] = np.where(r[:, None] > r[None, :], MASKED, 0.0)
    c[:, CST_ORDER:] = 8 - np.arange(8)
    return c


def rotation():
    freqs = (np.float32(1.0) / np.float32(10000.0) ** (np.arange(0, 8, 2, dtype=np.float32) / np.float32(8))) \
        .astype(np.float32)
    ang = np.outer(freqs, np.arange(T, dtype=np.float32)).astype(np.float32)
    p = np.arange(P)
    a = ang[(p % 8) // 2]
    sign = np.where(p % 2 == 0, -1.0, 1.0).astype(np.float32)[:, None]
    return np.ascontiguousarray(np.stack([np.cos(a), sign * np.sin(a)], axis=1).astype(np.float32))


INPUTS = ["L0_attn_a_x", "L0_attn_a_W_r", "L0_attn_a_W_k", "L0_attn_a_W_v", "L0_attn_a_W_w", "L0_attn_a_W_o",
          "L0_attn_a_u", "L0_attn_a_tm_r", "L0_attn_a_tm_k", "L0_attn_a_tm_v", "L0_attn_a_tm_w", "L0_attn_a_ln_w",
          "L0_attn_a_ln_b", "L0_attn_b_W_qkv", "L0_attn_b_W_out", "L0_ffn_Wg", "L0_ffn_bg", "L0_ffn_W1", "L0_ffn_b1",
          "L0_ffn_W2", "L0_ffn_b2", "L1_attn_a_W_q", "L1_attn_a_W_k", "L1_attn_a_W_v", "L1_attn_a_b_q",
          "L1_attn_a_b_k", "L1_attn_a_b_v", "L1_attn_b_wq", "L1_attn_b_wk_down", "L1_attn_b_wv_down",
          "L1_attn_b_wk_up", "L1_attn_b_wv_up", "L1_attn_b_wo", "L1_ffn_W1", "L1_ffn_b1", "L1_ffn_W2", "L1_ffn_b2",
          "L1_ffn_ln_gamma", "L1_ffn_ln_beta", "L1_ffn_Wr", "L1_ffn_br"]


def build(nc, d, upto=8, start=0):
    with ExitStack() as ctx:
        k = Kernel(nc, ctx, d)
        k.setup = Setup(k)
        perturb = Perturb(k)
        stages = []
        x_ready = lambda c: [(k.setup.loaded_x, 16)]

        def norm():
            ln = LayerNorm(k, k.X, k.H, k.HT, x_ready)
            for producer in reversed(stages):
                if producer.tiles_ahead:
                    producer.next_ln, ln.ahead = ln, producer.tiles_ahead
                    break
            stages.append(ln)
            return ln

        def experts0(name):
            ln = norm()
            r = Router(k, name + "_router", ln.dst_t, ln, k.wg[:, :], k.bg, True)
            e = Experts(k, name, ln.dst_t, ln, r, lambda e, m: k.w0[:, e, m * P:(m + 1) * P],
                        lambda e, m: k.w0b[:, e, m, :], lambda e, m: k.b0[:, e, m:m + 1], k.seed0, ACT.Gelu, 8, 2)
            with ExitStack() as arena:
                e.alloc(arena)
            stages.extend([r, e])
            return e.x_ready

        def rope_attention():
            ln = norm()
            blocks = ([(0, 24 * a, 0, 3) for a in range(3)],
                      [(0, 0, 0, 3), (0, 24, 1, 2), (0, 40, 0, 1), (0, 48, 2, 1), (0, 56, 0, 2)])
            a = CausalHeads(k, "rope", ln, 4, [(k.wqkvT[:, i, :], k.wqkvT[:, 3 + i, :]) for i in range(2)],
                            blocks, 96, 4, k.wqkvT[:, 2, :], 16, 8, float(8 ** -0.5), k.woutT,
                            d["rope_parts"], True, False, 4.0)
            with ExitStack() as arena:
                a.alloc(arena)
            stages.append(a)
            return a.x_ready

        def rwkv():
            stages.append(k.setup)
            ln = norm()
            rw = Rwkv(k, ln.dst_t, ln)
            with ExitStack() as arena:
                k.setup.alloc(arena)
                rw.alloc(arena)
            stages.extend([SetupCopies(k), rw, LaterWeights(k)])
            return lambda c: [(rw.ready, c + 1)]

        if start:
            with ExitStack() as arena:
                k.setup.alloc(arena)
            stages.extend([k.setup, SetupCopies(k), LaterWeights(k)])
        def full_attention():
            ln = norm()
            a = FullHead(k, "full", ln)
            with ExitStack() as arena:
                a.alloc(arena)
            stages.append(a)
            return a.x_ready

        def experts1(name, first):
            with ExitStack() as arena:
                ln = norm()
                h2 = k.sb(name + "_h2", [P, NT, P], F32, arena)
                h2t = k.sb(name + "_h2t", [P, 1 + T], F32, arena)
                if first:
                    stages.append(PerturbedRows(perturb))
                inner = LayerNorm(k, k.H, h2, h2t, lambda c: [(k.ln_mem.normed, ln.chunk_ready(c))],
                                  gamma=k.vec[:, 9:10], beta=k.vec[:, 10:11], banks=(6, 7, 6, 7))
                r = Router(k, name + "_router", h2t, inner, k.wr[:, :], k.br, False)
                e = Experts(k, name, k.HT, ln, r, lambda e, m: k.w1[:, e, m * P:(m + 1) * P],
                            lambda e, m: k.w1b[:, e, m, :], lambda e, m: k.b1[:, e, m:m + 1], k.seed1,
                            ACT.Gelu_apprx_tanh, 2, 4, needs=[(perturb.rows_split, 8), (perturb.ready, 16)],
                            between=[inner, r])
                e.alloc(arena)
            stages.append(e)
            return e.x_ready

        def latent_attention():
            ln = norm()
            qb = [(0, 0, 0, 2), (0, 64, 0, 1), (1, 0, 0, 3)]
            kb = [(0, 0, 0, 1), (0, 32, 0, 2), (1, 0, 2, 1), (1, 32, 1, 1), (1, 64, 0, 1)]
            sources = [(k.wc[:, 4 * g:4 * g + 4, :].rearrange("p h l -> p (h l)"), None) for g in range(2)]
            a = CausalHeads(k, "latent", ln, 2, sources + [(k.wkv[:, :, :].rearrange("p a l -> p (a l)"), None)], (qb, kb), 96, 1,
                            k.wkv[:, 1, :], 2, 32, float(P ** -0.5), k.wy, d["latent_parts"], False, True, 4.5)
            with ExitStack() as arena:
                a.alloc(arena)
            stages.append(a)
            return a.x_ready

        makers = [rwkv, lambda: experts0("moe1"), rope_attention, lambda: experts0("moe2"), full_attention,
                  lambda: experts1("ffn1", True), latent_attention, lambda: experts1("ffn2", int(start) == 7)]
        for make in makers[start:int(upto)]:
            x_ready = make()
        stored = k.sem("stored")
        block = ctx.enter_context(nc.Block())
        out = d["out"][0].rearrange("(n p) d -> p n d", p=P)

        @block.sync
        def _(sp):
            for s in stages:
                s.sync(sp)
            for c in range(NC):
                for sem, val in x_ready(c):
                    sp.wait_ge(sem, val)
                sp.dma_start(out[:, c * TPC:(c + 1) * TPC, :], k.X[:, c * TPC:(c + 1) * TPC, :]) \
                    .then_inc(stored, 16)
            sp.wait_ge(stored, 16 * NC)

        @block.gpsimd
        def _(g):
            for s in stages:
                s.gpsimd(g)

        @block.tensor
        def _(pe):
            for s in stages:
                s.tensor(pe)

        @block.scalar
        def _(act):
            for s in stages:
                s.scalar(act)

        @block.vector
        def _(v):
            for s in stages:
                s.vector(v)


def scratch(nc, d):
    d["b2_scratch"] = nc.dram_tensor("b2_scratch", (2 * P,), F32).ap()
    d["rope_parts"] = nc.dram_tensor("rope_parts", (2, 16, 3 * 8, T), BF16).ap()
    d["latent_parts"] = nc.dram_tensor("latent_parts", (3, 4, 3 * 32, T), BF16).ap()


def kernel(**inputs):
    import concourse.bacc as bacc
    from concourse.bass_utils import run_bass_kernel_spmd

    nc = bacc.Bacc("TRN2", target_bir_lowering=False, num_devices=1)
    arrays = {f"in_{n}": np.ascontiguousarray(inputs[n]) for n in INPUTS}
    arrays["in_const"] = constants()
    arrays["in_rotation"] = rotation()
    d = {n[3:]: nc.dram_tensor(n, a.shape, F32, kind="ExternalInput").ap() for n, a in arrays.items()}
    d["out"] = nc.dram_tensor("out", (1, T, P), F32, kind="ExternalOutput").ap()
    scratch(nc, d)
    build(nc, d)
    r = run_bass_kernel_spmd(nc, [arrays], core_ids=[0])
    return r.results[0]["out"]
```
